# Optimizing a Trainium2 kernel written in Bass

```python
import numpy as np
import jax
import jax.numpy as jnp

def _softmax(x, axis=-1):
    return jax.nn.softmax(x, axis=axis)

def _gelu(x):
    return jax.nn.gelu(x, approximate=True)

def _silu(x):
    return jax.nn.silu(x)

def _sigmoid(x):
    return jax.nn.sigmoid(x)

def _layernorm(x, axis=-1, eps=1e-05):
    m = jnp.mean(x, axis=axis, keepdims=True)
    v = jnp.var(x, axis=axis, keepdims=True)
    return (x - m) / jnp.sqrt(v + eps)

def _scatter_add(tgt, idx, src, axis=0):
    return tgt.at[idx].add(src)

def _segment_sum(src, seg, n):
    return jax.ops.segment_sum(src, seg, n)
kernel_name = 'mk_gps_d2_gnn_r16_1be55d'

def setup_inputs(seed: int=0):
    np.random.seed(seed)
    _w = jnp.asarray

    def _rec_inputs():
        import jax
        import jax.numpy as jnp
        _gk = jax.random.key(seed)
        x = -0.000364 + 1 * jax.random.normal(jax.random.fold_in(_gk, 1), (625, 768), jnp.float32)
        src = jax.random.randint(jax.random.fold_in(_gk, 2), (10000,), 0, 625, jnp.int32)
        dst = jax.random.randint(jax.random.fold_in(_gk, 3), (10000,), 0, 625, jnp.int32)
        _o = jnp.argsort(dst, stable=True)
        src = src[_o]
        dst = dst[_o]
        edge_type_8 = jax.random.randint(jax.random.fold_in(_gk, 12), (10000,), 0, 8, jnp.int32)
        return (x, src, dst, edge_type_8)
    x, src, dst, edge_type_8 = _rec_inputs()

    def _L0_gnn_setup():
        import jax, jax.numpy as jnp
        import numpy as np
        N, IN, OUT, R, E = (1250, 768, 768, 8, 20000)

        def _rgcn_conv(x, src, dst, etype, W, root, b):
            num_nodes = x.shape[0]
            num_rel = W.shape[0]
            x_src = x[src]
            seg = dst * num_rel + etype
            sums = jax.ops.segment_sum(x_src, seg, num_segments=num_nodes * num_rel)
            cnt = jax.ops.segment_sum(jnp.ones((src.shape[0],), dtype=x.dtype), seg, num_segments=num_nodes * num_rel)
            mean = sums / jnp.maximum(cnt, 1.0)[:, None]
            mean = mean.reshape(num_nodes, num_rel, -1)
            out = jnp.einsum('nri,rio->no', mean, W)
            return out + x @ root + b
        key = jax.random.key(seed)
        ks = jax.random.split(key, 9)
        x = jax.random.normal(ks[0], (N, IN), dtype=jnp.float32)
        edge_index = jax.random.randint(ks[1], (2, E), 0, N, dtype=jnp.int64)
        edge_type = jax.random.randint(ks[2], (E,), 0, R, dtype=jnp.int64)
        s1 = 1.0 / np.sqrt(IN)
        s2 = 1.0 / np.sqrt(OUT)
        W1 = jax.random.normal(ks[3], (R, IN, OUT), dtype=jnp.float32) * s1
        root1 = jax.random.normal(ks[4], (IN, OUT), dtype=jnp.float32) * s1
        b1 = jnp.zeros((OUT,), dtype=jnp.float32)
        W2 = jax.random.normal(ks[5], (R, OUT, OUT), dtype=jnp.float32) * s2
        root2 = jax.random.normal(ks[6], (OUT, OUT), dtype=jnp.float32) * s2
        b2 = jnp.zeros((OUT,), dtype=jnp.float32)
        return {'x': x, 'edge_index': edge_index, 'edge_type': edge_type, 'W1': W1, 'root1': root1, 'b1': b1, 'W2': W2, 'root2': root2, 'b2': b2}
    _L0_gnn_all = _L0_gnn_setup()
    _L0_gnn_in = {k: v for k, v in _L0_gnn_all.items() if k in ('W1', 'root1', 'b1', 'W2', 'root2', 'b2')}
    del _L0_gnn_all

    def _L0_mix_setup():
        import jax, jax.numpy as jnp
        import numpy as np
        B, N, C = (16, 256, 768)
        H, D, M = (12, 64, 256)
        key = jax.random.key(seed)
        ks = jax.random.split(key, 6)
        rf = jax.random.normal(ks[5], (M, D), jnp.float32)
        rf = rf / jnp.linalg.norm(rf, axis=1, keepdims=True)
        return {'x': jax.random.normal(ks[0], (B, N, C), jnp.float32), 'W_qkv': jax.random.normal(ks[1], (C, 3 * C), jnp.float32) * C ** (-0.5), 'b_qkv': jax.random.normal(ks[2], (3 * C,), jnp.float32) * 0.02, 'W_proj': jax.random.normal(ks[3], (C, C), jnp.float32) * C ** (-0.5), 'b_proj': jax.random.normal(ks[4], (C,), jnp.float32) * 0.02, 'random_features': rf}
    _L0_mix_all = _L0_mix_setup()
    _L0_mix_in = {k: v for k, v in _L0_mix_all.items() if k in ('W_qkv', 'b_qkv', 'W_proj', 'b_proj', 'random_features')}
    del _L0_mix_all

    def _L0_ffn_setup():
        import jax, jax.numpy as jnp
        import numpy as np
        EMB = 768
        HID = 192
        HID2 = 2 * HID
        NE = 8
        K = 2
        B, N = (8, 128)

        def _gelu(x):
            return jax.nn.gelu(x, approximate=False)
        key = jax.random.key(seed)
        ks = jax.random.split(key, 9)
        s = lambda *d: 1.0 / np.sqrt(d[-2])
        inp = {'x': jax.random.normal(ks[0], (B, N, EMB), dtype=jnp.float32), 'Wg': jax.random.normal(ks[1], (EMB, NE), dtype=jnp.float32) * (1.0 / np.sqrt(EMB)), 'bg': jnp.zeros((NE,), dtype=jnp.float32), 'W1': jax.random.normal(ks[2], (NE, EMB, HID), dtype=jnp.float32) * (1.0 / np.sqrt(EMB)), 'b1': jnp.zeros((NE, HID), dtype=jnp.float32), 'W2': jax.random.normal(ks[3], (NE, HID, HID2), dtype=jnp.float32) * (1.0 / np.sqrt(HID)), 'b2': jnp.zeros((NE, HID2), dtype=jnp.float32), 'W3': jax.random.normal(ks[4], (NE, HID2, EMB), dtype=jnp.float32) * (1.0 / np.sqrt(HID2)), 'b3': jnp.zeros((NE, EMB), dtype=jnp.float32)}
        return inp
    _L0_ffn_all = _L0_ffn_setup()
    _L0_ffn_in = {k: v for k, v in _L0_ffn_all.items() if k in ('Wg', 'bg', 'W1', 'b1', 'W2', 'b2', 'W3', 'b3')}
    del _L0_ffn_all

    def _L1_gnn_setup():
        import jax, jax.numpy as jnp
        import numpy as np
        N_NODES = 1250
        N_EDGES = 10000
        IN_DIM = 768
        HID = 256
        HEADS = 4
        OUT_DIM = 768
        LN_EPS = 1e-05

        def _add_self_loops(edge_index, n):
            loop = jnp.arange(n, dtype=edge_index.dtype)
            return jnp.concatenate([edge_index, jnp.stack([loop, loop])], axis=1)

        def gat_conv(x, edge_index, W, a_src, a_dst, bias, heads, out_ch, concat):
            n = x.shape[0]
            ei = _add_self_loops(edge_index, n)
            src, dst = (ei[0], ei[1])
            xl = (x @ W).reshape(n, heads, out_ch)
            alpha_src = jnp.einsum('nhc,hc->nh', xl, a_src)
            alpha_dst = jnp.einsum('nhc,hc->nh', xl, a_dst)
            e = jax.nn.leaky_relu(alpha_src[src] + alpha_dst[dst], 0.2)
            m = jax.ops.segment_max(e, dst, num_segments=n)
            e = jnp.exp(e - m[dst])
            s = jax.ops.segment_sum(e, dst, num_segments=n)
            alpha = e / (s[dst] + 1e-16)
            msg = xl[src] * alpha[:, :, None]
            out = jax.ops.segment_sum(msg, dst, num_segments=n)
            out = out.reshape(n, heads * out_ch) if concat else out.mean(axis=1)
            return out + bias

        def layer_norm(x, g, b):
            mu = jnp.mean(x, axis=-1, keepdims=True)
            var = jnp.var(x, axis=-1, keepdims=True)
            return (x - mu) * jax.lax.rsqrt(var + LN_EPS) * g + b
        key = jax.random.key(seed)
        ks = jax.random.split(key, 16)
        s = 0.02
        HC = HID * HEADS
        return {'x': jax.random.normal(ks[0], (N_NODES, IN_DIM), jnp.float32), 'edge_index': jax.random.randint(ks[1], (2, N_EDGES), 0, N_NODES, jnp.int64 if jax.config.jax_enable_x64 else jnp.int32), 'W1': jax.random.normal(ks[2], (IN_DIM, HC), jnp.float32) * s, 'a_src1': jax.random.normal(ks[3], (HEADS, HID), jnp.float32) * s, 'a_dst1': jax.random.normal(ks[4], (HEADS, HID), jnp.float32) * s, 'b1': jnp.zeros((HC,), jnp.float32), 'g1': jnp.ones((HC,), jnp.float32), 'be1': jnp.zeros((HC,), jnp.float32), 'Wr1': jax.random.normal(ks[5], (IN_DIM, HC), jnp.float32) * s, 'br1': jnp.zeros((HC,), jnp.float32), 'W2': jax.random.normal(ks[6], (HC, OUT_DIM), jnp.float32) * s, 'a_src2': jax.random.normal(ks[7], (1, OUT_DIM), jnp.float32) * s, 'a_dst2': jax.random.normal(ks[8], (1, OUT_DIM), jnp.float32) * s, 'b2': jnp.zeros((OUT_DIM,), jnp.float32), 'g2': jnp.ones((OUT_DIM,), jnp.float32), 'be2': jnp.zeros((OUT_DIM,), jnp.float32), 'Wr2': jax.random.normal(ks[9], (HC, OUT_DIM), jnp.float32) * s, 'br2': jnp.zeros((OUT_DIM,), jnp.float32)}
    _L1_gnn_all = _L1_gnn_setup()
    _L1_gnn_in = {k: v for k, v in _L1_gnn_all.items() if k in ('W1', 'a_src1', 'a_dst1', 'b1', 'g1', 'be1', 'Wr1', 'br1', 'W2', 'a_src2', 'a_dst2', 'b2', 'g2', 'be2', 'Wr2', 'br2')}
    del _L1_gnn_all

    def _L1_mix_setup():
        import jax, jax.numpy as jnp
        import numpy as np
        LN_EPS = 1e-05
        NORM_EPS = 1e-12

        def _layernorm(x, gamma, beta):
            mu = jnp.mean(x, axis=-1, keepdims=True)
            var = jnp.mean(jnp.square(x - mu), axis=-1, keepdims=True)
            return (x - mu) * jax.lax.rsqrt(var + LN_EPS) * gamma + beta

        def _l2norm(x):
            n = jnp.sqrt(jnp.sum(jnp.square(x), axis=-1, keepdims=True))
            return x / jnp.maximum(n, NORM_EPS)
        key = jax.random.key(seed)
        ks = jax.random.split(key, 4)
        B, N, C, E = (8, 256, 768, 768)
        x = jax.random.normal(ks[0], (B, N, C), dtype=jnp.float32)
        w_qkv = jax.random.normal(ks[1], (C, 3 * E), dtype=jnp.float32) * (1.0 / np.sqrt(C))
        w_proj = jax.random.normal(ks[2], (E, C), dtype=jnp.float32) * (1.0 / np.sqrt(E))
        ln_in_g = jnp.ones((C,), jnp.float32)
        ln_in_b = jnp.zeros((C,), jnp.float32)
        ln_out_g = jnp.ones((E,), jnp.float32)
        ln_out_b = jnp.zeros((E,), jnp.float32)
        return {'x': x, 'w_qkv': w_qkv, 'w_proj': w_proj, 'ln_in_g': ln_in_g, 'ln_in_b': ln_in_b, 'ln_out_g': ln_out_g, 'ln_out_b': ln_out_b}
    _L1_mix_all = _L1_mix_setup()
    _L1_mix_in = {k: v for k, v in _L1_mix_all.items() if k in ('w_qkv', 'w_proj', 'ln_in_g', 'ln_in_b', 'ln_out_g', 'ln_out_b')}
    del _L1_mix_all

    def _L1_ffn_setup():
        import jax, jax.numpy as jnp
        import numpy as np
        EMB = 768
        HID = 1152
        NUM_EXPERTS = 8
        TOP_K = 2
        key = jax.random.key(seed)
        ks = jax.random.split(key, 8)
        s = 0.02
        x = jax.random.normal(ks[0], (4, 1024, EMB), dtype=jnp.float32)
        router_w = jax.random.normal(ks[1], (EMB, NUM_EXPERTS), dtype=jnp.float32) * s
        router_b = jnp.zeros((NUM_EXPERTS,), dtype=jnp.float32)
        w1 = jax.random.normal(ks[2], (NUM_EXPERTS, EMB, HID), dtype=jnp.float32) * s
        b1 = jnp.zeros((NUM_EXPERTS, HID), dtype=jnp.float32)
        w2 = jax.random.normal(ks[3], (NUM_EXPERTS, HID, EMB), dtype=jnp.float32) * s
        b2 = jnp.zeros((NUM_EXPERTS, EMB), dtype=jnp.float32)
        return {'x': x, 'router_w': router_w, 'router_b': router_b, 'w1': w1, 'b1': b1, 'w2': w2, 'b2': b2}
    _L1_ffn_all = _L1_ffn_setup()
    _L1_ffn_in = {k: v for k, v in _L1_ffn_all.items() if k in ('router_w', 'router_b', 'w1', 'b1', 'w2', 'b2')}
    del _L1_ffn_all
    return {'x': x, 'src': src, 'dst': dst, 'edge_type_8': edge_type_8, 'L0_gnn_W1': _L0_gnn_in['W1'], 'L0_gnn_root1': _L0_gnn_in['root1'], 'L0_gnn_b1': _L0_gnn_in['b1'], 'L0_gnn_W2': _L0_gnn_in['W2'], 'L0_gnn_root2': _L0_gnn_in['root2'], 'L0_gnn_b2': _L0_gnn_in['b2'], 'L0_mix_W_qkv': _L0_mix_in['W_qkv'], 'L0_mix_b_qkv': _L0_mix_in['b_qkv'], 'L0_mix_W_proj': _L0_mix_in['W_proj'], 'L0_mix_b_proj': _L0_mix_in['b_proj'], 'L0_mix_random_features': _L0_mix_in['random_features'], 'L0_ffn_Wg': _L0_ffn_in['Wg'], 'L0_ffn_bg': _L0_ffn_in['bg'], 'L0_ffn_W1': _L0_ffn_in['W1'], 'L0_ffn_b1': _L0_ffn_in['b1'], 'L0_ffn_W2': _L0_ffn_in['W2'], 'L0_ffn_b2': _L0_ffn_in['b2'], 'L0_ffn_W3': _L0_ffn_in['W3'], 'L0_ffn_b3': _L0_ffn_in['b3'], 'L1_gnn_W1': _L1_gnn_in['W1'], 'L1_gnn_a_src1': _L1_gnn_in['a_src1'], 'L1_gnn_a_dst1': _L1_gnn_in['a_dst1'], 'L1_gnn_b1': _L1_gnn_in['b1'], 'L1_gnn_g1': _L1_gnn_in['g1'], 'L1_gnn_be1': _L1_gnn_in['be1'], 'L1_gnn_Wr1': _L1_gnn_in['Wr1'], 'L1_gnn_br1': _L1_gnn_in['br1'], 'L1_gnn_W2': _L1_gnn_in['W2'], 'L1_gnn_a_src2': _L1_gnn_in['a_src2'], 'L1_gnn_a_dst2': _L1_gnn_in['a_dst2'], 'L1_gnn_b2': _L1_gnn_in['b2'], 'L1_gnn_g2': _L1_gnn_in['g2'], 'L1_gnn_be2': _L1_gnn_in['be2'], 'L1_gnn_Wr2': _L1_gnn_in['Wr2'], 'L1_gnn_br2': _L1_gnn_in['br2'], 'L1_mix_w_qkv': _L1_mix_in['w_qkv'], 'L1_mix_w_proj': _L1_mix_in['w_proj'], 'L1_mix_ln_in_g': _L1_mix_in['ln_in_g'], 'L1_mix_ln_in_b': _L1_mix_in['ln_in_b'], 'L1_mix_ln_out_g': _L1_mix_in['ln_out_g'], 'L1_mix_ln_out_b': _L1_mix_in['ln_out_b'], 'L1_ffn_router_w': _L1_ffn_in['router_w'], 'L1_ffn_router_b': _L1_ffn_in['router_b'], 'L1_ffn_w1': _L1_ffn_in['w1'], 'L1_ffn_b1': _L1_ffn_in['b1'], 'L1_ffn_w2': _L1_ffn_in['w2'], 'L1_ffn_b2': _L1_ffn_in['b2']}

def reference(x, src, dst, edge_type_8, L0_gnn_W1, L0_gnn_root1, L0_gnn_b1, L0_gnn_W2, L0_gnn_root2, L0_gnn_b2, L0_mix_W_qkv, L0_mix_b_qkv, L0_mix_W_proj, L0_mix_b_proj, L0_mix_random_features, L0_ffn_Wg, L0_ffn_bg, L0_ffn_W1, L0_ffn_b1, L0_ffn_W2, L0_ffn_b2, L0_ffn_W3, L0_ffn_b3, L1_gnn_W1, L1_gnn_a_src1, L1_gnn_a_dst1, L1_gnn_b1, L1_gnn_g1, L1_gnn_be1, L1_gnn_Wr1, L1_gnn_br1, L1_gnn_W2, L1_gnn_a_src2, L1_gnn_a_dst2, L1_gnn_b2, L1_gnn_g2, L1_gnn_be2, L1_gnn_Wr2, L1_gnn_br2, L1_mix_w_qkv, L1_mix_w_proj, L1_mix_ln_in_g, L1_mix_ln_in_b, L1_mix_ln_out_g, L1_mix_ln_out_b, L1_ffn_router_w, L1_ffn_router_b, L1_ffn_w1, L1_ffn_b1, L1_ffn_w2, L1_ffn_b2):
    import jax
    import jax.numpy as jnp

    def _L0_gnn_ref(x, edge_index, edge_type, W1, root1, b1, W2, root2, b2):
        import jax, jax.numpy as jnp
        import numpy as np
        N, IN, OUT, R, E = (1250, 768, 768, 8, 20000)

        def _rgcn_conv(x, src, dst, etype, W, root, b):
            num_nodes = x.shape[0]
            num_rel = W.shape[0]
            x_src = x[src]
            seg = dst * num_rel + etype
            sums = jax.ops.segment_sum(x_src, seg, num_segments=num_nodes * num_rel)
            cnt = jax.ops.segment_sum(jnp.ones((src.shape[0],), dtype=x.dtype), seg, num_segments=num_nodes * num_rel)
            mean = sums / jnp.maximum(cnt, 1.0)[:, None]
            mean = mean.reshape(num_nodes, num_rel, -1)
            out = jnp.einsum('nri,rio->no', mean, W)
            return out + x @ root + b
        src, dst = (edge_index[0], edge_index[1])
        h = _rgcn_conv(x, src, dst, edge_type, W1, root1, b1)
        h = jax.nn.relu(h)
        out = _rgcn_conv(h, src, dst, edge_type, W2, root2, b2)
        return out

    def _L0_mix_ref(x, W_qkv, b_qkv, W_proj, b_proj, random_features):
        import jax, jax.numpy as jnp
        import numpy as np
        B, N, C = (16, 256, 768)
        H, D, M = (12, 64, 256)
        b, n, c = x.shape
        qkv = (x @ W_qkv + b_qkv).reshape(b, n, 3, H, D)
        qkv = jnp.transpose(qkv, (2, 0, 3, 1, 4))
        q, k, v = (qkv[0], qkv[1], qkv[2])
        scale = D ** (-0.5)
        q = q * scale
        k = k * scale
        phi_q = jax.nn.relu(jnp.einsum('bhnd,md->bhnm', q, random_features))
        phi_k = jax.nn.relu(jnp.einsum('bhnd,md->bhnm', k, random_features))
        kv = jnp.einsum('bhnm,bhnd->bhmd', phi_k, v)
        attn = jnp.einsum('bhnm,bhmd->bhnd', phi_q, kv) / M
        out = jnp.transpose(attn, (0, 2, 1, 3)).reshape(b, n, c)
        return out @ W_proj + b_proj

    def _L0_ffn_ref(x, Wg, bg, W1, b1, W2, b2, W3, b3):
        import jax, jax.numpy as jnp
        import numpy as np
        EMB = 768
        HID = 192
        HID2 = 2 * HID
        NE = 8
        K = 2
        B, N = (8, 128)

        def _gelu(x):
            return jax.nn.gelu(x, approximate=False)
        scores = x @ Wg + bg
        topk_vals, topk_idx = jax.lax.top_k(scores, K)
        gates = jax.nn.softmax(topk_vals, axis=-1)
        onehot = jax.nn.one_hot(topk_idx, NE, dtype=x.dtype)
        comb = jnp.einsum('bnk,bnke->bne', gates, onehot)
        out = jnp.zeros_like(x)
        for e in range(NE):
            h = _gelu(x @ W1[e] + b1[e])
            h = _gelu(h @ W2[e] + b2[e])
            y = h @ W3[e] + b3[e]
            out = out + comb[..., e:e + 1] * y
        return out

    def _L1_gnn_ref(x, edge_index, W1, a_src1, a_dst1, b1, g1, be1, Wr1, br1, W2, a_src2, a_dst2, b2, g2, be2, Wr2, br2):
        import jax, jax.numpy as jnp
        import numpy as np
        N_NODES = 1250
        N_EDGES = 10000
        IN_DIM = 768
        HID = 256
        HEADS = 4
        OUT_DIM = 768
        LN_EPS = 1e-05

        def _add_self_loops(edge_index, n):
            loop = jnp.arange(n, dtype=edge_index.dtype)
            return jnp.concatenate([edge_index, jnp.stack([loop, loop])], axis=1)

        def gat_conv(x, edge_index, W, a_src, a_dst, bias, heads, out_ch, concat):
            n = x.shape[0]
            ei = _add_self_loops(edge_index, n)
            src, dst = (ei[0], ei[1])
            xl = (x @ W).reshape(n, heads, out_ch)
            alpha_src = jnp.einsum('nhc,hc->nh', xl, a_src)
            alpha_dst = jnp.einsum('nhc,hc->nh', xl, a_dst)
            e = jax.nn.leaky_relu(alpha_src[src] + alpha_dst[dst], 0.2)
            m = jax.ops.segment_max(e, dst, num_segments=n)
            e = jnp.exp(e - m[dst])
            s = jax.ops.segment_sum(e, dst, num_segments=n)
            alpha = e / (s[dst] + 1e-16)
            msg = xl[src] * alpha[:, :, None]
            out = jax.ops.segment_sum(msg, dst, num_segments=n)
            out = out.reshape(n, heads * out_ch) if concat else out.mean(axis=1)
            return out + bias

        def layer_norm(x, g, b):
            mu = jnp.mean(x, axis=-1, keepdims=True)
            var = jnp.var(x, axis=-1, keepdims=True)
            return (x - mu) * jax.lax.rsqrt(var + LN_EPS) * g + b
        h0 = x
        h = gat_conv(x, edge_index, W1, a_src1, a_dst1, b1, HEADS, HID, True)
        h = layer_norm(h, g1, be1)
        h = jax.nn.relu(h)
        h = h + (h0 @ Wr1 + br1)
        h1 = h
        h = gat_conv(h, edge_index, W2, a_src2, a_dst2, b2, 1, OUT_DIM, False)
        h = layer_norm(h, g2, be2)
        h = h + (h1 @ Wr2 + br2)
        return h

    def _L1_mix_ref(x, w_qkv, w_proj, ln_in_g, ln_in_b, ln_out_g, ln_out_b):
        import jax, jax.numpy as jnp
        import numpy as np
        LN_EPS = 1e-05
        NORM_EPS = 1e-12

        def _layernorm(x, gamma, beta):
            mu = jnp.mean(x, axis=-1, keepdims=True)
            var = jnp.mean(jnp.square(x - mu), axis=-1, keepdims=True)
            return (x - mu) * jax.lax.rsqrt(var + LN_EPS) * gamma + beta

        def _l2norm(x):
            n = jnp.sqrt(jnp.sum(jnp.square(x), axis=-1, keepdims=True))
            return x / jnp.maximum(n, NORM_EPS)
        h = _layernorm(x, ln_in_g, ln_in_b)
        qkv = h @ w_qkv
        q, k, v = jnp.split(qkv, 3, axis=-1)
        phi_q = _l2norm(q)
        phi_k = _l2norm(k)
        kv = jnp.sum(phi_k * v, axis=1)
        attn = phi_q * kv[:, None, :]
        out = _layernorm(attn, ln_out_g, ln_out_b) @ w_proj
        return out

    def _L1_ffn_ref(x, router_w, router_b, w1, b1, w2, b2):
        import jax, jax.numpy as jnp
        import numpy as np
        EMB = 768
        HID = 1152
        NUM_EXPERTS = 8
        TOP_K = 2
        B, N, E = x.shape
        T = B * N
        logits = jnp.einsum('bne,ef->bnf', x, router_w) + router_b
        probs = jax.nn.softmax(logits, axis=-1)
        topk_probs, topk_idx = jax.lax.top_k(probs, TOP_K)
        flat_x = x.reshape(T, E)
        flat_idx = topk_idx.reshape(T, TOP_K)
        flat_w = topk_probs.reshape(T, TOP_K)
        gates = jnp.zeros((T, NUM_EXPERTS), dtype=x.dtype)
        gates = gates.at[jnp.arange(T)[:, None], flat_idx].add(flat_w)
        out = jnp.zeros((T, E), dtype=x.dtype)
        for e in range(NUM_EXPERTS):
            h = jax.nn.gelu(flat_x @ w1[e] + b1[e], approximate=False)
            y = h @ w2[e] + b2[e]
            out = out + y * gates[:, e:e + 1]
        return out.reshape(B, N, E)
    edge_index = jnp.stack([src, dst])
    xn = _layernorm(x, axis=-1)
    x = x + _L0_gnn_ref(xn, edge_index, edge_type_8, L0_gnn_W1, L0_gnn_root1, L0_gnn_b1, L0_gnn_W2, L0_gnn_root2, L0_gnn_b2) + _L0_mix_ref(xn[None], L0_mix_W_qkv, L0_mix_b_qkv, L0_mix_W_proj, L0_mix_b_proj, L0_mix_random_features)[0]
    x = x + _L0_ffn_ref(_layernorm(x, axis=-1)[None], L0_ffn_Wg, L0_ffn_bg, L0_ffn_W1, L0_ffn_b1, L0_ffn_W2, L0_ffn_b2, L0_ffn_W3, L0_ffn_b3)[0]
    xn = _layernorm(x, axis=-1)
    x = x + _L1_gnn_ref(xn, edge_index, L1_gnn_W1, L1_gnn_a_src1, L1_gnn_a_dst1, L1_gnn_b1, L1_gnn_g1, L1_gnn_be1, L1_gnn_Wr1, L1_gnn_br1, L1_gnn_W2, L1_gnn_a_src2, L1_gnn_a_dst2, L1_gnn_b2, L1_gnn_g2, L1_gnn_be2, L1_gnn_Wr2, L1_gnn_br2) + _L1_mix_ref(xn[None], L1_mix_w_qkv, L1_mix_w_proj, L1_mix_ln_in_g, L1_mix_ln_in_b, L1_mix_ln_out_g, L1_mix_ln_out_b)[0]
    x = x + _L1_ffn_ref(_layernorm(x, axis=-1)[None], L1_ffn_router_w, L1_ffn_router_b, L1_ffn_w1, L1_ffn_b1, L1_ffn_w2, L1_ffn_b2)[0]
    return x

_drawn_inputs = setup_inputs


def setup_inputs(seed=0):
    import zlib

    import numpy as np

    out = dict(_drawn_inputs(seed))
    spreads = {'L0_gnn_b1': (0.0, 0.8),
     'L0_gnn_b2': (0.0, 2.0),
     'L0_ffn_bg': (0.0, 2.0),
     'L0_ffn_b1': (0.0, 2.0),
     'L0_ffn_b2': (0.0, 2.0),
     'L0_ffn_b3': (0.0, 2.0),
     'L1_gnn_b1': (0.0, 2.0),
     'L1_gnn_g1': (1.0, 0.6),
     'L1_gnn_be1': (0.0, 2.0),
     'L1_gnn_br1': (0.0, 2.0),
     'L1_gnn_b2': (0.0, 2.0),
     'L1_gnn_g2': (1.0, 0.6),
     'L1_gnn_be2': (0.0, 2.0),
     'L1_gnn_br2': (0.0, 2.0),
     'L1_mix_ln_in_g': (1.0, 0.6),
     'L1_mix_ln_in_b': (0.0, 0.8),
     'L1_mix_ln_out_g': (1.0, 0.6),
     'L1_mix_ln_out_b': (0.0, 2.0),
     'L1_ffn_router_b': (0.0, 2.0),
     'L1_ffn_b1': (0.0, 2.0),
     'L1_ffn_b2': (0.0, 2.0)}
    factors = {'L0_mix_W_qkv': 2.824,
     'L0_mix_b_qkv': 6.224,
     'L0_mix_b_proj': 191.602,
     'L0_mix_random_features': 8.0,
     'L1_gnn_a_src1': 200.0,
     'L1_gnn_a_dst1': 200.0,
     'L1_gnn_a_src2': 200.0,
     'L1_gnn_a_dst2': 200.0,
     'L1_ffn_router_w': 16.079,
     'L1_ffn_w1': 20.636,
     'L1_ffn_w2': 15.615,
     'L0_gnn_W1': 2.937,
     'L0_gnn_root1': 5.39,
     'L0_gnn_root2': 4.975,
     'L0_ffn_Wg': 8.0,
     'L0_ffn_W1': 8.0,
     'L0_ffn_W2': 8.0,
     'L0_ffn_W3': 8.0,
     'L1_gnn_W1': 21.827,
     'L1_gnn_Wr1': 8.0,
     'L1_gnn_W2': 61.704,
     'L1_gnn_Wr2': 8.0,
     'L1_mix_w_qkv': 7.827,
     'L1_mix_w_proj': 7.78}
    for name, (base, spread) in spreads.items():
        noise = np.random.default_rng([zlib.crc32(name.encode()), seed]).standard_normal(out[name].shape)
        drawn = base * np.exp(spread * noise) if base else spread * noise
        out[name] = jnp.asarray(drawn.astype(out[name].dtype))
    for name, factor in factors.items():
        out[name] = (out[name] * factor).astype(out[name].dtype)
    return out
```

```python
from contextlib import ExitStack

import concourse.bass as bass
from concourse import mybir

F32 = mybir.dt.float32
F32R = mybir.dt.float32r
I32 = mybir.dt.int32
I16 = mybir.dt.int16
U16 = mybir.dt.uint16
U32 = mybir.dt.uint32
BF16 = mybir.dt.bfloat16
ALU = mybir.AluOpType
ACT = mybir.ActivationFunctionType
AX = mybir.AxisListType
ds = bass.ds

P = 128
NODES = 625
TILES = 5
FULL = TILES - 1
LAST = NODES - FULL * P
COLS = TILES * P
HALF = COLS // 2
EDGES = 10000
EDGE_ROWS = 125
EDGE_COLS = EDGES // EDGE_ROWS
RELS = 8
DIM = 768
KD = DIM // P
WCOL = 384
UNIT = KD * WCOL
BANK = 512
EPS = 1e-5

GROUPS = RELS * TILES
SLOT = 2 * P
SLOTS = (EDGES + GROUPS * (SLOT - 1)) // SLOT
SUBS = 2 * SLOTS

HEADS0, HEAD0 = 12, 64
PAIRS = HEADS0 // 2
FEATS = 256
MIX0_SCALE = (HEAD0 ** -0.5) ** 2 / FEATS

EXPERTS = 8
HID0 = 192
HC0, HP0 = 2, HID0 // 2
HID0B = 2 * HID0
HB0 = HID0B // P
HID1 = 1152
HC1 = HID1 // P
YCOL1 = 256
BELOW = -3e38
GHEADS, GCOL = 4, 256
GAT1 = GHEADS * GCOL
NORM_EPS = 1e-12
SUM_EPS = 1e-16
SLOPE = 0.2
NO_EDGE = -1e30


class Unit:

    def __init__(self, first, i=0, per=0):
        self.n = first + per * i
        self.slot = first % 2
        twice = min(first + 2, 2 * PAIRS) // 2 if self.slot == 0 else 0
        self.loads = 16 * twice + 16 * (first // 2 + 1) + 8 * per * i


class Order:

    def __init__(self, eng, sem):
        self.eng, self.sem, self.before, self.n = eng, sem, 0, 0

    def step(self, ins):
        ins.then_inc(self.sem, 1)
        self.n += 1

    def wait(self):
        self.eng.wait_ge(self.sem, self.before + self.n)

    def enter(self, i, per):
        self.start, self.per = self.before + self.n, per
        self.before, self.n = self.start + per * i, 0

    def leave(self, times):
        assert self.n == self.per, (self.n, self.per)
        self.before, self.n = self.start + self.per * times, 0


def build(nc, a, out):
    with ExitStack() as ctx:
        def dram(name, shape, dt):
            return nc.dram_tensor(name, shape, dt, kind="Internal").ap()

        def sem(name):
            return ctx.enter_context(nc.semaphore(name))

        def sems(name, n):
            return [sem(f"{name}{k}") for k in range(n)]

        def allocator(stack):
            def one(name, shape, dt):
                return stack.enter_context(nc.sbuf_tensor(name, shape, dt))

            def pair(name, shape):
                return one(name + "_hi", shape, F32R), one(name + "_lo", shape, F32R)

            return one, pair

        sorted_dram = dram("edges_sorted", (P * SUBS, 1), I32)
        adj_dram = dram("adjacency", (RELS, P, TILES * COLS), U16)

        keep, keep2 = allocator(ctx)
        X = keep("x_rows", [P, TILES, DIM], F32)
        XT = keep2("xt", [P, KD, COLS])
        raw = [keep(f"weight_raw{s}", [P, UNIT], F32) for s in range(2)]
        W = [keep2(f"weight{s}", [P, UNIT]) for s in range(2)]
        ident = keep("ident", [P, P], F32)
        ones_r = keep("ones_r", [P, P], F32R)
        zero_col = keep("zero_col", [P, 1], F32)
        eps_col = keep("eps_col", [P, 1], F32)
        stats = keep("stats", [P, TILES, 2, 6], F32)
        mv = keep("mean_var", [P, TILES, 2], F32)
        std = keep("std", [P, TILES], F32)
        rstd = keep("rstd", [P, TILES], F32)
        bias_row = [keep(f"bias_row{s}", [P, DIM], F32) for s in range(2)]
        ps = ctx.enter_context(nc.psum_tensor("banks", [P, 8, BANK], F32))

        early = ExitStack()
        er, er2 = allocator(early)
        XN = er("xn_rows", [P, TILES, DIM], F32)
        rf2 = er("rf2", [P, 2, P], F32)
        rfT = er2("rfT", [P, FEATS])
        qk_bias = er("qk_bias", [P, 2 * KD], F32)
        sorted_sb = er("sorted_sb", [P, SUBS], I32)
        part_i = er("part_i", [P, SUBS], I32)
        srcl_f = er("srcl_f", [P, SUBS], F32)
        dst_f = er("dst_f", [P, SUBS], F32)
        dst_iota = er("dst_iota", [P, COLS], I16)
        slot_group = er("slot_group", [1, SLOTS], I32)
        pos_i = er("pos_i", [EDGE_ROWS, EDGE_COLS], I32)
        code_i = er("code_i", [EDGE_ROWS, EDGE_COLS], I32)
        with ExitStack() as here:
            srt, _ = allocator(here)
            src_i = srt("src_i", [EDGE_ROWS, EDGE_COLS], I32)
            dst_i = srt("dst_i", [EDGE_ROWS, EDGE_COLS], I32)
            typ_i = srt("typ_i", [EDGE_ROWS, EDGE_COLS], I32)
            tile_i = srt("tile_i", [EDGE_ROWS, EDGE_COLS], I32)
            low_i = srt("low_i", [EDGE_ROWS, EDGE_COLS], I32)
            sub_i = srt("sub_i", [EDGE_ROWS, EDGE_COLS], I32)
            spot_i = srt("spot_i", [EDGE_ROWS, EDGE_COLS], I32)
            group_f = srt("group_f", [EDGE_ROWS, EDGE_COLS], F32)
            pos_f = srt("pos_f", [EDGE_ROWS, EDGE_COLS], F32)
            iota_g = srt("iota_g", [EDGE_ROWS, GROUPS], F32)
            iota_s = srt("iota_s", [1, SLOTS], F32)
            onehot_g = srt("onehot_g", [EDGE_ROWS, GROUPS, EDGE_COLS], F32)
            restart = srt("restart", [EDGE_ROWS, GROUPS, EDGE_COLS], F32)
            rank = srt("rank", [EDGE_ROWS, GROUPS, EDGE_COLS], F32)
            in_row = srt("in_row", [EDGE_ROWS, GROUPS], F32)
            before = srt("before", [P, P], F32)
            ones_f = srt("ones_f", [P, P], F32)
            ones_g = srt("ones_g", [EDGE_ROWS, GROUPS], F32)
            need_i = srt("need_i", [EDGE_ROWS, GROUPS], I32)
            need_s = srt("need_s", [EDGE_ROWS, GROUPS], I32)
            need_f = srt("need_f", [EDGE_ROWS, GROUPS], F32)
            slot_end = srt("slot_end", [EDGE_ROWS, GROUPS], F32)
            slot_base = srt("slot_base", [EDGE_ROWS, GROUPS], F32)
            offset_g = srt("offset_g", [EDGE_ROWS, GROUPS], F32)
            past = srt("past", [1, SLOTS, GROUPS], F32)
            group_of = srt("group_of", [1, SLOTS], F32)
            fill_i = srt("fill_i", [P, SUBS], I32)
        with ExitStack() as here:
            mx, mx2 = allocator(here)
            attnT = mx2("attnT", [P, KD, COLS])
            qT = mx2("qT", [P, COLS])
            kT = mx2("kT", [P, COLS])
            v = mx2("v", [P, TILES, P])
            v_f = mx("v_f", [P, TILES, P], F32)
            phi_k = mx2("phi_k", [P, TILES, FEATS])
            phi_qT = mx2("phi_qT", [P, 2, COLS])
            kv = mx2("kv", [P, 2, 2, P])
        with ExitStack() as here:
            aj, _ = allocator(here)
            adj = aj("adj", [P, GROUPS, COLS], U16)
            src_hot = [aj(f"src_hot{s}", [P, 2, P], BF16) for s in range(2)]
            dst_hot = [aj(f"dst_hot{s}", [P, 2, COLS], BF16) for s in range(2)]
        early.close()
        with ExitStack() as here:
            rg, rg2 = allocator(here)
            A_r = [rg(f"a_rel{s}", [P, TILES, COLS], F32R) for s in range(2)]
            xn = rg2("xn", [P, TILES, DIM])
            A_u = [rg(f"a_stage{s}", [P, TILES, COLS], U16) for s in range(2)]
            cnt_m = rg("cnt_m", [P, 2, HALF], F32)
            inv = [rg(f"inv{s}", [P, 2, HALF], F32) for s in range(2)]
            ACC = rg("acc_rows", [P, TILES, DIM], F32)
            agg_f = [rg(f"agg_f{s}", [P, HALF], F32) for s in range(3)]

        late = ExitStack()
        lt, lt2 = allocator(late)
        wide = lt("wide_rows", [P, TILES, GAT1], F32)
        XN1 = wide[:, :, 0:DIM]
        with ExitStack() as here:
            ma, _ = allocator(here)
            XM = ma("xm_rows", [P, TILES, DIM], F32)
            Q, K, V = [ma(n, [P, TILES, DIM], F32) for n in ("q_rows", "k_rows", "v_rows")]
            in_gain, in_shift, out_gain, out_shift = [ma(n, [P, DIM], F32) for n in ("in_gain", "in_shift", "out_gain", "out_shift")]
            square = ma("square", [P, DIM], F32)
            norm = ma("norm", [P, 2, TILES], F32)
            norm_m = ma("norm_m", [P, 2, TILES], F32)
            inv_norm = ma("inv_norm", [P, 2, TILES], F32)
        count = lt("count", [P, TILES, COLS], U16)
        absent = lt("absent", [P, TILES, COLS], BF16)
        with ExitStack() as here:
            cs, _ = allocator(here)
            C_u = [cs(f"c_stage{s}", [P, TILES, COLS], U16) for s in range(2)]
            csum = cs("csum", [P, TILES, COLS], F32)
        g_e = [lt(f"att_logit{s}", [P, COLS], F32) for s in range(2)]
        g_p = [lt(f"att_p{s}", [P, COLS], F32) for s in range(2)]
        g_max = lt("att_max", [P, 2], F32)
        g_neg = lt("att_neg", [P, 2], F32)
        g_sum = lt("att_sum", [P, 4 * TILES], F32)
        g_sum_e = lt("att_sum_e", [P, 4 * TILES], F32)
        g_inv = lt("att_inv", [P, 4 * TILES], F32)
        junk = [lt(f"junk{s}", [P, GCOL], F32) for s in range(2)]
        part_of = [lt(f"alpha_part{k}", [P, TILES, 3], F32) for k in range(2)]
        alpha = [[lt(f"alpha{k}_{s}", [P, TILES], F32) for s in range(2)] for k in range(2)]
        with ExitStack() as here:
            g1, g12 = allocator(here)
            PT1 = [g12(f"attT{s}", [P, TILES, P]) for s in range(2)]
            XL1 = [g12(f"xl_head{s}", [P, TILES, GCOL]) for s in range(3)]
            a_row1 = [g1(f"a_row1_{k}", [P, GAT1], F32) for k in range(2)]
            row1 = {n: g1(n + "1_row", [P, GAT1], F32) for n in ("b", "g")}
        with ExitStack() as here:
            g2, g22 = allocator(here)
            XT_more = g22("xt_more", [P, GAT1 // P - KD, COLS])
            PT2 = [g22("att2T", [P, TILES, P])]
            XL2 = [g22("xl2", [P, TILES, DIM])]
            a_row2 = [g2(f"a_row2_{k}", [P, DIM], F32) for k in range(2)]
            diag = [bias_row[0][:, 0:COLS], g2("diag", [P, COLS], F32)]
        late.close()
        with ExitStack() as here:
            fe, fe2 = allocator(here)
            XE = fe("xe_rows", [P, TILES, DIM], F32)
            gate_raw = fe("gate_raw", [P, KD, EXPERTS], F32)
            gate_w = fe2("gate_w", [P, KD, EXPERTS])
            gate_b = fe("gate_b", [P, EXPERTS], F32)
            iota_e = fe("iota_e", [P, EXPERTS], F32)
            scores = fe("scores", [P, TILES, EXPERTS], F32)
            choice = fe("choice", [P, TILES, EXPERTS], F32)
            others = fe("others", [P, TILES, EXPERTS], F32)
            top = [fe(f"top{k}", [P, TILES, 8], F32) for k in range(2)]
            top_at = [fe(f"top_at{k}", [P, TILES, 8], U32) for k in range(2)]
            top_f = [fe(f"top_f{k}", [P, TILES], F32) for k in range(2)]
            diff = fe("diff", [P, TILES, EXPERTS], F32)
            expo = fe("expo", [P, TILES, EXPERTS], F32)
            total = fe("total", [P, TILES], F32)
            share = [fe(f"share{k}", [P, TILES], F32) for k in range(2)]
            comb_k = [fe(f"comb{k}", [P, TILES, EXPERTS], F32) for k in range(2)]
            comb = fe("comb", [P, TILES * EXPERTS], F32)
            combT = fe("combT", [EXPERTS, COLS], F32)
            out_b = fe("out_b", [EXPERTS, DIM], F32)
            in_b_rows = [fe(f"in_b_rows{m}", [P, P], F32) for m in range(2)]
            in_b = [fe(f"in_b{m}", [P, EXPERTS * HC1], F32) for m in range(2)]
            h_f = [fe(f"h_f{s}", [P, COLS], F32) for s in range(2)]
            h1T = fe2("h1T", [P, HC1, COLS])
            h2T = fe2("h2T", [P, HB0, COLS])

        raw_ready = sems("raw_ready", 2)
        hi_ready = sem("hi_ready")
        unit_ready = sem("unit_ready")
        unit_used = sem("unit_used")
        x_in, edges_in, rf_in = sem("x_in"), sem("edges_in"), sem("rf_in")
        bias_in = sem("bias_in")
        pad_zero, consts, masks = sem("pad_zero"), sem("consts"), sem("masks")
        vec_order = sem("vec_order")
        ln_var = sem("ln_var")
        ln_std = sem("ln_std")
        rows_ready = sem("rows_ready")
        tr_full = sem("tr_full")
        tr_hi = sem("tr_hi")
        tr_done = sem("tr_done")
        prod_full = sem("prod_full")
        prod_used = sem("prod_used")
        sort_row = sem("sort_row")
        sort_sum = sem("sort_sum")
        pos_ready = sem("pos_ready")
        filled = sem("filled")
        scattered = sem("scattered")
        sorted_in = sem("sorted_in")
        rf_full, rf_hi = sem("rf_full"), sem("rf_hi")
        A_full, A_hi, A_done = sem("mixA_full"), sem("mixA_hi"), sem("mixA_done")
        B_full, B_val, B_hi, B_done = sem("mixB_full"), sem("mixB_val"), sem("mixB_hi"), sem("mixB_done")
        C_full, C_hi, C_done = sem("mixC_full"), sem("mixC_hi"), sem("mixC_done")
        hot = sem("hot")
        slot_full = sem("slot_full")
        slot_done = sem("slot_done")
        adj_out = sem("adj_out")
        rows_hi = sem("rows_hi")
        rows_lo = sem("rows_lo")
        a_in = [sems(f"a_in{layer}_", 2) for layer in range(2)]
        a_ready = sems("a_ready", 2)
        cnt_full, cnt_used = sems("cnt_full", 2), sems("cnt_used", 2)
        agg_full, agg_val, agg_hi, agg_done = sems("agg_full", 2), sems("agg_val", 2), sems("agg_hi", 2), sems("agg_done", 2)
        tra_full, tra_used = sems("tra_full", 2), sems("tra_used", 2)
        ends = {e: sem(f"{e}_end") for e in ("pe", "act", "vec")}
        gate_in = sems("gate_in", 2)
        gate_split = sems("gate_split", 2)
        gate_full = sems("gate_full", 2)
        gate_arg = sems("gate_arg", 2)
        gate_exp = sems("gate_exp", 2)
        comb_ready = sems("comb_ready", 2)
        comb_full = sems("comb_full", 2)
        combT_ready = sems("combT_ready", 2)
        in_b_full = sems("in_b_full", 2)
        in_b_ready = sems("in_b_ready", 2)
        h_full = sems("h_full", 2)
        h_act = sems("h_act", 2)
        h_lo = sems("h_lo", 2)
        y_full = sems("y_full", 2)
        y_used = sems("y_used", 2)
        mix_in, kv_rows, kv_full, norm_done = sem("mix_in"), sem("kv_rows"), sem("kv_full"), sem("norm_done")
        c_in = sems("c_in", 2)
        c_added = sem("c_added")
        c_full, c_done = sem("c_full"), sem("c_done")
        gat_in = sems("gat_in", 2)
        late_in = sems("late_in", 2)
        xl_full = sems("xl_full", 2)
        xl_hi = sems("xl_hi", 2)
        xl_done = sems("xl_done", 2)
        diag_ready = sems("diag_ready", 2)
        row_full = sems("row_full", 2)
        e_ready = sems("e_ready", 2)
        e_exp = sems("e_exp", 2)
        p_ready = sems("p_ready", 2)
        pt_full = sems("pt_full", 2)
        pt_hi = sems("pt_hi", 2)
        pt_done = sems("pt_done", 2)
        o_full = sems("o_full", 2)
        o_used = sems("o_used", 2)
        stored = sem("stored")

        U_MIX = 0
        U_PROJ = U_MIX + 2 * PAIRS
        U_ROOT1 = U_PROJ + 2
        U_REL = [U_ROOT1 + 2, U_ROOT1 + 2 + 2 * RELS + 2]
        U_ROOT2 = U_REL[1] - 2
        U_FFN0 = U_REL[1] + 2 * RELS
        U_MIX1 = U_FFN0 + 4 * EXPERTS
        U_XL = [U_MIX1 + 8, U_MIX1 + 8 + 2 * GHEADS]
        U_SKIP = [U_XL[0] + GHEADS, U_XL[1] + DIM // GCOL]
        U_FFN = [U_FFN0, U_SKIP[1] + DIM // GCOL]

        FFN_UNITS = [[(P, KD, HID0), (HP0, HC0, HID0B), (P, HB0, WCOL), (P, HB0, WCOL)],
                     [(P, KD, WCOL)] * 3 + [(P, HC1, YCOL1)] * 3]
        HIDDEN = [[(0, c * HP0, HP0, XT, h1T, c, 0) for c in range(HC0)] + [(1, c * P, P, h1T, h2T, c, 1) for c in range(HB0)],
                  [(c // 3, c % 3 * P, P, XT, h1T, c, 0) for c in range(HC1)]]
        OUTPUT = [(2, 2, WCOL, HB0, h2T), (3, 3, YCOL1, HC1, h1T)]
        IN_B = [[(HC0, HP0), (HB0, P)], [(HC1, P)]]
        Y_BANKS = [4, 3]
        FREE_H, FREE_LO = 2, 2
        LN_FFN, LN_IN1, LN_MIX_IN, LN_MIX_OUT, LN_GAT = [1, 7], 2, 3, 4, [5, 6]
        ROWS_0, ROWS_H, ROWS_FFN, ROWS_MIX_IN, ROWS_MIX_OUT, ROWS_H1 = 0, TILES, [2 * TILES, 6 * TILES], 3 * TILES, 4 * TILES, 5 * TILES
        SET = 2 * TILES
        TR_0, TR_H, TR_MIX_IN, TR_MIX_OUT, TR_XN1, TR_H1 = 0, SET, 3 * SET, 4 * SET, 5 * SET, 6 * SET
        TR_FFN = [2 * SET, TR_H1 + 3 * TILES]
        PR_PROJ, PR_ROOT1, PR_ROOT2, PR_Q, PR_K, PR_V, PR_MIX1 = 0, SET, 2 * SET, 4 * SET, 5 * SET, 6 * SET, 7 * SET
        PR_SKIP = [8 * SET, 8 * SET + GHEADS * TILES]
        PR_FFN = [3 * SET, PR_SKIP[1] + DIM // GCOL * TILES]
        GAT = [(GHEADS, 1, KD), (1, DIM // GCOL, GAT1 // P)]

        FREE_A, FREE_B, FREE_C = 4, 2, 2
        FREE_AGG, FREE_TRA, FREE_CNT = 4, 2 * TILES, 2
        AGGS = 2 * KD
        FREE_BUF = 2
        FREE_DONE = 3
        FREE_SUM = 1
        FREE_HOT = 2
        LAST_PHASE = 13

        def mm3(pe, dst, s, m, start, stop):
            pe.matmul(dst, s[0], m[0], start=start, stop=False)
            pe.matmul(dst, s[0], m[1], start=False, stop=False)
            return pe.matmul(dst, s[1], m[0], start=False, stop=stop)

        def at(pair, *idx):
            return pair[0][idx], pair[1][idx]

        def unit_view(slot, k, n, rows=P):
            return [w[0:rows, 0:k * n].rearrange("p (k n) -> p k n", k=k) for w in W[slot]]

        def chunks(w):
            return w.rearrange("(k p) o -> p k o", p=P)

        def f32(ap):
            return ap.bitcast(F32)

        def end_phase(eng, me, n):
            eng.drain().then_inc(ends[me], 1)
            for e in ends:
                if e != me:
                    eng.wait_ge(ends[e], n)

        def after_phase(eng, n):
            for e in ends:
                eng.wait_ge(ends[e], n)

        def groups_of(kd):
            return [range(c, min(c + 3, kd)) for c in range(0, kd, 3)]

        def chunk_of(g):
            return (XT, g) if g < KD else (XT_more, g - KD)

        def cols_half(n):
            return slice((n % 2) * HALF, (n % 2 + 1) * HALF)

        def halves(ap):
            return ap.rearrange("p (h n) -> p h n", h=2)

        def wcols(c):
            return slice(c * WCOL, (c + 1) * WCOL)

        block = ctx.enter_context(nc.Block())

        @block.sync
        def _(sp):
            def load(u, *parts):
                if not (isinstance(u.n, int) and u.n < 2):
                    sp.wait_ge(unit_ready, u.n - 1)
                at_word = 0
                for src in parts:
                    rows, k, n = src.shape
                    dst = raw[u.slot][0:rows, at_word:at_word + k * n].rearrange("p (k n) -> p k n", k=k)
                    sp.dma_start(dst, src).then_inc(raw_ready[u.slot], 16)
                    at_word += k * n

            def store():
                sp.dma_start(out[0:FULL * P, :].rearrange("(t p) d -> p t d", p=P), X[:, 0:FULL, :]).then_inc(stored, 16)
                sp.dma_start(out[FULL * P:NODES, :], X[0:LAST, FULL, :]).then_inc(stored, 16)
                sp.wait_ge(stored, 32)

            x = a["x"]
            sp.dma_start(X[:, 0:FULL, :], x[0:FULL * P, :].rearrange("(t p) d -> p t d", p=P)).then_inc(x_in, 16)
            sp.wait_ge(pad_zero, 1)
            sp.dma_start(X[0:LAST, FULL, :], x[FULL * P:NODES, :]).then_inc(x_in, 16)
            for t, n in ((src_i, "src"), (dst_i, "dst"), (typ_i, "edge_type_8")):
                sp.dma_start(t[:, :], a[n].rearrange("(p c) -> p c", p=EDGE_ROWS)).then_inc(edges_in, 16)
            qkv = a["L0_mix_W_qkv"].rearrange("(k p) (s o) -> p k s o", p=P, s=3)
            load(Unit(U_MIX), qkv[:, :, 0, 0:P], qkv[:, :, 1, 0:P])
            load(Unit(U_MIX + 1), qkv[:, :, 2, 0:P])
            with sp.Fori(1, PAIRS) as j:
                load(Unit(U_MIX, j, 2), qkv[:, :, 0, ds(j * P, P)], qkv[:, :, 1, ds(j * P, P)])
                load(Unit(U_MIX + 1, j, 2), qkv[:, :, 2, ds(j * P, P)])
            for c in range(2):
                load(Unit(U_PROJ + c), chunks(a["L0_mix_W_proj"])[:, :, wcols(c)])
            sp.wait_ge(scattered, 16 * EDGE_COLS)
            sp.dma_start(sorted_sb[:, :], sorted_dram.rearrange("(p c) o -> p (c o)", p=P)).then_inc(sorted_in, 16)
            sp.wait_ge(slot_done, FREE_SUM + SLOTS)
            sp.dma_start(adj_dram.rearrange("r p c -> p r c"), adj[:, :, :].rearrange("p (r t) c -> p r (t c)", r=RELS)).then_inc(adj_out, 16)
            sp.wait_ge(adj_out, 16)
            for c in range(2):
                load(Unit(U_ROOT1 + c), chunks(a["L0_gnn_root1"])[:, :, wcols(c)])
            after_phase(sp, 4)
            for layer in range(2):
                w = a[("L0_gnn_W1", "L0_gnn_W2")[layer]].rearrange("r (k p) o -> r p k o", p=P)
                if layer == 1:
                    for c in range(2):
                        load(Unit(U_ROOT2 + c), chunks(a["L0_gnn_root2"])[:, :, wcols(c)])
                    after_phase(sp, 6)
                with sp.Fori(0, RELS // 2) as i:
                    for b in range(2):
                        sp.wait_ge(a_ready[layer], 2 * i + b + 1)
                        sp.dma_start(A_u[b][:, :, :].rearrange("p t c -> p (t c)"),
                                     adj_dram[ds(2 * i + b, 1), :, :].rearrange("r p c -> (r p) c")).then_inc(a_in[layer][b], 16)
                        for c in range(2):
                            load(Unit(U_REL[layer] + 2 * b + c, i, 4),
                                 w[ds(2 * i + b, 1), :, :, wcols(c)].rearrange("r p k o -> (r p) k o"))
            def expert_loads(n, first, units):
                with sp.Fori(0, EXPERTS // 2) as i:
                    for b in range(2):
                        for c, w in enumerate(units):
                            load(Unit(first + b * len(units) + c, i, 2 * len(units)),
                                 w[ds(2 * i + b, 1)].rearrange("e p k o -> (e p) k o"))

            w1 = a["L0_ffn_W1"].rearrange("e (k p) o -> e p k o", p=P)
            w2 = a["L0_ffn_W2"].rearrange("e (k p) o -> e p k o", p=HP0)
            w3 = a["L0_ffn_W3"].rearrange("e (k p) o -> e p k o", p=P)
            expert_loads(0, U_FFN[0], [w1, w2] + [w3[:, :, :, wcols(c)] for c in range(2)])
            with sp.Fori(0, 3) as i:
                for c in range(2):
                    load(Unit(U_MIX1 + c, i, 2), chunks(a["L1_mix_w_qkv"])[:, :, ds((2 * i + c) * WCOL, WCOL)])
            for c in range(2):
                load(Unit(U_MIX1 + 6 + c), chunks(a["L1_mix_w_proj"])[:, :, wcols(c)])
            after_phase(sp, 9)
            with sp.Fori(0, RELS // 2) as i:
                for b in range(2):
                    sp.wait_ge(c_added, 2 * i + b + 1)
                    sp.dma_start(C_u[b][:, :, :].rearrange("p t c -> p (t c)"),
                                 adj_dram[ds(2 * i + b, 1), :, :].rearrange("r p c -> (r p) c")).then_inc(c_in[b], 16)
            for layer in range(2):
                units = DIM // GCOL if layer else GHEADS
                for first, name in ((U_XL, ("L1_gnn_W1", "L1_gnn_W2")), (U_SKIP, ("L1_gnn_Wr1", "L1_gnn_Wr2"))):
                    for c in range(units):
                        load(Unit(first[layer] + c), chunks(a[name[layer]])[:, :, c * GCOL:(c + 1) * GCOL])
            w1 = a["L1_ffn_w1"].rearrange("e (k p) o -> e p k o", p=P)
            w2 = a["L1_ffn_w2"].rearrange("e (k p) o -> e p k o", p=P)
            expert_loads(1, U_FFN[1], [w1[:, :, :, wcols(c)] for c in range(3)] + [w2[:, :, :, c * YCOL1:(c + 1) * YCOL1] for c in range(3)])
            after_phase(sp, LAST_PHASE)
            store()

        @block.gpsimd
        def _(pool):
            def split(u, n, rows=P):
                s = u.slot
                pool.wait_ge(raw_ready[s], u.loads)
                if not (isinstance(u.n, int) and u.n < 2):
                    pool.wait_ge(unit_used, u.n - 1)
                hi, lo = at(W[s], slice(0, rows), slice(0, n))
                pool.tensor_tensor(hi, raw[s][0:rows, 0:n], zero_col[0:rows, :].broadcast_to([rows, n]), ALU.add).then_inc(hi_ready, 1)
                pool.wait_ge(hi_ready, u.n + 1)
                pool.tensor_tensor(lo, raw[s][0:rows, 0:n], f32(hi), ALU.subtract).then_inc(unit_ready, 1)

            def split_rest(first, times, per, n):
                with pool.Fori(0, times) as i:
                    for c in range(per):
                        split(Unit(first + c, i, per), n)

            pool.memset(X[:, FULL, :], 0.0).then_inc(pad_zero, 1)
            pool.memset(ident[:, :], 0.0).then_inc(consts, 1)
            pool.memset(before[:, :], 0.0).then_inc(consts, 1)
            pool.memset(fill_i[:, :], -1).then_inc(consts, 1)
            pool.memset(eps_col[:, :], EPS).then_inc(consts, 1)
            pool.memset(ones_f[:, :], 1.0).then_inc(consts, 1)
            pool.memset(f32(ones_r[:, :]), 1.0).then_inc(consts, 1)
            pool.memset(ones_g[:, :], 1.0).then_inc(consts, 1)
            pool.memset(restart[:, :, 1:EDGE_COLS], 1.0).then_inc(consts, 1)
            pool.memset(restart[:, :, 0:1], 0.0).then_inc(consts, 1)
            pool.iota(iota_g[:, :], [[1, GROUPS]], base=0, channel_multiplier=0, allow_small_or_imprecise_dtypes=True).then_inc(consts, 1)
            pool.iota(iota_s[:, :], [[1, SLOTS]], base=0, channel_multiplier=0, allow_small_or_imprecise_dtypes=True).then_inc(consts, 1)
            pool.iota(dst_iota[:, :], [[1, COLS]], base=0, channel_multiplier=0, allow_small_or_imprecise_dtypes=True).then_inc(consts, 1)
            pool.memset(zero_col[:, :], 0.0).then_inc(consts, 1)
            pool.wait_ge(consts, 13)
            pool.affine_select(out=ident[:, :], in_=ident[:, :], compare_op=ALU.not_equal, fill=1.0, base=0,
                               pattern=[[-1, P]], channel_multiplier=1).then_inc(masks, 1)
            pool.affine_select(out=before[:, :], in_=before[:, :], compare_op=ALU.is_ge, fill=1.0, base=0,
                               pattern=[[-1, P]], channel_multiplier=1).then_inc(masks, 1)
            pool.wait_ge(filled, 16)
            pool.wait_ge(pos_ready, 1)
            sent = 0
            for j in range(PAIRS):
                for c in range(2):
                    split(Unit(U_MIX + 2 * j + c), KD * P * (2 - c))
                    while sent < min(EDGE_COLS, (2 * j + c + 1) * 8):
                        pool.indirect_dma_start(out=sorted_dram, out_offset=bass.IndirectOffsetOnAxis(ap=pos_i[:, sent:sent + 1], axis=0),
                                                in_=code_i[:, sent:sent + 1], in_offset=None).then_inc(scattered, 16)
                        sent += 1
            split_rest(U_PROJ, 1, 2, UNIT)
            split_rest(U_ROOT1, 1, 2, UNIT)
            split_rest(U_REL[0], RELS, 2, UNIT)
            split_rest(U_ROOT2, 1, 2, UNIT)
            split_rest(U_REL[1], RELS, 2, UNIT)
            def expert_splits(n):
                pool.iota(iota_e[:, :], [[1, EXPERTS]], base=0, channel_multiplier=0, allow_small_or_imprecise_dtypes=True).then_inc(consts, 1)
                units = FFN_UNITS[n]
                with pool.Fori(0, EXPERTS // 2) as i:
                    for b in range(2):
                        for c, (rows, k, cols) in enumerate(units):
                            split(Unit(U_FFN[n] + b * len(units) + c, i, 2 * len(units)), k * cols, rows)

            after_phase(pool, 7)
            expert_splits(0)
            split_rest(U_MIX1, 4, 2, UNIT)
            split_rest(U_XL[0], GHEADS, 2, KD * GCOL)
            split_rest(U_XL[1], DIM // GCOL, 2, GAT1 // P * GCOL)
            after_phase(pool, 12)
            expert_splits(1)

        @block.scalar
        def _(act):
            def std_of(n):
                act.wait_ge(ln_var, TILES * (n + 1))
                act.activation(std[:, :], mv[:, :, 1], ACT.Sqrt, bias=eps_col[:, :]).then_inc(ln_std, 1)

            def transposes_hi(start, kd=KD):
                g = start
                for t in range(TILES):
                    for ks in groups_of(kd):
                        (into, k), n = chunk_of(ks[0]), len(ks)
                        act.wait_ge(tr_full, g + 1)
                        act.activation(into[0][:, k:k + n, t * P:(t + 1) * P], ps[:, g % 8, 0:n * P].rearrange("p (k n) -> p k n", k=n),
                                       ACT.Copy).then_inc(tr_hi, 1)
                        g += 1

            def rows_split_hi(src, ready):
                for t in range(TILES):
                    ready(t)
                    act.activation(xn[0][:, t, :], src[:, t, :], ACT.Copy).then_inc(rows_hi, 1)

            act.wait_ge(consts, 12)
            act.dma_start(sorted_dram.rearrange("(p c) o -> p (c o)", p=P), fill_i[:, :]).then_inc(filled, 16)
            act.dma_start(bias_row[0][:, :], a["L0_mix_b_qkv"][2 * DIM:3 * DIM].partition_broadcast(P)).then_inc(bias_in, 16)
            act.dma_start(bias_row[1][:, :], a["L0_mix_b_proj"].partition_broadcast(P)).then_inc(bias_in, 16)
            for h in range(2):
                act.dma_start(rf2[:, :, h * HEAD0:(h + 1) * HEAD0], a["L0_mix_random_features"].rearrange("(c p) d -> p c d", p=P)).then_inc(rf_in, 16)
            act.dma_start(qk_bias[:, :], a["L0_mix_b_qkv"][0:2 * DIM].rearrange("(j p) -> p j", p=P), allow_slow_non_contiguous=True).then_inc(rf_in, 16)
            std_of(0)
            transposes_hi(TR_0)
            act.wait_ge(rf_full, 1)
            act.activation(rfT[0][:, :], ps[:, 2, 0:FEATS], ACT.Copy).then_inc(rf_hi, 1)
            end_phase(act, "act", 1)
            with act.Fori(0, PAIRS) as j:
                for n in range(2):
                    act.wait_ge(A_full, 12 * j + 2 * n + 2)
                    act.activation(halves((qT, kT)[n][0][:, :]), ps[:, 2 * n:2 * n + 2, 0:HALF], ACT.Identity,
                                   bias=qk_bias[:, ds(n * KD + j, 1)]).then_inc(A_hi, 2)
                for n in range(2):
                    t = slice(4 * n, min(4 * n + 4, TILES))
                    act.wait_ge(B_val, 2 * j + n + 1)
                    act.activation(v[0][:, t, :], v_f[:, t, :], ACT.Copy).then_inc(B_hi, 1)
                for s in range(2):
                    for n in range(3):
                        t = slice(2 * n, min(2 * n + 2, TILES))
                        w = t.stop - t.start
                        act.wait_ge(B_full, 10 * j + 4 * s + n + 3)
                        act.activation(phi_k[0][:, t, :], ps[:, 4 + n % 2, 0:w * FEATS].rearrange("p (t m) -> p t m", t=w),
                                       ACT.Relu).then_inc(B_hi, 1)
                    for n in range(2):
                        act.wait_ge(A_full, 12 * j + 4 * s + 2 * n + 6)
                        act.activation(halves(phi_qT[0][:, n, :]), ps[:, 2 * n:2 * n + 2, 0:HALF], ACT.Relu).then_inc(A_hi, 2)
                    act.wait_ge(B_full, 10 * j + 4 * s + 6)
                    act.activation(kv[0][:, :, s, s * HEAD0:(s + 1) * HEAD0], ps[:, 5, 0:2 * HEAD0].rearrange("p (m d) -> p m d", m=2),
                                   ACT.Copy).then_inc(B_hi, 1)
                act.wait_ge(C_full, 2 * j + 2)
                act.activation(attnT[0][:, ds(j, 1), :].rearrange("p k (h n) -> p (k h) n", h=2), ps[:, 6:8, 0:HALF], ACT.Copy,
                               scale=MIX0_SCALE).then_inc(C_hi, 1)
            end_phase(act, "act", 2)
            act.dma_start(bias_row[0][:, :], a["L0_gnn_b1"].partition_broadcast(P)).then_inc(bias_in, 16)
            act.dma_start(bias_row[1][:, :], a["L0_gnn_b2"].partition_broadcast(P)).then_inc(bias_in, 16)
            end_phase(act, "act", 3)
            act.wait_ge(adj_out, 16)
            rows_split_hi(XN, lambda t: None)
            end_phase(act, "act", 4)
            for layer in range(2):
                if layer == 1:
                    rows_split_hi(ACC, lambda t: act.wait_ge(rows_ready, ROWS_H + t + 1))
                    transposes_hi(TR_H)
                    end_phase(act, "act", 6)
                act.sem_inc(a_ready[layer], FREE_BUF)
                with act.Fori(0, RELS // 2) as i:
                    for b in range(2):
                        act.wait_ge(a_in[layer][b], 16 * i + 16)
                        act.wait_ge(agg_full[layer], AGGS * (2 * i + b + 1))
                        act.activation(A_r[b][:, :, :], A_u[b][:, :, :], ACT.Copy).then_inc(a_ready[layer], 1)
                        for n in range(AGGS):
                            act.wait_ge(agg_val[layer], FREE_AGG + AGGS * (2 * i + b) + n + 1)
                            act.activation(XT[0][:, n // 2, cols_half(n)], agg_f[n % 3][:, :], ACT.Copy).then_inc(agg_hi[layer], 1)
                end_phase(act, "act", (5, 7)[layer])

            def experts(n, router_w, router_b, out_bias, in_biases):
                act.dma_start(gate_raw[:, :, :], chunks(router_w)).then_inc(gate_in[n], 16)
                act.dma_start(gate_b[:, :], router_b.partition_broadcast(P)).then_inc(gate_in[n], 16)
                act.dma_start(out_b[:, :], out_bias).then_inc(gate_in[n], 16)
                for m, src in enumerate(in_biases):
                    count, width = IN_B[n][m]
                    act.dma_start(in_b_rows[m][0:EXPERTS * count, 0:width], src.rearrange("e (c p) -> (e c) p", p=width)).then_inc(gate_in[n], 16)
                std_of(LN_FFN[n])
                transposes_hi(TR_FFN[n])
                for m, (count, width) in enumerate(IN_B[n]):
                    act.wait_ge(in_b_full[n], m + 1)
                    act.activation(in_b[m][0:width, 0:EXPERTS * count], ps[0:width, 3 + m, 0:EXPERTS * count], ACT.Copy).then_inc(in_b_ready[n], 1)
                act.wait_ge(gate_arg[n], 1)
                act.activation(expo[:, :, :], diff[:, :, :], ACT.Exp).then_inc(gate_exp[n], 1)
                act.wait_ge(in_b_ready[n], len(IN_B[n]))
                act.sem_inc(h_act[n], FREE_H)
                steps = HIDDEN[n]
                with act.Fori(0, EXPERTS // 2) as i:
                    for b in range(2):
                        for g, (_, _, width, _, into, c, m) in enumerate(steps):
                            at_step = 2 * len(steps) * i + b * len(steps) + g
                            act.wait_ge(h_lo[n], at_step + 1)
                            act.wait_ge(h_full[n], at_step + 1)
                            pair = (b * len(steps) + g) % 2
                            bias = in_b[m][0:width, ds((2 * i + b) * IN_B[n][m][0] + c, 1)]
                            banks = ps[0:width, 2 * pair:2 * pair + 2, 0:HALF]
                            act.activation(halves(into[0][0:width, c, :]), banks, ACT.Gelu, bias=bias)
                            act.activation(halves(h_f[pair][0:width, :]), banks, ACT.Gelu, bias=bias).then_inc(h_act[n], 1)

            experts(0, a["L0_ffn_Wg"], a["L0_ffn_bg"], a["L0_ffn_b3"], [a["L0_ffn_b1"], a["L0_ffn_b2"]])
            end_phase(act, "act", 8)

            for t, name in ((in_gain, "ln_in_g"), (in_shift, "ln_in_b"), (out_gain, "ln_out_g"), (out_shift, "ln_out_b")):
                act.dma_start(t[:, :], a["L1_mix_" + name].partition_broadcast(P)).then_inc(mix_in, 16)
            std_of(LN_IN1)
            std_of(LN_MIX_IN)
            transposes_hi(TR_MIX_IN)
            for n, (rows, start) in enumerate(((Q, PR_Q), (K, PR_K))):
                for t in range(TILES):
                    act.wait_ge(prod_used, start + TILES + t + 1)
                    if n * TILES + t > 0:
                        act.wait_ge(norm_done, n * TILES + t)
                    act.activation(square[:, :], rows[:, t, :], ACT.Square, accum_out=norm[:, n, t:t + 1]).then_inc(norm_done, 1)
            act.wait_ge(norm_done, 2 * TILES)
            act.activation(norm[:, :, :], norm[:, :, :], ACT.Sqrt).then_inc(norm_done, 1)
            std_of(LN_MIX_OUT)
            transposes_hi(TR_MIX_OUT)
            end_phase(act, "act", 9)
            transposes_hi(TR_XN1)
            end_phase(act, "act", 10)

            def gat(layer):
                heads, units, kd = GAT[layer]
                tiles = heads * TILES
                XL, PT, a_row = ((XL1, PT1, a_row1), (XL2, PT2, a_row2))[layer]

                def xl_chunk(h, u, t):
                    n = (h * units + u) * TILES + t
                    act.wait_ge(xl_full[layer], n + 1)
                    if h >= len(XL):
                        act.wait_ge(o_full[layer], (h - len(XL) + 1) * TILES)
                    act.activation(XL[h % len(XL)][0][:, t, u * GCOL:(u + 1) * GCOL], ps[:, n % 2, 0:GCOL], ACT.Copy).then_inc(xl_hi[layer], 1)

                def weights_hi(g):
                    act.wait_ge(pt_full[layer], g + 1)
                    r = len(PT)
                    if g >= r:
                        act.wait_ge(o_full[layer], g - r + 1)
                    hi = PT[g % r][0]
                    act.activation(hi[:, 0:FULL, :], ps[:, 4, 0:FULL * P].rearrange("p (t n) -> p t n", t=FULL), ACT.Copy)
                    act.activation(hi[:, FULL, :], ps[:, 5, 0:P], ACT.Copy).then_inc(pt_hi[layer], 1)

                def exponentials(g):
                    act.wait_ge(e_ready[layer], g + 1)
                    act.activation(g_e[g % 2][:, :], g_e[g % 2][:, :], ACT.Exp, bias=g_neg[:, g % 2:g % 2 + 1]).then_inc(e_exp[layer], 1)

                for u in range(units):
                    for t in range(TILES):
                        xl_chunk(0, u, t)
                for g in range(tiles + 2):
                    h, t = g // TILES, g % TILES
                    if h + 1 < heads:
                        xl_chunk(h + 1, 0, t)
                    if 0 <= g - 2 < tiles:
                        weights_hi(g - 2)
                    if g < tiles:
                        exponentials(g)
                act.wait_ge(xl_done[layer], heads * units * TILES)
                for k, n in enumerate(("be", "br")):
                    act.dma_start(a_row[k][:, :], a[f"L1_gnn_{n}{layer + 1}"].partition_broadcast(P)).then_inc(late_in[layer], 16)
                std_of(LN_GAT[layer])
                if layer == 0:
                    transposes_hi(TR_H1, GAT1 // P)

            for k, n in enumerate(("L1_gnn_a_src1", "L1_gnn_a_dst1")):
                act.dma_start(a_row1[k][:, :], a[n].rearrange("h c -> (h c)").partition_broadcast(P)).then_inc(gat_in[0], 16)
            for n in row1:
                act.dma_start(row1[n][:, :], a[f"L1_gnn_{n}1"].partition_broadcast(P)).then_inc(gat_in[0], 16)
            gat(0)
            end_phase(act, "act", 11)
            for k, n in enumerate(("L1_gnn_a_src2", "L1_gnn_a_dst2")):
                act.dma_start(a_row2[k][:, :], a[n].rearrange("h c -> (h c)").partition_broadcast(P)).then_inc(gat_in[1], 16)
            act.dma_start(bias_row[0][:, :], a["L1_gnn_b2"].partition_broadcast(P)).then_inc(gat_in[1], 16)
            act.dma_start(bias_row[1][:, :], a["L1_gnn_g2"].partition_broadcast(P)).then_inc(gat_in[1], 16)
            gat(1)
            end_phase(act, "act", 12)
            experts(1, a["L1_ffn_router_w"], a["L1_ffn_router_b"], a["L1_ffn_b2"], [a["L1_ffn_b1"]])
            end_phase(act, "act", 13)

        @block.vector
        def _(vec):
            order = Order(vec, vec_order)

            def normalise(n, src, dst, ready=True, width=DIM):
                for t in range(TILES):
                    for c in range(2):
                        order.step(vec.bn_stats(stats[:, t, c, :], src[:, t, c * width // 2:(c + 1) * width // 2]))
                order.wait()
                for t in range(TILES):
                    vec.bn_aggr(mv[:, t, :], stats[:, t, :, :]).then_inc(ln_var, 1)
                vec.wait_ge(ln_std, n + 1)
                order.step(vec.reciprocal(rstd[:, :], std[:, :]))
                order.wait()
                for t in range(TILES):
                    ins = vec.tensor_scalar(dst[:, t, :], src[:, t, :], mv[:, t, 0:1], rstd[:, t:t + 1], ALU.subtract, ALU.mult)
                    if ready:
                        ins.then_inc(rows_ready, 1)
                    else:
                        order.step(ins)

            def transposes_lo(start, kd=KD):
                g = start
                for t in range(TILES):
                    for ks in groups_of(kd):
                        (into, k), n = chunk_of(ks[0]), len(ks)
                        vec.wait_ge(tr_hi, g + 1)
                        hi, lo = at(into, slice(None), slice(k, k + n), slice(t * P, (t + 1) * P))
                        vec.tensor_tensor(lo, ps[:, g % 8, 0:n * P].rearrange("p (k n) -> p k n", k=n), f32(hi), ALU.subtract).then_inc(tr_done, 1)
                        g += 1

            def rows_split_lo(n, src):
                for t in range(TILES):
                    vec.wait_ge(rows_hi, TILES * n + t + 1)
                    vec.tensor_tensor(xn[1][:, t, :], src[:, t, :], f32(xn[0][:, t, :]), ALU.subtract).then_inc(rows_lo, 1)

            def add_products(start, rows, bias=None, units=2, cols=WCOL):
                for j in range(units * TILES):
                    g = start + j
                    c, t = j // TILES, j % TILES
                    col = slice(c * cols, (c + 1) * cols)
                    vec.wait_ge(prod_full, g + 1)
                    vec.tensor_tensor(rows[:, t, col], ps[:, g % 8, 0:cols],
                                      rows[:, t, col] if bias is None else bias[:, col], ALU.add).then_inc(prod_used, 1)

            def take_products(start, rows):
                for j in range(SET):
                    c, t = j // TILES, j % TILES
                    vec.wait_ge(prod_full, start + j + 1)
                    vec.tensor_copy(rows[:, t, wcols(c)], ps[:, (start + j) % 8, 0:WCOL]).then_inc(prod_used, 1)

            def scale_shift(rows, gain, shift, ready):
                order.wait()
                for t in range(TILES):
                    order.step(vec.tensor_tensor(rows[:, t, :], rows[:, t, :], gain[:, :], ALU.mult))
                order.wait()
                for t in range(TILES):
                    ins = vec.tensor_tensor(rows[:, t, :], rows[:, t, :], shift[:, :], ALU.add)
                    if ready:
                        ins.then_inc(rows_ready, 1)
                    else:
                        order.step(ins)

            def add_bias(rows, bias):
                for t in range(TILES):
                    order.step(vec.tensor_tensor(rows[:, t, :], rows[:, t, :], bias[:, :], ALU.add))

            vec.wait_ge(x_in, 32)
            vec.wait_ge(pad_zero, 1)
            normalise(0, X, XN)
            transposes_lo(TR_0)
            vec.wait_ge(rf_hi, 1)
            order.step(vec.tensor_tensor(rfT[1][:, :], ps[:, 2, 0:FEATS], f32(rfT[0][:, :]), ALU.subtract))
            vec.wait_ge(edges_in, 48)
            vec.wait_ge(consts, 12)
            order.step(vec.tensor_scalar(tile_i[:, :], src_i[:, :], 7, None, ALU.arith_shift_right))
            order.step(vec.tensor_scalar(low_i[:, :], src_i[:, :], P - 1, None, ALU.bitwise_and))
            order.wait()
            order.step(vec.scalar_tensor_tensor(group_f[:, :], typ_i[:, :], float(TILES), tile_i[:, :], ALU.mult, ALU.add))
            order.step(vec.scalar_tensor_tensor(code_i[:, :], low_i[:, :], 1024.0, dst_i[:, :], ALU.mult, ALU.add))
            order.wait()
            every = [EDGE_ROWS, GROUPS, EDGE_COLS]
            order.step(vec.tensor_tensor(onehot_g[:, :, :], group_f[:, :].unsqueeze(1).broadcast_to(every),
                                         iota_g[:, :].unsqueeze(2).broadcast_to(every), ALU.is_equal))
            order.wait()
            order.step(vec.tensor_tensor_scan(rank[:, :, :].rearrange("p g c -> p (g c)"), restart[:, :, :].rearrange("p g c -> p (g c)"),
                                              onehot_g[:, :, :].rearrange("p g c -> p (g c)"), 0.0, ALU.mult, ALU.add))
            order.wait()
            vec.tensor_copy(in_row[:, :], rank[:, :, EDGE_COLS - 1]).then_inc(sort_row, 1)
            vec.wait_ge(sort_sum, 2)
            order.step(vec.tensor_scalar(need_i[:, :], ps[0:EDGE_ROWS, 1, 0:GROUPS], float(SLOT - 1), None, ALU.add))
            order.wait()
            order.step(vec.tensor_scalar(need_s[:, :], need_i[:, :], SLOT.bit_length() - 1, None, ALU.arith_shift_right))
            order.wait()
            order.step(vec.tensor_copy(need_f[:, :], need_s[:, :]))
            order.wait()
            order.step(vec.tensor_tensor_scan(slot_end[:, :], ones_g[:, :], need_f[:, :], 0.0, ALU.mult, ALU.add))
            order.wait()
            order.step(vec.tensor_tensor(slot_base[:, :], slot_end[:, :], need_f[:, :], ALU.subtract))
            order.wait()
            order.step(vec.scalar_tensor_tensor(offset_g[:, :], slot_base[:, :], float(SLOT), ps[0:EDGE_ROWS, 0, 0:GROUPS], ALU.mult, ALU.add))
            order.wait()
            order.step(vec.scalar_tensor_tensor(rank[:, :, :], rank[:, :, :], -1.0, offset_g[:, :].unsqueeze(2).broadcast_to(every), ALU.add, ALU.add))
            order.wait()
            order.step(vec.tensor_tensor(rank[:, :, :], rank[:, :, :], onehot_g[:, :, :], ALU.mult))
            order.wait()
            order.step(vec.tensor_reduce(pos_f[:, :], rank[:, :, :].rearrange("p g c -> p c g"), AX.X, ALU.add))
            order.wait()
            order.step(vec.tensor_copy(spot_i[:, :], pos_f[:, :]))
            order.wait()
            order.step(vec.tensor_scalar(low_i[:, :], spot_i[:, :], P - 1, None, ALU.bitwise_and))
            order.step(vec.tensor_scalar(sub_i[:, :], spot_i[:, :], 7, None, ALU.arith_shift_right))
            order.wait()
            vec.scalar_tensor_tensor(pos_i[:, :], low_i[:, :], float(SUBS), sub_i[:, :], ALU.mult, ALU.add).then_inc(pos_ready, 1)
            sg = [1, SLOTS, GROUPS]
            order.step(vec.tensor_tensor(past[:, :, :], slot_end[0:1, :].unsqueeze(1).broadcast_to(sg), iota_s[:, :].unsqueeze(2).broadcast_to(sg), ALU.is_le))
            order.wait()
            order.step(vec.tensor_reduce(group_of[:, :], past[:, :, :], AX.X, ALU.add))
            order.wait()
            order.step(vec.tensor_scalar(slot_group[:, :], group_of[:, :], float(GROUPS - 1), None, ALU.min))
            vec.wait_ge(bias_in, 32)
            add_bias(X, bias_row[1])
            end_phase(vec, "vec", 1)
            for part in kv:
                order.step(vec.memset(f32(part[:, :, :, :]), 0.0))
            vec.sem_inc(A_done, FREE_A)
            vec.sem_inc(B_done, FREE_B)
            vec.sem_inc(C_done, FREE_C)
            with vec.Fori(0, PAIRS) as j:
                for n in range(2):
                    t = (qT, kT)[n]
                    vec.wait_ge(A_hi, 12 * j + 2 * n + 2)
                    vec.scalar_tensor_tensor(halves(t[1][:, :]), ps[:, 2 * n:2 * n + 2, 0:HALF], qk_bias[:, ds(n * KD + j, 1)], halves(f32(t[0][:, :])),
                                             ALU.add, ALU.subtract).then_inc(A_done, 2)
                for n in range(2):
                    t = slice(4 * n, min(4 * n + 4, TILES))
                    w = t.stop - t.start
                    vec.wait_ge(B_full, 10 * j + n + 1)
                    vec.tensor_tensor(v_f[:, t, :], ps[:, 4 + n, 0:w * P].rearrange("p (t d) -> p t d", t=w),
                                      bias_row[0][:, ds(j * P, P)].unsqueeze(1).broadcast_to([P, w, P]), ALU.add).then_inc(B_val, 1)
                for n in range(2):
                    t = slice(4 * n, min(4 * n + 4, TILES))
                    vec.wait_ge(B_hi, 10 * j + n + 1)
                    vec.tensor_tensor(v[1][:, t, :], v_f[:, t, :], f32(v[0][:, t, :]), ALU.subtract).then_inc(B_done, 1)
                for s in range(2):
                    for n in range(3):
                        t = slice(2 * n, min(2 * n + 2, TILES))
                        w = t.stop - t.start
                        vec.wait_ge(B_hi, 10 * j + 4 * s + n + 3)
                        vec.scalar_tensor_tensor(phi_k[1][:, t, :], ps[:, 4 + n % 2, 0:w * FEATS].rearrange("p (t m) -> p t m", t=w), 0.0,
                                                 f32(phi_k[0][:, t, :]), ALU.max, ALU.subtract).then_inc(B_done, 1)
                    for n in range(2):
                        vec.wait_ge(A_hi, 12 * j + 4 * s + 2 * n + 6)
                        vec.scalar_tensor_tensor(halves(phi_qT[1][:, n, :]), ps[:, 2 * n:2 * n + 2, 0:HALF], 0.0, halves(f32(phi_qT[0][:, n, :])),
                                                 ALU.max, ALU.subtract).then_inc(A_done, 2)
                    vec.wait_ge(B_hi, 10 * j + 4 * s + 6)
                    own = slice(s * HEAD0, (s + 1) * HEAD0)
                    vec.tensor_tensor(kv[1][:, :, s, own], ps[:, 5, 0:2 * HEAD0].rearrange("p (m d) -> p m d", m=2),
                                      f32(kv[0][:, :, s, own]), ALU.subtract).then_inc(B_done, 1)
                vec.wait_ge(C_hi, j + 1)
                hi, lo = [t[:, ds(j, 1), :].rearrange("p k (h n) -> p (k h) n", h=2) for t in attnT]
                vec.scalar_tensor_tensor(lo, ps[:, 6:8, 0:HALF], MIX0_SCALE, f32(hi), ALU.mult, ALU.subtract).then_inc(C_done, 2)
            add_products(PR_PROJ, X)
            end_phase(vec, "vec", 2)
            order.step(vec.memset(adj[:, :, :], 0))
            vec.wait_ge(sorted_in, 16)
            order.step(vec.tensor_scalar(part_i[:, :], sorted_sb[:, :], 10, None, ALU.arith_shift_right))
            order.wait()
            order.step(vec.tensor_copy(srcl_f[:, :], part_i[:, :]))
            order.step(vec.tensor_scalar(sorted_sb[:, :], sorted_sb[:, :], 1023, None, ALU.bitwise_and))
            order.wait()
            order.step(vec.tensor_copy(dst_f[:, :], sorted_sb[:, :]))
            order.wait()
            vec.sem_inc(slot_done, FREE_SUM)
            with vec.Fori(0, SLOTS // 2) as i:
                for b in range(2):
                    vec.wait_ge(slot_full, 2 * i + b + 1)
                    for h in range(2):
                        sub = ds(4 * i + 2 * b + h, 1)
                        vec.tensor_scalar(src_hot[b][:, h, :], dst_iota[:, 0:P], srcl_f[:, sub], None, ALU.is_equal)
                        ins = vec.tensor_scalar(dst_hot[b][:, h, :], dst_iota[:, :], dst_f[:, sub], None, ALU.is_equal)
                        ins.then_inc(hot, 1)
                for b in range(2):
                    g = vec.value_load(slot_group[0:1, ds(2 * i + b, 1)], min_val=0, max_val=GROUPS - 1)
                    vec.wait_ge(slot_full, FREE_HOT + 2 * i + b + 1)
                    vec.wait_ge(slot_done, 2 * i + b + 1)
                    block_of = adj[:, ds(g, 1), :].rearrange("p g (h c) -> p (g h) c", h=2)
                    vec.tensor_tensor(block_of, block_of, ps[:, 2 * b:2 * b + 2, 0:HALF], ALU.add).then_inc(slot_done, 1)
            end_phase(vec, "vec", 3)
            vec.wait_ge(adj_out, 16)
            rows_split_lo(0, XN)
            vec.wait_ge(bias_in, 64)
            add_products(PR_ROOT1, ACC, bias_row[0])
            add_bias(X, bias_row[1])
            end_phase(vec, "vec", 4)
            for layer in range(2):
                rows = (ACC, X)[layer]
                if layer == 1:
                    for t in range(TILES):
                        vec.tensor_scalar(ACC[:, t, :], ACC[:, t, :], 0.0, None, ALU.max).then_inc(rows_ready, 1)
                    rows_split_lo(1, ACC)
                    transposes_lo(TR_H)
                    add_products(PR_ROOT2, X)
                    end_phase(vec, "vec", 6)
                vec.sem_inc(cnt_used[layer], FREE_CNT)
                vec.sem_inc(agg_val[layer], FREE_AGG)
                vec.sem_inc(agg_done[layer], FREE_DONE)
                vec.sem_inc(tra_used[layer], FREE_TRA)
                with vec.Fori(0, RELS // 2) as i:
                    for b in range(2):
                        for n in range(2):
                            vec.wait_ge(cnt_full[layer], 4 * i + 2 * b + n + 1)
                            vec.tensor_scalar(cnt_m[:, n, :], ps[:, 6 + n, 0:HALF], 1.0, None, ALU.max).then_inc(cnt_used[layer], 1)
                        vec.wait_ge(cnt_used[layer], FREE_CNT + 4 * i + 2 * b + 2)
                        if b == 0:
                            order.enter(i, 2)
                        order.step(vec.reciprocal(inv[b][:, :, :], cnt_m[:, :, :]))
                        order.wait()
                        for n in range(AGGS + 1):
                            if n < AGGS:
                                vec.wait_ge(agg_full[layer], FREE_BUF * AGGS + AGGS * (2 * i + b) + n + 1)
                                vec.wait_ge(agg_done[layer], AGGS * (2 * i + b) + n + 1)
                                vec.tensor_tensor(agg_f[n % 3][:, :], ps[:, n % 4, 0:HALF], inv[b][:, n % 2, :], ALU.mult).then_inc(agg_val[layer], 1)
                            if n > 0:
                                m = n - 1
                                vec.wait_ge(agg_hi[layer], AGGS * (2 * i + b) + m + 1)
                                vec.tensor_tensor(XT[1][:, m // 2, cols_half(m)], agg_f[m % 3][:, :], f32(XT[0][:, m // 2, cols_half(m)]),
                                                  ALU.subtract).then_inc(agg_done[layer], 1)
                        for n in range(2 * TILES):
                            c, t = n // TILES, n % TILES
                            vec.wait_ge(tra_full[layer], 2 * TILES * (2 * i + b) + n + 1)
                            vec.wait_ge(tra_used[layer], 2 * TILES * (2 * i + b) + n + 1)
                            vec.tensor_tensor(rows[:, t, wcols(c)], rows[:, t, wcols(c)], ps[:, 4 + n % 2, 0:WCOL], ALU.add).then_inc(tra_used[layer], 1)
                order.leave(RELS // 2)
                end_phase(vec, "vec", (5, 7)[layer])

            def experts(n):
                normalise(LN_FFN[n], X, XE)
                transposes_lo(TR_FFN[n])
                vec.wait_ge(gate_in[n], 16 * (3 + len(IN_B[n])))
                order.step(vec.tensor_copy(gate_w[0][:, :, :], gate_raw[:, :, :]))
                order.wait()
                vec.tensor_tensor(gate_w[1][:, :, :], gate_raw[:, :, :], f32(gate_w[0][:, :, :]), ALU.subtract).then_inc(gate_split[n], 1)
                every = [P, TILES, EXPERTS]
                vec.wait_ge(gate_full[n], 1)
                order.step(vec.tensor_tensor(scores[:, :, :], ps[:, 0, 0:TILES * EXPERTS].rearrange("p (t e) -> p t e", t=TILES),
                                             gate_b[:, :].unsqueeze(1).broadcast_to(every), ALU.add))
                order.wait()
                if n == 1:
                    order.step(vec.tensor_reduce(total[:, :], scores[:, :, :], AX.X, ALU.max))
                    order.wait()
                    vec.tensor_tensor(diff[:, :, :], scores[:, :, :], total[:, :].unsqueeze(2).broadcast_to(every), ALU.subtract).then_inc(gate_arg[n], 1)
                    vec.wait_ge(gate_exp[n], 1)
                    order.step(vec.tensor_reduce(total[:, :], expo[:, :, :], AX.X, ALU.add))
                    order.wait()
                    order.step(vec.reciprocal(share[0][:, :], total[:, :]))
                    order.wait()
                    order.step(vec.tensor_tensor(choice[:, :, :], expo[:, :, :], share[0][:, :].unsqueeze(2).broadcast_to(every), ALU.mult))
                    order.wait()
                values = (scores, choice)[n]
                vec.wait_ge(consts, 14 + n)
                for k in range(2):
                    src = values if k == 0 else others
                    for t in range(TILES):
                        order.step(vec.max(top[k][:, t, :], src[:, t, :]))
                    order.wait()
                    for t in range(TILES):
                        order.step(vec.max_index(top_at[k][:, t, :], top[k][:, t, :], src[:, t, :]))
                    order.wait()
                    order.step(vec.tensor_copy(top_f[k][:, :], top_at[k][:, :, 0]))
                    order.wait()
                    order.step(vec.tensor_tensor(comb_k[k][:, :, :], top_f[k][:, :].unsqueeze(2).broadcast_to(every),
                                                 iota_e[:, :].unsqueeze(1).broadcast_to(every), ALU.is_equal))
                    order.wait()
                    if k == 0:
                        order.step(vec.scalar_tensor_tensor(others[:, :, :], comb_k[k][:, :, :], BELOW, values[:, :, :], ALU.mult, ALU.add))
                        order.wait()
                if n == 0:
                    vec.tensor_tensor(diff[:, :, :], scores[:, :, :], top[0][:, :, 0].unsqueeze(2).broadcast_to(every), ALU.subtract).then_inc(gate_arg[n], 1)
                    vec.wait_ge(gate_exp[n], 1)
                    order.step(vec.tensor_tensor(choice[:, :, :], expo[:, :, :], comb_k[1][:, :, :], ALU.mult))
                    order.wait()
                    order.step(vec.tensor_tensor(choice[:, :, :], choice[:, :, :], comb_k[0][:, :, :], ALU.add))
                    order.wait()
                    order.step(vec.tensor_reduce(total[:, :], choice[:, :, :], AX.X, ALU.add))
                    order.wait()
                    order.step(vec.reciprocal(share[0][:, :], total[:, :]))
                    order.wait()
                    weights = share[0][:, :].unsqueeze(2).broadcast_to(every)
                else:
                    order.step(vec.tensor_tensor(comb_k[0][:, :, :], comb_k[0][:, :, :], comb_k[1][:, :, :], ALU.add))
                    order.wait()
                    weights = comb_k[0][:, :, :]
                vec.tensor_tensor(comb[:, :].rearrange("p (t e) -> p t e", t=TILES), choice[:, :, :], weights, ALU.mult).then_inc(comb_ready[n], 1)
                vec.wait_ge(comb_full[n], 1)
                vec.tensor_copy(combT[:, 0:FULL * P], ps[0:EXPERTS, 5, 0:FULL * P]).then_inc(combT_ready[n], 1)
                vec.tensor_copy(combT[:, FULL * P:COLS], ps[0:EXPERTS, 6, 0:P]).then_inc(combT_ready[n], 1)
                add_products(PR_FFN[n], X)
                vec.wait_ge(prod_used, PR_FFN[n] + SET)
                steps = HIDDEN[n]
                _, units, cols, _, _ = OUTPUT[n]
                chunks_y = units * TILES
                vec.sem_inc(h_lo[n], FREE_LO)
                vec.sem_inc(y_used[n], chunks_y)
                with vec.Fori(0, EXPERTS // 2) as i:
                    for b in range(2):
                        for g, (_, _, width, _, into, c, _) in enumerate(steps):
                            vec.wait_ge(h_act[n], FREE_H + 2 * len(steps) * i + b * len(steps) + g + 1)
                            vec.tensor_tensor(into[1][0:width, c, :], h_f[(b * len(steps) + g) % 2][0:width, :], f32(into[0][0:width, c, :]),
                                              ALU.subtract).then_inc(h_lo[n], 1)
                        for c in range(units):
                            for t in range(TILES):
                                y = (b * units + c) * TILES + t
                                vec.wait_ge(y_full[n], 2 * chunks_y * i + y + 1)
                                vec.wait_ge(y_used[n], 2 * chunks_y * i + y + 1)
                                rows = X[:, t, c * cols:(c + 1) * cols]
                                vec.scalar_tensor_tensor(rows, ps[:, 4 + y % Y_BANKS[n], 0:cols], comb[:, ds(2 * i + b + t * EXPERTS, 1)], rows,
                                                         ALU.mult, ALU.add).then_inc(y_used[n], 1)

            experts(0)
            end_phase(vec, "vec", 8)

            normalise(LN_IN1, X, XN1, ready=False)
            order.wait()
            normalise(LN_MIX_IN, XN1, XM, ready=False)
            vec.wait_ge(mix_in, 64)
            scale_shift(XM, in_gain, in_shift, True)
            transposes_lo(TR_MIX_IN)
            for start, rows in ((PR_Q, Q), (PR_K, K), (PR_V, V)):
                take_products(start, rows)
            vec.wait_ge(norm_done, 2 * TILES + 1)
            order.step(vec.tensor_scalar(norm_m[:, :, :], norm[:, :, :], NORM_EPS, None, ALU.max))
            order.wait()
            order.step(vec.reciprocal(inv_norm[:, :, :], norm_m[:, :, :]))
            order.wait()
            vec.wait_ge(prod_used, PR_V + SET)
            for t in range(TILES):
                vec.scalar_tensor_tensor(K[:, t, :], K[:, t, :], inv_norm[:, 1, t:t + 1], V[:, t, :], ALU.mult, ALU.mult).then_inc(kv_rows, 1)
            vec.wait_ge(kv_full, 2)
            for t in range(TILES):
                rows = Q[:, t, :].rearrange("p (c n) -> p c n", c=2)
                order.step(vec.scalar_tensor_tensor(rows, rows, inv_norm[:, 0, t:t + 1], ps[:, 0:2, 0:WCOL], ALU.mult, ALU.mult))
            order.wait()
            normalise(LN_MIX_OUT, Q, Q, ready=False)
            scale_shift(Q, out_gain, out_shift, True)
            transposes_lo(TR_MIX_OUT)
            add_products(PR_MIX1, X)
            end_phase(vec, "vec", 9)
            transposes_lo(TR_XN1)
            order.step(vec.memset(csum[:, :, :], 0.0))
            order.wait()
            vec.sem_inc(c_added, FREE_BUF)
            with vec.Fori(0, RELS // 2) as i:
                for b in range(2):
                    vec.wait_ge(c_in[b], 16 * i + 16)
                    vec.wait_ge(c_added, 2 * i + b + FREE_BUF)
                    vec.tensor_tensor(csum[:, :, :], csum[:, :, :], C_u[b][:, :, :], ALU.add).then_inc(c_added, 1)
            vec.wait_ge(c_added, RELS + FREE_BUF)
            for t in range(TILES):
                own = csum[:, t, t * P:(t + 1) * P]
                vec.tensor_tensor(own, own, ident[:, :], ALU.add).then_inc(c_added, 1)
            for t in range(TILES):
                vec.wait_ge(c_full, t + 1)
                order.step(vec.tensor_copy(count[:, t, 0:FULL * P], ps[:, 2 * (t % 2), 0:FULL * P]))
                order.step(vec.tensor_copy(count[:, t, FULL * P:COLS], ps[:, 2 * (t % 2) + 1, 0:P]))
                order.wait()
                vec.tensor_scalar(absent[:, t, :], count[:, t, :], 0.0, NO_EDGE, ALU.is_equal, ALU.mult).then_inc(c_done, 1)
            end_phase(vec, "vec", 10)

            def gat(layer):
                heads, units, kd = GAT[layer]
                tiles = heads * TILES
                XL, PT, a_row = ((XL1, PT1, a_row1), (XL2, PT2, a_row2))[layer]
                width = units * GCOL

                def xl_chunk(h, u, t):
                    n = (h * units + u) * TILES + t
                    vec.wait_ge(xl_hi[layer], n + 1)
                    chunk = ps[:, n % 2, 0:GCOL]
                    hi, lo = at(XL[h % len(XL)], slice(None), t, slice(u * GCOL, (u + 1) * GCOL))
                    order.step(vec.tensor_tensor(lo, chunk, f32(hi), ALU.subtract))
                    if n > 0:
                        vec.wait_ge(xl_done[layer], n)
                    for k in range(2):
                        sums = part_of[k][:, t, u:u + 1] if units > 1 else alpha[k][h % 2][:, t:t + 1]
                        col = slice((h * units + u) * GCOL, (h * units + u + 1) * GCOL)
                        ins = vec.scalar_tensor_tensor(junk[k][:, :], chunk, 1.0, a_row[k][:, col], ALU.mult, ALU.mult, accum_out=sums)
                        if k == 0:
                            order.step(ins)
                        else:
                            ins.then_inc(xl_done[layer], 1)

                def diagonal(h):
                    vec.wait_ge(xl_done[layer], (h + 1) * units * TILES)
                    order.wait()
                    if units > 1:
                        for k in range(2):
                            order.step(vec.tensor_reduce(alpha[k][h % 2][:, :], part_of[k][:, :, :], AX.X, ALU.add))
                        order.wait()
                    if h > 0:
                        vec.wait_ge(row_full[layer], h)
                    for t in range(TILES):
                        vec.tensor_scalar(diag[layer][:, t * P:(t + 1) * P], ident[:, :], alpha[0][h % 2][:, t:t + 1], None, ALU.mult).then_inc(diag_ready[layer], 1)

                def logits(g):
                    h, t, s = g // TILES, g % TILES, g % 2
                    vec.wait_ge(row_full[layer], h + 1)
                    if g >= 2:
                        vec.wait_ge(p_ready[layer], g - 1)
                    e = g_e[s]
                    order.step(vec.tensor_scalar(halves(e[:, :]), ps[:, 2:4, 0:HALF], alpha[1][h % 2][:, t:t + 1], None, ALU.add))
                    order.wait()
                    order.step(vec.scalar_tensor_tensor(e[:, :], e[:, :], SLOPE, e[:, :], ALU.mult, ALU.max))
                    order.wait()
                    order.step(vec.tensor_tensor(e[:, :], e[:, :], absent[:, t, :], ALU.add))
                    order.wait()
                    order.step(vec.tensor_reduce(g_max[:, s:s + 1], e[:, :], AX.X, ALU.max))
                    order.wait()
                    vec.tensor_scalar(g_neg[:, s:s + 1], g_max[:, s:s + 1], -1.0, None, ALU.mult).then_inc(e_ready[layer], 1)

                def weights(g):
                    vec.wait_ge(e_exp[layer], g + 1)
                    if g >= 2:
                        vec.wait_ge(pt_full[layer], g - 1)
                    vec.scalar_tensor_tensor(g_p[g % 2][:, :], g_e[g % 2][:, :], 1.0, count[:, g % TILES, :], ALU.mult, ALU.mult,
                                             accum_out=g_sum[:, g:g + 1]).then_inc(p_ready[layer], 1)

                def weights_lo(g):
                    vec.wait_ge(pt_hi[layer], g + 1)
                    hi, lo = PT[g % len(PT)]
                    order.step(vec.tensor_tensor(lo[:, 0:FULL, :], ps[:, 4, 0:FULL * P].rearrange("p (t n) -> p t n", t=FULL), f32(hi[:, 0:FULL, :]), ALU.subtract))
                    vec.tensor_tensor(lo[:, FULL, :], ps[:, 5, 0:P], f32(hi[:, FULL, :]), ALU.subtract).then_inc(pt_done[layer], 1)
                    order.step(vec.tensor_scalar(g_sum_e[:, g:g + 1], g_sum[:, g:g + 1], SUM_EPS, None, ALU.add))
                    order.wait()
                    order.step(vec.reciprocal(g_inv[:, g:g + 1], g_sum_e[:, g:g + 1]))

                def output(g):
                    h, t = g // TILES, g % TILES
                    vec.wait_ge(o_full[layer], g + 1)
                    order.wait()
                    if layer == 0:
                        vec.tensor_scalar(wide[:, t, h * GCOL:(h + 1) * GCOL], ps[:, 6 + g % 2, 0:GCOL], g_inv[:, g:g + 1], None, ALU.mult).then_inc(o_used[layer], 1)
                    else:
                        vec.tensor_scalar(wide[:, t, 0:DIM].rearrange("p (c n) -> p c n", c=2), ps[:, 6:8, 0:WCOL], g_inv[:, g:g + 1], None,
                                          ALU.mult).then_inc(o_used[layer], 1)

                vec.wait_ge(gat_in[layer], 64)
                for u in range(units):
                    for t in range(TILES):
                        xl_chunk(0, u, t)
                diagonal(0)
                for g in range(tiles + 4):
                    h, t = g // TILES, g % TILES
                    if 0 <= g - 3 < tiles:
                        weights_lo(g - 3)
                    if 0 <= g - 4 < tiles:
                        output(g - 4)
                    if g < tiles:
                        logits(g)
                    if 0 <= g - 1 < tiles:
                        weights(g - 1)
                    if h + 1 < heads:
                        xl_chunk(h + 1, 0, t)
                        if t == FULL:
                            diagonal(h + 1)
                rows = wide if layer == 0 else wide[:, :, 0:DIM]
                bias, gain = (row1["b"], row1["g"]) if layer == 0 else bias_row
                vec.wait_ge(o_used[layer], tiles)
                for t in range(TILES):
                    order.step(vec.tensor_tensor(rows[:, t, :], rows[:, t, :], bias[:, :], ALU.add))
                order.wait()
                normalise(LN_GAT[layer], rows, rows, ready=False, width=heads * width)
                if layer == 0:
                    vec.wait_ge(late_in[0], 32)
                    scale_shift(rows, gain, a_row[0], False)
                    order.wait()
                    for j in range(heads * TILES):
                        n = PR_SKIP[0] + j
                        c, t = j // TILES, j % TILES
                        mine = rows[:, t, c * GCOL:(c + 1) * GCOL]
                        vec.wait_ge(prod_full, n + 1)
                        vec.scalar_tensor_tensor(mine, mine, 0.0, ps[:, n % 8, 0:GCOL], ALU.max, ALU.add).then_inc(prod_used, 1)
                    vec.wait_ge(prod_used, PR_SKIP[0] + heads * TILES)
                    for t in range(TILES):
                        vec.tensor_tensor(rows[:, t, :], rows[:, t, :], a_row[1][:, :], ALU.add).then_inc(rows_ready, 1)
                    transposes_lo(TR_H1, GAT1 // P)
                else:
                    vec.wait_ge(late_in[1], 32)
                    scale_shift(rows, gain, a_row[0], False)
                    order.wait()
                    for t in range(TILES):
                        order.step(vec.tensor_tensor(rows[:, t, :], rows[:, t, :], a_row[1][:, :], ALU.add))
                    order.wait()
                    add_products(PR_SKIP[1], rows, units=units, cols=GCOL)
                    vec.wait_ge(prod_used, PR_SKIP[1] + units * TILES)
                    for t in range(TILES):
                        order.step(vec.tensor_tensor(X[:, t, :], X[:, t, :], rows[:, t, :], ALU.add))
                    order.wait()

            gat(0)
            end_phase(vec, "vec", 11)
            gat(1)
            end_phase(vec, "vec", 12)
            experts(1)
            end_phase(vec, "vec", 13)

        @block.tensor
        def _(pe):
            def transposes(start, src, ready=None, kd=KD):
                g = start
                for t in range(TILES):
                    if ready is not None:
                        pe.wait_ge(rows_ready, ready + t + 1)
                    for ks in groups_of(kd):
                        if g >= 8:
                            pe.wait_ge(tr_done, g - 7)
                        for k in ks:
                            ins = pe.transpose(ps[:, g % 8, (k - ks[0]) * P:(k - ks[0] + 1) * P], src[:, t, k * P:(k + 1) * P], ident[:, :])
                        ins.then_inc(tr_full, 1)
                        g += 1
                return g

            def products(start, first, act_of, kd=KD, units=2, cols=WCOL):
                g = start
                for c in range(units):
                    pe.wait_ge(unit_ready, first + c + 1)
                    w = unit_view((first + c) % 2, kd, cols)
                    for t in range(TILES):
                        if g >= 8:
                            pe.wait_ge(prod_used, g - 7)
                        for k in range(kd):
                            act_t, m = act_of(k)
                            ins = mm3(pe, ps[:, g % 8, 0:cols], at(act_t, slice(None), m, slice(t * P, (t + 1) * P)), at(w, slice(None), k),
                                      k == 0, k == kd - 1)
                        ins.then_inc(prod_full, 1)
                        g += 1
                    used()

            def used(n=1):
                pe.drain().then_inc(unit_used, n)

            pe.wait_ge(masks, 2)
            transposes(TR_0, XN, ROWS_0)
            pe.wait_ge(rf_in, 48)
            pe.wait_ge(tr_done, 10)
            for c in range(2):
                ins = pe.transpose(ps[:, 2, c * P:(c + 1) * P], rf2[:, c, :], ident[:, :])
            ins.then_inc(rf_full, 1)
            pe.wait_ge(sort_row, 1)
            pe.wait_ge(consts, 12)
            pe.matmul(ps[0:EDGE_ROWS, 0, 0:GROUPS], before[0:EDGE_ROWS, 0:EDGE_ROWS], in_row[:, :], start=True, stop=True).then_inc(sort_sum, 1)
            pe.matmul(ps[0:EDGE_ROWS, 1, 0:GROUPS], ones_f[0:EDGE_ROWS, 0:EDGE_ROWS], in_row[:, :], start=True, stop=True).then_inc(sort_sum, 1)
            pe.wait_ge(pos_ready, 1)
            end_phase(pe, "pe", 1)
            with pe.Fori(0, PAIRS) as j:
                pe.wait_ge(unit_ready, U_MIX + 2 * j + 1)
                w = [x[:, 0:KD * 2 * P].rearrange("p (s k o) -> p s k o", k=KD, s=2) for x in W[0]]
                for n in range(4):
                    pe.wait_ge(A_done, 12 * j + n + 1)
                    for k in range(KD):
                        ins = mm3(pe, ps[:, n, 0:HALF], at(w, slice(None), n // 2, k), at(XT, slice(None), k, cols_half(n)), k == 0, k == KD - 1)
                    ins.then_inc(A_full, 1)
                pe.wait_ge(unit_ready, U_MIX + 2 * j + 2)
                w = unit_view(1, KD, P)
                for n in range(2):
                    pe.wait_ge(B_done, 10 * j + n + 1)
                    for t in range(4 * n, min(4 * n + 4, TILES)):
                        for k in range(KD):
                            ins = mm3(pe, ps[:, 4 + n, (t - 4 * n) * P:(t - 4 * n + 1) * P], at(XT, slice(None), k, slice(t * P, (t + 1) * P)),
                                      at(w, slice(None), k), k == 0, k == KD - 1)
                    ins.then_inc(B_full, 1)
                used(2)
                for s in range(2):
                    rows = slice(s * HEAD0, (s + 1) * HEAD0)
                    pe.wait_ge(A_done, FREE_A + 12 * j + 4)
                    for n in range(3):
                        pe.wait_ge(B_done, 10 * j + 4 * s + n + 3)
                        for t in range(2 * n, min(2 * n + 2, TILES)):
                            ins = mm3(pe, ps[:, 4 + n % 2, (t - 2 * n) * FEATS:(t - 2 * n + 1) * FEATS], at(kT, rows, slice(t * P, (t + 1) * P)),
                                      at(rfT, rows), True, True)
                        ins.then_inc(B_full, 1)
                    for n in range(4):
                        pe.wait_ge(A_done, 12 * j + 4 * s + n + 5)
                        mm3(pe, ps[:, n, 0:HALF], at(rfT, rows, slice((n // 2) * P, (n // 2 + 1) * P)), at(qT, rows, cols_half(n)),
                            True, True).then_inc(A_full, 1)
                    pe.wait_ge(B_done, FREE_B + 10 * j + 4 * s + 5)
                    for m in range(2):
                        for t in range(TILES):
                            rows_of = LAST if t == FULL else P
                            ins = mm3(pe, ps[:, 5, m * HEAD0:(m + 1) * HEAD0], at(phi_k, slice(0, rows_of), t, slice(m * P, (m + 1) * P)),
                                      at(v, slice(0, rows_of), t, rows), t == 0, t == TILES - 1)
                    ins.then_inc(B_full, 1)
                    pe.wait_ge(B_done, FREE_B + 10 * j + 4 * s + 6)
                    pe.wait_ge(A_done, FREE_A + 12 * j + 4 * s + 8)
                    for n in range(2):
                        if s == 0:
                            pe.wait_ge(C_done, 2 * j + n + 1)
                        for m in range(2):
                            ins = mm3(pe, ps[:, 6 + n, 0:HALF], at(kv, slice(None), m, s), at(phi_qT, slice(None), m, cols_half(n)),
                                      s == 0 and m == 0, s == 1 and m == 1)
                        if s == 1:
                            ins.then_inc(C_full, 1)
            pe.wait_ge(C_done, FREE_C + 2 * PAIRS)
            products(PR_PROJ, U_PROJ, lambda k: (attnT, k))
            end_phase(pe, "pe", 2)
            pe.sem_inc(slot_full, FREE_HOT)
            with pe.Fori(0, SLOTS // 2) as i:
                for b in range(2):
                    pe.wait_ge(hot, 4 * i + 2 * b + 2)
                    for n in range(2):
                        for h in range(2):
                            ins = pe.matmul(ps[:, 2 * b + n, 0:HALF], src_hot[b][:, h, :], dst_hot[b][:, h, cols_half(n)], start=(h == 0), stop=(h == 1))
                    ins.then_inc(slot_full, 1)
            end_phase(pe, "pe", 3)
            products(PR_ROOT1, U_ROOT1, chunk_of)
            end_phase(pe, "pe", 4)
            for layer in range(2):
                if layer == 1:
                    transposes(TR_H, ACC, ROWS_H)
                    pe.wait_ge(tr_done, 4 * TILES)
                    products(PR_ROOT2, U_ROOT2, chunk_of)
                    end_phase(pe, "pe", 6)
                pe.sem_inc(agg_full[layer], FREE_BUF * AGGS)
                with pe.Fori(0, RELS // 2) as i:
                    for b in range(2):
                        pe.wait_ge(a_ready[layer], FREE_BUF + 2 * i + b + 1)
                        for n in range(2):
                            pe.wait_ge(cnt_used[layer], 4 * i + 2 * b + n + 1)
                            for t in range(TILES):
                                ins = pe.matmul(ps[:, 6 + n, 0:HALF], ones_r[:, :], A_r[b][:, t, cols_half(n)], start=(t == 0), stop=(t == TILES - 1))
                            ins.then_inc(cnt_full[layer], 1)
                        for n in range(AGGS):
                            pe.wait_ge(agg_val[layer], AGGS * (2 * i + b) + n + 1)
                            k = slice((n // 2) * P, (n // 2 + 1) * P)
                            for t in range(TILES):
                                for part in range(2):
                                    ins = pe.matmul(ps[:, n % 4, 0:HALF], xn[part][:, t, k], A_r[b][:, t, cols_half(n)],
                                                    start=(t == 0 and part == 0), stop=(t == FULL and part == 1))
                            ins.then_inc(agg_full[layer], 1)
                        pe.wait_ge(agg_done[layer], FREE_DONE + AGGS * (2 * i + b + 1))
                        for c in range(2):
                            pe.wait_ge(unit_ready, U_REL[layer] + 4 * i + 2 * b + c + 1)
                            w = unit_view(c, KD, WCOL)
                            for t in range(TILES):
                                n = c * TILES + t
                                pe.wait_ge(tra_used[layer], FREE_TRA - 2 + 2 * TILES * (2 * i + b) + n + 1)
                                for k in range(KD):
                                    ins = mm3(pe, ps[:, 4 + n % 2, 0:WCOL], at(XT, slice(None), k, slice(t * P, (t + 1) * P)), at(w, slice(None), k),
                                              k == 0, k == KD - 1)
                                ins.then_inc(tra_full[layer], 1)
                            used()
                end_phase(pe, "pe", (5, 7)[layer])

            def experts(n):
                transposes(TR_FFN[n], XE, ROWS_FFN[n])
                pe.wait_ge(tr_done, TR_FFN[n] + SET)
                pe.wait_ge(gate_in[n], 16 * (3 + len(IN_B[n])))
                for m, (count, width) in enumerate(IN_B[n]):
                    pe.transpose(ps[0:width, 3 + m, 0:EXPERTS * count], in_b_rows[m][0:EXPERTS * count, 0:width],
                                 ident[0:EXPERTS * count, 0:EXPERTS * count]).then_inc(in_b_full[n], 1)
                pe.wait_ge(gate_split[n], 1)
                for t in range(TILES):
                    for k in range(KD):
                        ins = mm3(pe, ps[:, 0, t * EXPERTS:(t + 1) * EXPERTS], at(XT, slice(None), k, slice(t * P, (t + 1) * P)),
                                  at(gate_w, slice(None), k), k == 0, k == KD - 1)
                ins.then_inc(gate_full[n], 1)
                pe.wait_ge(comb_ready[n], 1)
                for t in range(TILES):
                    ins = pe.transpose(ps[0:EXPERTS, 5 + t // 4, (t % 4) * P:(t % 4 + 1) * P], comb[:, t * EXPERTS:(t + 1) * EXPERTS], ident[:, :])
                ins.then_inc(comb_full[n], 1)
                pe.wait_ge(combT_ready[n], 2)
                pe.wait_ge(in_b_ready[n], len(IN_B[n]))
                for j in range(2 * TILES):
                    pe.wait_ge(prod_used, PR_FFN[n] + j - 7)
                    c, t = j // TILES, j % TILES
                    pe.matmul(ps[:, (PR_FFN[n] + j) % 8, 0:WCOL], combT[:, t * P:(t + 1) * P], out_b[:, wcols(c)], start=True, stop=True).then_inc(prod_full, 1)
                pe.wait_ge(prod_used, PR_FFN[n] + SET)
                steps, sizes = HIDDEN[n], FFN_UNITS[n]
                first_y, units, cols, ks, hidden = OUTPUT[n]
                chunks_y = units * TILES
                with pe.Fori(0, EXPERTS // 2) as i:
                    for b in range(2):
                        def weights(u):
                            number = U_FFN[n] + b * len(sizes) + u
                            pe.wait_ge(unit_ready, number + 2 * len(sizes) * i + 1)
                            rows, k, width = sizes[u]
                            return unit_view(number % 2, k, width, rows)

                        last = -1
                        for g, (u, col, width, src, _, c, _) in enumerate(steps):
                            done = 2 * len(steps) * i + b * len(steps)
                            if u != last:
                                if last >= 0:
                                    used()
                                w, last = weights(u), u
                            rows, k_of, _ = sizes[u]
                            if src is not XT and c == 0:
                                pe.wait_ge(h_lo[n], FREE_LO + done + g)
                            pe.wait_ge(h_act[n], done + g + 1)
                            pair = (b * len(steps) + g) % 2
                            for half in range(2):
                                for k in range(k_of):
                                    ins = mm3(pe, ps[0:width, 2 * pair + half, 0:HALF], at(w, slice(None), k, slice(col, col + width)),
                                              at(src, slice(0, rows), k, cols_half(half)), k == 0, k == k_of - 1)
                            ins.then_inc(h_full[n], 1)
                        used()
                        pe.wait_ge(h_lo[n], FREE_LO + 2 * len(steps) * i + (b + 1) * len(steps))
                        for c in range(units):
                            w = weights(first_y + c)
                            for t in range(TILES):
                                y = (b * units + c) * TILES + t
                                pe.wait_ge(y_used[n], chunks_y - Y_BANKS[n] + 2 * chunks_y * i + y + 1)
                                for k in range(ks):
                                    ins = mm3(pe, ps[:, 4 + y % Y_BANKS[n], 0:cols], at(hidden, slice(None), k, slice(t * P, (t + 1) * P)),
                                              at(w, slice(None), k), k == 0, k == ks - 1)
                                ins.then_inc(y_full[n], 1)
                            used()

            experts(0)
            end_phase(pe, "pe", 8)

            transposes(TR_MIX_IN, XM, ROWS_MIX_IN)
            pe.wait_ge(tr_done, TR_MIX_IN + SET)
            for n, start in enumerate((PR_Q, PR_K, PR_V)):
                products(start, U_MIX1 + 2 * n, chunk_of)
            pe.wait_ge(prod_used, PR_V + SET)
            pe.wait_ge(kv_rows, TILES)
            for c in range(2):
                for t in range(TILES):
                    rows = LAST if t == FULL else P
                    ins = pe.matmul(ps[:, c, 0:WCOL], f32(ones_r[0:rows, :]), K[0:rows, t, wcols(c)], start=(t == 0), stop=(t == FULL))
                ins.then_inc(kv_full, 1)
            transposes(TR_MIX_OUT, Q, ROWS_MIX_OUT)
            pe.wait_ge(tr_done, TR_MIX_OUT + SET)
            products(PR_MIX1, U_MIX1 + 6, chunk_of)
            end_phase(pe, "pe", 9)
            transposes(TR_XN1, XN1)
            pe.wait_ge(c_added, RELS + FREE_BUF + TILES)
            pe.wait_ge(tr_done, TR_XN1 + SET)
            for d in range(TILES):
                if d >= 2:
                    pe.wait_ge(c_done, d - 1)
                for t in range(TILES):
                    ins = pe.transpose(ps[:, 2 * (d % 2) + t // FULL, (t % FULL) * P:(t % FULL + 1) * P], csum[:, t, d * P:(d + 1) * P], ident[:, :])
                ins.then_inc(c_full, 1)
            end_phase(pe, "pe", 10)

            def gat(layer):
                heads, units, kd = GAT[layer]
                tiles = heads * TILES
                XL, PT = ((XL1, PT1), (XL2, PT2))[layer]

                def xl_chunk(h, u, t):
                    n = (h * units + u) * TILES + t
                    unit = U_XL[layer] + h * units + u
                    if t == 0:
                        pe.wait_ge(unit_ready, unit + 1)
                    if n >= 2:
                        pe.wait_ge(xl_done[layer], n - 1)
                    w = unit_view(unit % 2, kd, GCOL)
                    for k in range(kd):
                        act_t, m = chunk_of(k)
                        ins = mm3(pe, ps[:, n % 2, 0:GCOL], at(act_t, slice(None), m, slice(t * P, (t + 1) * P)), at(w, slice(None), k), k == 0, k == kd - 1)
                    ins.then_inc(xl_full[layer], 1)
                    if t == FULL:
                        used()

                def source_row(h):
                    pe.wait_ge(diag_ready[layer], (h + 1) * TILES)
                    if h > 0:
                        pe.wait_ge(e_ready[layer], h * TILES)
                    for c in range(2):
                        ins = pe.matmul(ps[:, 2 + c, 0:HALF], f32(ones_r[:, :]), diag[layer][:, cols_half(c)], start=True, stop=True)
                    ins.then_inc(row_full[layer], 1)

                def weights_t(g):
                    pe.wait_ge(p_ready[layer], g + 1)
                    if g > 0:
                        pe.wait_ge(pt_done[layer], g)
                    for t in range(TILES):
                        ins = pe.transpose(ps[:, 4 + t // FULL, (t % FULL) * P:(t % FULL + 1) * P], g_p[g % 2][:, t * P:(t + 1) * P], ident[:, :])
                    ins.then_inc(pt_full[layer], 1)

                def output(g):
                    h = g // TILES
                    pe.wait_ge(pt_done[layer], g + 1)
                    ring = (2, 1)[layer]
                    if g >= ring:
                        pe.wait_ge(o_used[layer], g - ring + 1)
                    cols = (GCOL, WCOL)[layer]
                    for c in range(units * GCOL // cols):
                        for t in range(TILES):
                            ins = mm3(pe, ps[:, 6 + (g % 2 if layer == 0 else c), 0:cols], at(PT[g % len(PT)], slice(None), t),
                                      at(XL[h % len(XL)], slice(None), t, slice(c * cols, (c + 1) * cols)), t == 0, t == FULL)
                    ins.then_inc(o_full[layer], 1)

                for u in range(units):
                    for t in range(TILES):
                        xl_chunk(0, u, t)
                source_row(0)
                for g in range(tiles + 3):
                    h, t = g // TILES, g % TILES
                    if h + 1 < heads:
                        xl_chunk(h + 1, 0, t)
                    if 0 <= g - 2 < tiles:
                        weights_t(g - 2)
                    if 0 <= g - 3 < tiles:
                        output(g - 3)
                    if h + 1 < heads and t == FULL:
                        source_row(h + 1)
                pe.wait_ge(o_used[layer], tiles)
                products(PR_SKIP[layer], U_SKIP[layer], chunk_of, kd, (heads, units)[layer], GCOL)
                if layer == 0:
                    pe.wait_ge(prod_used, PR_SKIP[0] + heads * TILES)
                    transposes(TR_H1, wide, ROWS_H1, GAT1 // P)
                    pe.wait_ge(tr_done, TR_H1 + 3 * TILES)

            gat(0)
            end_phase(pe, "pe", 11)
            gat(1)
            end_phase(pe, "pe", 12)
            experts(1)
            end_phase(pe, "pe", 13)


_INPUTS = ['x', 'src', 'dst', 'edge_type_8', 'L0_gnn_W1', 'L0_gnn_root1', 'L0_gnn_b1', 'L0_gnn_W2', 'L0_gnn_root2', 'L0_gnn_b2',
           'L0_mix_W_qkv', 'L0_mix_b_qkv', 'L0_mix_W_proj', 'L0_mix_b_proj', 'L0_mix_random_features',
           'L0_ffn_Wg', 'L0_ffn_bg', 'L0_ffn_W1', 'L0_ffn_b1', 'L0_ffn_W2', 'L0_ffn_b2', 'L0_ffn_W3', 'L0_ffn_b3',
           'L1_gnn_W1', 'L1_gnn_a_src1', 'L1_gnn_a_dst1', 'L1_gnn_b1', 'L1_gnn_g1', 'L1_gnn_be1', 'L1_gnn_Wr1', 'L1_gnn_br1',
           'L1_gnn_W2', 'L1_gnn_a_src2', 'L1_gnn_a_dst2', 'L1_gnn_b2', 'L1_gnn_g2', 'L1_gnn_be2', 'L1_gnn_Wr2', 'L1_gnn_br2',
           'L1_mix_w_qkv', 'L1_mix_w_proj', 'L1_mix_ln_in_g', 'L1_mix_ln_in_b', 'L1_mix_ln_out_g', 'L1_mix_ln_out_b',
           'L1_ffn_router_w', 'L1_ffn_router_b', 'L1_ffn_w1', 'L1_ffn_b1', 'L1_ffn_w2', 'L1_ffn_b2']


def kernel(**inputs):
    import numpy as np
    import concourse.bacc as bacc
    from concourse.bass_utils import run_bass_kernel_spmd

    nc = bacc.Bacc("TRN2", target_bir_lowering=False, num_devices=1)
    arrays, views = {}, {}
    for name in _INPUTS:
        arrays[name + "_in"] = np.ascontiguousarray(inputs[name])
        views[name] = nc.dram_tensor(name + "_in", arrays[name + "_in"].shape, mybir.dt.from_np(arrays[name + "_in"].dtype), kind="ExternalInput").ap()
    result = nc.dram_tensor("rows_out", (NODES, DIM), F32, kind="ExternalOutput").ap()
    build(nc, views, result)
    got = run_bass_kernel_spmd(nc, [arrays], core_ids=[0])
    return got.results[0]["rows_out"]
```

```python
from contextlib import ExitStack

import concourse.bass as bass
from concourse import mybir

F32 = mybir.dt.float32
F32R = mybir.dt.float32r
I32 = mybir.dt.int32
I16 = mybir.dt.int16
U16 = mybir.dt.uint16
U32 = mybir.dt.uint32
BF16 = mybir.dt.bfloat16
ALU = mybir.AluOpType
ACT = mybir.ActivationFunctionType
AX = mybir.AxisListType
ds = bass.ds

P = 128
NODES = 625
TILES = 5
FULL = TILES - 1
LAST = NODES - FULL * P
COLS = TILES * P
HALF = COLS // 2
EDGES = 10000
EDGE_ROWS = 125
EDGE_COLS = EDGES // EDGE_ROWS
RELS = 8
DIM = 768
KD = DIM // P
WCOL = 384
UNIT = KD * WCOL
BANK = 512
EPS = 1e-5

GROUPS = RELS * TILES
SLOT = 2 * P
SLOTS = (EDGES + GROUPS * (SLOT - 1)) // SLOT
SUBS = 2 * SLOTS

HEADS0, HEAD0 = 12, 64
PAIRS = HEADS0 // 2
FEATS = 256
MIX0_SCALE = (HEAD0 ** -0.5) ** 2 / FEATS

EXPERTS = 8
HID0 = 192
HC0, HP0 = 2, HID0 // 2
HID0B = 2 * HID0
HB0 = HID0B // P
HID1 = 1152
HC1 = HID1 // P
YCOL1 = 256
BELOW = -3e38
SLOT_ROWS = 2 * P
CHOSEN = 2
MORE = NODES * CHOSEN // (SLOT_ROWS + 1)
XSLOTS = EXPERTS + MORE
CHOICES = TILES * CHOSEN
RING = 4
GHEADS, GCOL = 4, 256
GAT1 = GHEADS * GCOL
NORM_EPS = 1e-12
SUM_EPS = 1e-16
SLOPE = 0.2
NO_EDGE = -1e30


class Unit:

    def __init__(self, first, i=0, per=0):
        self.n = first + per * i
        self.slot = first % 2
        twice = min(first + 2, 2 * PAIRS) // 2 if self.slot == 0 else 0
        self.loads = 16 * twice + 16 * (first // 2 + 1) + 8 * per * i


class Order:

    def __init__(self, eng, sem):
        self.eng, self.sem, self.before, self.n = eng, sem, 0, 0

    def step(self, ins):
        ins.then_inc(self.sem, 1)
        self.n += 1

    def wait(self):
        self.eng.wait_ge(self.sem, self.before + self.n)

    def enter(self, i, per):
        self.start, self.per = self.before + self.n, per
        self.before, self.n = self.start + per * i, 0

    def leave(self, times):
        assert self.n == self.per, (self.n, self.per)
        self.before, self.n = self.start + self.per * times, 0


def build(nc, a, out):
    with ExitStack() as ctx:
        def dram(name, shape, dt):
            return nc.dram_tensor(name, shape, dt, kind="Internal").ap()

        def sem(name):
            return ctx.enter_context(nc.semaphore(name))

        def sems(name, n):
            return [sem(f"{name}{k}") for k in range(n)]

        def allocator(stack):
            def one(name, shape, dt):
                return stack.enter_context(nc.sbuf_tensor(name, shape, dt))

            def pair(name, shape):
                return one(name + "_hi", shape, F32R), one(name + "_lo", shape, F32R)

            return one, pair

        sorted_dram = dram("edges_sorted", (P * SUBS, 1), I32)
        slot_rows_dram = dram("slot_rows", (XSLOTS * SLOT_ROWS, DIM), F32)
        slot_out_dram = [dram(f"slot_out{n}", (XSLOTS * SLOT_ROWS, DIM), F32) for n in range(2)]
        adj_dram = dram("adjacency", (RELS, P, TILES * COLS), U16)

        keep, keep2 = allocator(ctx)
        X = keep("x_rows", [P, TILES, DIM], F32)
        XT = keep2("xt", [P, KD, COLS])
        raw = [keep(f"weight_raw{s}", [P, UNIT], F32) for s in range(2)]
        W = [keep2(f"weight{s}", [P, UNIT]) for s in range(2)]
        ident = keep("ident", [P, P], F32)
        ones_r = keep("ones_r", [P, P], F32R)
        zero_col = keep("zero_col", [P, 1], F32)
        eps_col = keep("eps_col", [P, 1], F32)
        stats = keep("stats", [P, TILES, 2, 6], F32)
        mv = keep("mean_var", [P, TILES, 2], F32)
        std = keep("std", [P, TILES], F32)
        rstd = keep("rstd", [P, TILES], F32)
        bias_rows = keep("bias_rows", [P, 2, DIM], F32)
        bias_row = [bias_rows[:, s, :] for s in range(2)]
        ps = ctx.enter_context(nc.psum_tensor("banks", [P, 8, BANK], F32))

        early = ExitStack()
        er, er2 = allocator(early)
        XN = er("xn_rows", [P, TILES, DIM], F32)
        rf2 = er("rf2", [P, 2, P], F32)
        rfT = er2("rfT", [P, FEATS])
        qk_bias = er("qk_bias", [P, 2 * KD], F32)
        sorted_sb = er("sorted_sb", [P, SUBS], I32)
        part_i = er("part_i", [P, SUBS], I32)
        srcl_f = er("srcl_f", [P, SUBS], F32)
        dst_f = er("dst_f", [P, SUBS], F32)
        dst_iota = er("dst_iota", [P, COLS], I16)
        slot_group = er("slot_group", [1, SLOTS], I32)
        zero_row = er("zero_row", [P, DIM], F32)
        pos_i = er("pos_i", [EDGE_ROWS, EDGE_COLS], I32)
        code_i = er("code_i", [EDGE_ROWS, EDGE_COLS], I32)
        with ExitStack() as here:
            srt, _ = allocator(here)
            src_i = srt("src_i", [EDGE_ROWS, EDGE_COLS], I32)
            dst_i = srt("dst_i", [EDGE_ROWS, EDGE_COLS], I32)
            typ_i = srt("typ_i", [EDGE_ROWS, EDGE_COLS], I32)
            tile_i = srt("tile_i", [EDGE_ROWS, EDGE_COLS], I32)
            low_i = srt("low_i", [EDGE_ROWS, EDGE_COLS], I32)
            sub_i = srt("sub_i", [EDGE_ROWS, EDGE_COLS], I32)
            spot_i = srt("spot_i", [EDGE_ROWS, EDGE_COLS], I32)
            group_f = srt("group_f", [EDGE_ROWS, EDGE_COLS], F32)
            pos_f = srt("pos_f", [EDGE_ROWS, EDGE_COLS], F32)
            iota_g = srt("iota_g", [EDGE_ROWS, GROUPS], F32)
            iota_s = srt("iota_s", [1, SLOTS], F32)
            onehot_g = srt("onehot_g", [EDGE_ROWS, GROUPS, EDGE_COLS], F32)
            restart = srt("restart", [EDGE_ROWS, GROUPS, EDGE_COLS], F32)
            rank = srt("rank", [EDGE_ROWS, GROUPS, EDGE_COLS], F32)
            in_row = srt("in_row", [EDGE_ROWS, GROUPS], F32)
            before = srt("before", [P, P], F32)
            ones_f = srt("ones_f", [P, P], F32)
            ones_g = srt("ones_g", [EDGE_ROWS, GROUPS], F32)
            need_i = srt("need_i", [EDGE_ROWS, GROUPS], I32)
            need_s = srt("need_s", [EDGE_ROWS, GROUPS], I32)
            need_f = srt("need_f", [EDGE_ROWS, GROUPS], F32)
            slot_end = srt("slot_end", [EDGE_ROWS, GROUPS], F32)
            slot_base = srt("slot_base", [EDGE_ROWS, GROUPS], F32)
            offset_g = srt("offset_g", [EDGE_ROWS, GROUPS], F32)
            past = srt("past", [1, SLOTS, GROUPS], F32)
            group_of = srt("group_of", [1, SLOTS], F32)
            fill_i = srt("fill_i", [P, SUBS], I32)
        with ExitStack() as here:
            mx, mx2 = allocator(here)
            attnT = mx2("attnT", [P, KD, COLS])
            qT = mx2("qT", [P, COLS])
            kT = mx2("kT", [P, COLS])
            v = mx2("v", [P, TILES, P])
            v_f = mx("v_f", [P, TILES, P], F32)
            phi_k = mx2("phi_k", [P, TILES, FEATS])
            phi_qT = mx2("phi_qT", [P, 2, COLS])
            kv = mx2("kv", [P, 2, 2, P])
        with ExitStack() as here:
            aj, _ = allocator(here)
            adj = aj("adj", [P, GROUPS, COLS], U16)
            src_hot = [aj(f"src_hot{s}", [P, 2, P], BF16) for s in range(2)]
            dst_hot = [aj(f"dst_hot{s}", [P, 2, COLS], BF16) for s in range(2)]
        early.close()
        with ExitStack() as here:
            rg, rg2 = allocator(here)
            A_r = [rg(f"a_rel{s}", [P, TILES, COLS], F32R) for s in range(2)]
            xn = rg2("xn", [P, TILES, DIM])
            A_u = [rg(f"a_stage{s}", [P, TILES, COLS], U16) for s in range(2)]
            cnt_m = rg("cnt_m", [P, 2, HALF], F32)
            inv = [rg(f"inv{s}", [P, 2, HALF], F32) for s in range(2)]
            ACC = rg("acc_rows", [P, TILES, DIM], F32)
            agg_f = [rg(f"agg_f{s}", [P, HALF], F32) for s in range(3)]

        late = ExitStack()
        lt, lt2 = allocator(late)
        wide = lt("wide_rows", [P, TILES, GAT1], F32)
        XN1 = wide[:, :, 0:DIM]
        with ExitStack() as here:
            ma, _ = allocator(here)
            XM = ma("xm_rows", [P, TILES, DIM], F32)
            Q, K, V = [ma(n, [P, TILES, DIM], F32) for n in ("q_rows", "k_rows", "v_rows")]
            in_gain, in_shift, out_gain, out_shift = [ma(n, [P, DIM], F32) for n in ("in_gain", "in_shift", "out_gain", "out_shift")]
            square = ma("square", [P, DIM], F32)
            norm = ma("norm", [P, 2, TILES], F32)
            norm_m = ma("norm_m", [P, 2, TILES], F32)
            inv_norm = ma("inv_norm", [P, 2, TILES], F32)
        count = lt("count", [P, TILES, COLS], U16)
        absent = lt("absent", [P, TILES, COLS], BF16)
        with ExitStack() as here:
            cs, _ = allocator(here)
            C_u = [cs(f"c_stage{s}", [P, TILES, COLS], U16) for s in range(2)]
            csum = cs("csum", [P, TILES, COLS], F32)
        g_e = [lt(f"att_logit{s}", [P, COLS], F32) for s in range(2)]
        g_p = [lt(f"att_p{s}", [P, COLS], F32) for s in range(2)]
        g_max = lt("att_max", [P, 2], F32)
        g_neg = lt("att_neg", [P, 2], F32)
        g_sum = lt("att_sum", [P, 4 * TILES], F32)
        g_sum_e = lt("att_sum_e", [P, 4 * TILES], F32)
        g_inv = lt("att_inv", [P, 4 * TILES], F32)
        junk = [lt(f"junk{s}", [P, GCOL], F32) for s in range(2)]
        part_of = [lt(f"alpha_part{k}", [P, TILES, 3], F32) for k in range(2)]
        alpha = [[lt(f"alpha{k}_{s}", [P, TILES], F32) for s in range(2)] for k in range(2)]
        with ExitStack() as here:
            g1, g12 = allocator(here)
            PT1 = [g12(f"attT{s}", [P, TILES, P]) for s in range(2)]
            XL1 = [g12(f"xl_head{s}", [P, TILES, GCOL]) for s in range(3)]
            a_row1 = [g1(f"a_row1_{k}", [P, GAT1], F32) for k in range(2)]
            row1 = {n: g1(n + "1_row", [P, GAT1], F32) for n in ("b", "g")}
        with ExitStack() as here:
            g2, g22 = allocator(here)
            XT_more = g22("xt_more", [P, GAT1 // P - KD, COLS])
            PT2 = [g22("att2T", [P, TILES, P])]
            XL2 = [g22("xl2", [P, TILES, DIM])]
            a_row2 = [g2(f"a_row2_{k}", [P, DIM], F32) for k in range(2)]
            diag = [bias_row[0][:, 0:COLS], g2("diag", [P, COLS], F32)]
        late.close()
        with ExitStack() as here:
            fe, fe2 = allocator(here)
            raw_more = [fe(f"weight_raw{s}", [P, UNIT], F32) for s in range(2, RING)]
            W_more = [fe2(f"weight{s}", [P, UNIT]) for s in range(2, RING)]
            gate_w = fe2("gate_w", [P, KD, EXPERTS])
            gate_b = fe("gate_b", [EXPERTS, 1], F32)
            iota_e = fe("iota_e", [P, EXPERTS], F32)
            scores = fe("scores", [P, TILES, EXPERTS], F32)
            choice = fe("choice", [P, TILES, EXPERTS], F32)
            others = fe("others", [P, TILES, EXPERTS], F32)
            top = [fe(f"top{k}", [P, TILES, 8], F32) for k in range(CHOSEN)]
            top_at = [fe(f"top_at{k}", [P, TILES, 8], U32) for k in range(CHOSEN)]
            chosen = fe("chosen", [P, TILES, CHOSEN], F32)
            is_chosen = fe("is_chosen", [P, TILES, CHOSEN, EXPERTS], F32)
            diff = fe("diff", [P, TILES, EXPERTS], F32)
            expo = fe("expo", [P, TILES, EXPERTS], F32)
            total = fe("total", [P, TILES], F32)
            share = fe("share", [P, TILES], F32)
            comb = fe("comb", [P, TILES, EXPERTS], F32)
            gate_of = fe("gate_of", [P, TILES, CHOSEN, EXPERTS], F32)
            gate = fe("gate", [P, TILES, CHOSEN], F32)
            before_e = fe("before_e", [P, P], F32)
            restart_e = fe("restart_e", [P, EXPERTS, CHOICES], F32)
            ones_e = fe("ones_e", [P, EXPERTS], F32)
            in_tile = fe("in_tile", [P, EXPERTS, CHOICES], F32)
            through = fe("through", [P, EXPERTS, CHOICES], F32)
            rank_of = fe("rank_of", [P, CHOICES, EXPERTS], F32)
            rank_e = fe("rank_e", [P, CHOICES], F32)
            need_e = fe("need_e", [P, EXPERTS], I32)
            need_es = fe("need_es", [P, EXPERTS], I32)
            more = fe("more", [P, EXPERTS], F32)
            more_end = fe("more_end", [P, EXPERTS], F32)
            more_at = fe("more_at", [P, EXPERTS], F32)
            more_of = fe("more_of", [P, CHOICES, EXPERTS], F32)
            spill = fe("spill", [P, CHOICES], F32)
            is_more = fe("is_more", [P, CHOICES], F32)
            first_at = fe("first_at", [P, CHOICES], F32)
            place_f = fe("place_f", [P, CHOICES], F32)
            place = fe("place", [P, CHOICES], I32)
            past_e = fe("past_e", [1, MORE, EXPERTS], F32)
            slot_expert_f = fe("slot_expert_f", [1, XSLOTS], F32)
            slot_expert = fe("slot_expert", [1, XSLOTS], I32)
            iota_m = fe("iota_m", [1, MORE], F32)
            in_b = [fe(f"in_b{m}", [P, EXPERTS * HC1], F32) for m in range(2)]
            slot_in = [fe(f"slot_in{s}", [P, 2, DIM], F32) for s in range(2)]
            h_f = [fe(f"h_f{s}", [P, SLOT_ROWS], F32) for s in range(3)]
            with ExitStack() as first:
                start = allocator(first)[0]
                scoresT = start("scoresT", [EXPERTS, COLS], F32)
                combT = scoresT
                gate_raw = start("gate_raw", [P, KD, EXPERTS], F32)
                in_b_rows = [start(f"in_b_rows{m}", [P, P], F32) for m in range(2)]
            y_rows = [bias_rows, fe("y_rows", [P, 2, DIM], F32)]
            with ExitStack() as first:
                XE = allocator(first)[0]("xe_rows", [P, TILES, DIM], F32)
                out_b = allocator(first)[0]("out_b", [EXPERTS, DIM], F32)
            hT = fe2("hT", [P, HC1, SLOT_ROWS])

        raw_ready = sems("raw_ready", 2)
        hi_ready = sem("hi_ready")
        unit_ready = sem("unit_ready")
        unit_used = sem("unit_used")
        x_in, edges_in, rf_in = sem("x_in"), sem("edges_in"), sem("rf_in")
        bias_in = sem("bias_in")
        pad_zero, consts, masks = sem("pad_zero"), sem("consts"), sem("masks")
        vec_order = sem("vec_order")
        ln_var = sem("ln_var")
        ln_std = sem("ln_std")
        rows_ready = sem("rows_ready")
        tr_full = sem("tr_full")
        tr_hi = sem("tr_hi")
        tr_done = sem("tr_done")
        prod_full = sem("prod_full")
        prod_used = sem("prod_used")
        sort_row = sem("sort_row")
        sort_sum = sem("sort_sum")
        pos_ready = sem("pos_ready")
        filled = sem("filled")
        scattered = sem("scattered")
        sorted_in = sem("sorted_in")
        rf_full, rf_hi = sem("rf_full"), sem("rf_hi")
        A_full, A_hi, A_done = sem("mixA_full"), sem("mixA_hi"), sem("mixA_done")
        B_full, B_val, B_hi, B_done = sem("mixB_full"), sem("mixB_val"), sem("mixB_hi"), sem("mixB_done")
        C_full, C_hi, C_done = sem("mixC_full"), sem("mixC_hi"), sem("mixC_done")
        hot = sem("hot")
        slot_full = sem("slot_full")
        slot_done = sem("slot_done")
        adj_out = sem("adj_out")
        rows_hi = sem("rows_hi")
        rows_lo = sem("rows_lo")
        a_in = [sems(f"a_in{layer}_", 2) for layer in range(2)]
        a_ready = sems("a_ready", 2)
        cnt_full, cnt_used = sems("cnt_full", 2), sems("cnt_used", 2)
        agg_full, agg_val, agg_hi, agg_done = sems("agg_full", 2), sems("agg_val", 2), sems("agg_hi", 2), sems("agg_done", 2)
        tra_full, tra_used = sems("tra_full", 2), sems("tra_used", 2)
        ends = {e: sem(f"{e}_end") for e in ("pe", "act", "vec")}
        gate_in = sem("gate_in")
        gate_split = sem("gate_split")
        gate_full = sem("gate_full")
        scoresT_ready = sem("scoresT_ready")
        gate_arg = sem("gate_arg")
        gate_exp = sem("gate_exp")
        comb_ready = sem("comb_ready")
        comb_full = sem("comb_full")
        combT_ready = sem("combT_ready")
        in_b_full = sem("in_b_full")
        in_b_ready = sem("in_b_ready")
        cleared = sem("cleared")
        chosen_ready = sem("chosen_ready")
        rank_full = sem("rank_full")
        placed = sem("placed")
        sent = sem("sent")
        slot_ready = [sems(f"slot_ready{n}_", 2) for n in range(2)]
        t_full = sems("t_full", 2)
        t_hi = sems("t_hi", 2)
        t_lo = sems("t_lo", 2)
        eraw_ready = [sems(f"eraw_ready{n}_", RING) for n in range(2)]
        e_hi = sems("e_hi", 2)
        e_lo = sems("e_lo", 2)
        e_used = sems("e_used", 2)
        h_full = sems("h_full", 2)
        h_act = sems("h_act", 2)
        h_lo = sems("h_lo", 2)
        y_full = sems("y_full", 2)
        y_used = sems("y_used", 2)
        y_out = [sems(f"y_out{n}_", 2) for n in range(2)]
        back = sems("back", 2)
        mix_in, kv_rows, kv_full, norm_done = sem("mix_in"), sem("kv_rows"), sem("kv_full"), sem("norm_done")
        c_in = sems("c_in", 2)
        c_added = sem("c_added")
        c_full, c_done = sem("c_full"), sem("c_done")
        gat_in = sems("gat_in", 2)
        late_in = sems("late_in", 2)
        xl_full = sem("xl_full")
        xl_hi = sem("xl_hi")
        xl_done = sem("xl_done")
        diag_ready = sem("diag_ready")
        row_full = sem("row_full")
        e_ready = sem("e_ready")
        e_exp = sem("e_exp")
        p_ready = sem("p_ready")
        pt_full = sem("pt_full")
        pt_hi = sem("pt_hi")
        pt_done = sem("pt_done")
        o_full = sem("o_full")
        o_used = sem("o_used")
        stored = sem("stored")

        U_MIX = 0
        U_PROJ = U_MIX + 2 * PAIRS
        U_ROOT1 = U_PROJ + 2
        U_REL = [U_ROOT1 + 2, U_ROOT1 + 2 + 2 * RELS + 2]
        U_ROOT2 = U_REL[1] - 2
        U_FFN0 = U_REL[1] + 2 * RELS
        U_MIX1 = U_FFN0
        U_XL = [U_MIX1 + 8, U_MIX1 + 8 + 2 * GHEADS]
        U_SKIP = [U_XL[0] + GHEADS, U_XL[1] + DIM // GCOL]

        FFN_UNITS = [[(P, KD, HID0), (HP0, HC0, HID0B), (P, HB0, WCOL), (P, HB0, WCOL)],
                     [(P, KD, WCOL)] * 3 + [(P, HC1, YCOL1)] * 3]
        HIDDEN = [[(0, c * HP0, HP0, None, c, 0) for c in range(HC0)] + [(1, c * P, P, 0, HC0 + c, 1) for c in range(HB0)],
                  [(c // 3, c % 3 * P, P, None, c, 0) for c in range(HC1)]]
        OUTPUT = [(2, 2, WCOL, HB0, HC0), (3, 3, YCOL1, HC1, 0)]
        ROWS_AFTER = [0, 2]
        IN_B = [[(HC0, HP0), (HB0, P)], [(HC1, P)]]
        Q_T = KD // 2
        T_BANK = 5
        H_BANKS = (0, 1, 4)
        FREE_H = FREE_LO = len(H_BANKS)
        FREE_Y, FREE_T, FREE_IN = 2, Q_T, 2 * Q_T
        AHEAD = RING - 1
        SPLITS = [XSLOTS * len(u) for u in FFN_UNITS]
        RAW4, W4 = raw + raw_more, W + W_more
        out_rows = [x[:, :, :].rearrange("p k c -> p (k c)").bitcast(F32).rearrange("p (t d) -> p t d", t=TILES) for x in XT]
        LN_FFN, LN_IN1, LN_MIX_IN, LN_MIX_OUT, LN_GAT = [1, 7], 2, 3, 4, [5, 6]
        ROWS_0, ROWS_H, ROWS_FFN, ROWS_MIX_IN, ROWS_MIX_OUT, ROWS_H1 = 0, TILES, [2 * TILES, 6 * TILES], 3 * TILES, 4 * TILES, 5 * TILES
        SET = 2 * TILES
        TR_0, TR_H, TR_MIX_IN, TR_MIX_OUT, TR_XN1, TR_H1 = 0, SET, 3 * SET, 4 * SET, 5 * SET, 6 * SET
        TR_FFN = [2 * SET, TR_H1 + 3 * TILES]
        PR_PROJ, PR_ROOT1, PR_ROOT2, PR_Q, PR_K, PR_V, PR_MIX1 = 0, SET, 2 * SET, 4 * SET, 5 * SET, 6 * SET, 7 * SET
        PR_SKIP = [8 * SET, 8 * SET + GHEADS * TILES]
        PR_FFN = [3 * SET, PR_SKIP[1] + DIM // GCOL * TILES]
        GAT = [(GHEADS, 1, KD), (1, DIM // GCOL, GAT1 // P)]

        FREE_A, FREE_B, FREE_C = 4, 2, 2
        FREE_AGG, FREE_TRA, FREE_CNT = 4, 2 * TILES, 2
        AGGS = 2 * KD
        FREE_BUF = 2
        FREE_DONE = 3
        FREE_SUM = 1
        FREE_HOT = 2
        LAST_PHASE = 13

        def mm3(pe, dst, s, m, start, stop, after=None):
            ins = pe.matmul(dst, s[0], m[0], start=start, stop=False)
            if after is not None:
                ins.then_inc(after, 1)
            pe.matmul(dst, s[0], m[1], start=False, stop=False)
            return pe.matmul(dst, s[1], m[0], start=False, stop=stop)

        def at(pair, *idx):
            return pair[0][idx], pair[1][idx]

        def unit_view(slot, k, n, rows=P):
            return [w[0:rows, 0:k * n].rearrange("p (k n) -> p k n", k=k) for w in W4[slot]]

        def chunks(w):
            return w.rearrange("(k p) o -> p k o", p=P)

        def f32(ap):
            return ap.bitcast(F32)

        def end_phase(eng, me, n):
            eng.drain().then_inc(ends[me], 1)
            for e in ends:
                if e != me:
                    eng.wait_ge(ends[e], n)

        def after_phase(eng, n):
            for e in ends:
                eng.wait_ge(ends[e], n)

        def groups_of(kd):
            return [range(c, min(c + 3, kd)) for c in range(0, kd, 3)]

        def chunk_of(g):
            return (XT, g) if g < KD else (XT_more, g - KD)

        def hidden_at(g, width):
            s = g % len(H_BANKS)
            return ps[0:width, H_BANKS[s], 0:SLOT_ROWS], h_f[s][0:width, :]

        def places_left(n, g):
            return 1 if g + len(HIDDEN[n]) % len(H_BANKS) >= len(H_BANKS) or len(HIDDEN[n]) % len(H_BANKS) == 0 else 2

        def slot_at(base, i, b):
            return base[ds((2 * i + b) * SLOT_ROWS, SLOT_ROWS), :].rearrange("(h p) d -> p h d", p=P)

        def slot_pairs(eng, body):
            with eng.Fori(0, XSLOTS // 2 - 1) as i:
                for b in range(2):
                    body(i, b, False)
            for b in range(2):
                body(XSLOTS // 2 - 1, b, b == 1)

        def cols_half(n):
            return slice((n % 2) * HALF, (n % 2 + 1) * HALF)

        def halves(ap):
            return ap.rearrange("p (h n) -> p h n", h=2)

        def wcols(c):
            return slice(c * WCOL, (c + 1) * WCOL)

        block = ctx.enter_context(nc.Block())

        @block.sync
        def _(sp):
            def load(u, *parts):
                if not (isinstance(u.n, int) and u.n < 2):
                    sp.wait_ge(unit_ready, u.n - 1)
                at_word = 0
                for src in parts:
                    rows, k, n = src.shape
                    dst = raw[u.slot][0:rows, at_word:at_word + k * n].rearrange("p (k n) -> p k n", k=k)
                    sp.dma_start(dst, src).then_inc(raw_ready[u.slot], 16)
                    at_word += k * n

            def store():
                sp.dma_start(out[0:FULL * P, :].rearrange("(t p) d -> p t d", p=P), X[:, 0:FULL, :]).then_inc(stored, 16)
                sp.dma_start(out[FULL * P:NODES, :], X[0:LAST, FULL, :]).then_inc(stored, 16)
                sp.wait_ge(stored, 32)

            x = a["x"]
            sp.dma_start(X[:, 0:FULL, :], x[0:FULL * P, :].rearrange("(t p) d -> p t d", p=P)).then_inc(x_in, 16)
            sp.wait_ge(pad_zero, 1)
            sp.dma_start(X[0:LAST, FULL, :], x[FULL * P:NODES, :]).then_inc(x_in, 16)
            for t, n in ((src_i, "src"), (dst_i, "dst"), (typ_i, "edge_type_8")):
                sp.dma_start(t[:, :], a[n].rearrange("(p c) -> p c", p=EDGE_ROWS)).then_inc(edges_in, 16)
            qkv = a["L0_mix_W_qkv"].rearrange("(k p) (s o) -> p k s o", p=P, s=3)
            load(Unit(U_MIX), qkv[:, :, 0, 0:P], qkv[:, :, 1, 0:P])
            load(Unit(U_MIX + 1), qkv[:, :, 2, 0:P])
            with sp.Fori(1, PAIRS) as j:
                load(Unit(U_MIX, j, 2), qkv[:, :, 0, ds(j * P, P)], qkv[:, :, 1, ds(j * P, P)])
                load(Unit(U_MIX + 1, j, 2), qkv[:, :, 2, ds(j * P, P)])
            for c in range(2):
                load(Unit(U_PROJ + c), chunks(a["L0_mix_W_proj"])[:, :, wcols(c)])
            sp.wait_ge(scattered, 16 * EDGE_COLS)
            sp.dma_start(sorted_sb[:, :], sorted_dram.rearrange("(p c) o -> p (c o)", p=P)).then_inc(sorted_in, 16)
            sp.wait_ge(slot_done, FREE_SUM + SLOTS)
            sp.dma_start(adj_dram.rearrange("r p c -> p r c"), adj[:, :, :].rearrange("p (r t) c -> p r (t c)", r=RELS)).then_inc(adj_out, 16)
            sp.wait_ge(adj_out, 16)
            for c in range(2):
                load(Unit(U_ROOT1 + c), chunks(a["L0_gnn_root1"])[:, :, wcols(c)])
            after_phase(sp, 4)
            for layer in range(2):
                w = a[("L0_gnn_W1", "L0_gnn_W2")[layer]].rearrange("r (k p) o -> r p k o", p=P)
                if layer == 1:
                    for c in range(2):
                        load(Unit(U_ROOT2 + c), chunks(a["L0_gnn_root2"])[:, :, wcols(c)])
                    after_phase(sp, 6)
                with sp.Fori(0, RELS // 2) as i:
                    for b in range(2):
                        sp.wait_ge(a_ready[layer], 2 * i + b + 1)
                        sp.dma_start(A_u[b][:, :, :].rearrange("p t c -> p (t c)"),
                                     adj_dram[ds(2 * i + b, 1), :, :].rearrange("r p c -> (r p) c")).then_inc(a_in[layer][b], 16)
                        for c in range(2):
                            load(Unit(U_REL[layer] + 2 * b + c, i, 4),
                                 w[ds(2 * i + b, 1), :, :, wcols(c)].rearrange("r p k o -> (r p) k o"))
            def expert_loads(n, units):
                def slot(i, b, expert):
                    for c, w in enumerate(units):
                        u = (2 * i + b) * len(units) + c
                        s = (b * len(units) + c) % RING
                        rows, k, cols = FFN_UNITS[n][c]
                        sp.wait_ge(e_lo[n], u + 1)
                        sp.dma_start(RAW4[s][0:rows, 0:k * cols].rearrange("p (k n) -> p k n", k=k),
                                     w[ds(expert, 1)].rearrange("e p k o -> (e p) k o")).then_inc(eraw_ready[n][s], 16)

                with sp.Fori(0, EXPERTS // 2) as i:
                    for b in range(2):
                        slot(i, b, 2 * i + b)
                sp.wait_ge(placed, 2 * (n + 1))
                with sp.Fori(EXPERTS // 2, XSLOTS // 2) as i:
                    for b in range(2):
                        slot(i, b, sp.value_load(slot_expert[0:1, ds(2 * i + b, 1)], min_val=0, max_val=EXPERTS - 1))

            w1 = a["L0_ffn_W1"].rearrange("e (k p) o -> e p k o", p=P)
            w2 = a["L0_ffn_W2"].rearrange("e (k p) o -> e p k o", p=HP0)
            w3 = a["L0_ffn_W3"].rearrange("e (k p) o -> e p k o", p=P)
            expert_loads(0, [w1, w2] + [w3[:, :, :, wcols(c)] for c in range(2)])
            sp.wait_ge(e_lo[0], RING + SPLITS[0])
            with sp.Fori(0, 3) as i:
                for c in range(2):
                    load(Unit(U_MIX1 + c, i, 2), chunks(a["L1_mix_w_qkv"])[:, :, ds((2 * i + c) * WCOL, WCOL)])
            for c in range(2):
                load(Unit(U_MIX1 + 6 + c), chunks(a["L1_mix_w_proj"])[:, :, wcols(c)])
            after_phase(sp, 9)
            with sp.Fori(0, RELS // 2) as i:
                for b in range(2):
                    sp.wait_ge(c_added, 2 * i + b + 1)
                    sp.dma_start(C_u[b][:, :, :].rearrange("p t c -> p (t c)"),
                                 adj_dram[ds(2 * i + b, 1), :, :].rearrange("r p c -> (r p) c")).then_inc(c_in[b], 16)
            for layer in range(2):
                units = DIM // GCOL if layer else GHEADS
                for first, name in ((U_XL, ("L1_gnn_W1", "L1_gnn_W2")), (U_SKIP, ("L1_gnn_Wr1", "L1_gnn_Wr2"))):
                    for c in range(units):
                        load(Unit(first[layer] + c), chunks(a[name[layer]])[:, :, c * GCOL:(c + 1) * GCOL])
            w1 = a["L1_ffn_w1"].rearrange("e (k p) o -> e p k o", p=P)
            w2 = a["L1_ffn_w2"].rearrange("e (k p) o -> e p k o", p=P)
            expert_loads(1, [w1[:, :, :, wcols(c)] for c in range(3)] + [w2[:, :, :, c * YCOL1:(c + 1) * YCOL1] for c in range(3)])
            after_phase(sp, LAST_PHASE)
            store()

        @block.gpsimd
        def _(pool):
            def split(u, n, rows=P):
                s = u.slot
                pool.wait_ge(raw_ready[s], u.loads)
                if not (isinstance(u.n, int) and u.n < 2):
                    pool.wait_ge(unit_used, u.n - 1)
                hi, lo = at(W[s], slice(0, rows), slice(0, n))
                pool.tensor_tensor(hi, raw[s][0:rows, 0:n], zero_col[0:rows, :].broadcast_to([rows, n]), ALU.add).then_inc(hi_ready, 1)
                pool.wait_ge(hi_ready, u.n + 1)
                pool.tensor_tensor(lo, raw[s][0:rows, 0:n], f32(hi), ALU.subtract).then_inc(unit_ready, 1)

            def split_rest(first, times, per, n):
                with pool.Fori(0, times) as i:
                    for c in range(per):
                        split(Unit(first + c, i, per), n)

            pool.memset(X[:, FULL, :], 0.0).then_inc(pad_zero, 1)
            pool.memset(ident[:, :], 0.0).then_inc(consts, 1)
            pool.memset(before[:, :], 0.0).then_inc(consts, 1)
            pool.memset(fill_i[:, :], -1).then_inc(consts, 1)
            pool.memset(eps_col[:, :], EPS).then_inc(consts, 1)
            pool.memset(ones_f[:, :], 1.0).then_inc(consts, 1)
            pool.memset(f32(ones_r[:, :]), 1.0).then_inc(consts, 1)
            pool.memset(ones_g[:, :], 1.0).then_inc(consts, 1)
            pool.memset(restart[:, :, 1:EDGE_COLS], 1.0).then_inc(consts, 1)
            pool.memset(restart[:, :, 0:1], 0.0).then_inc(consts, 1)
            pool.iota(iota_g[:, :], [[1, GROUPS]], base=0, channel_multiplier=0, allow_small_or_imprecise_dtypes=True).then_inc(consts, 1)
            pool.iota(iota_s[:, :], [[1, SLOTS]], base=0, channel_multiplier=0, allow_small_or_imprecise_dtypes=True).then_inc(consts, 1)
            pool.iota(dst_iota[:, :], [[1, COLS]], base=0, channel_multiplier=0, allow_small_or_imprecise_dtypes=True).then_inc(consts, 1)
            pool.memset(zero_col[:, :], 0.0).then_inc(consts, 1)
            pool.memset(zero_row[:, :], 0.0).then_inc(consts, 1)
            pool.wait_ge(consts, 14)
            pool.affine_select(out=ident[:, :], in_=ident[:, :], compare_op=ALU.not_equal, fill=1.0, base=0,
                               pattern=[[-1, P]], channel_multiplier=1).then_inc(masks, 1)
            pool.affine_select(out=before[:, :], in_=before[:, :], compare_op=ALU.is_ge, fill=1.0, base=0,
                               pattern=[[-1, P]], channel_multiplier=1).then_inc(masks, 1)
            pool.wait_ge(filled, 16)
            pool.wait_ge(pos_ready, 1)
            begun = 0
            for j in range(PAIRS):
                for c in range(2):
                    split(Unit(U_MIX + 2 * j + c), KD * P * (2 - c))
                    while begun < min(EDGE_COLS, (2 * j + c + 1) * 8):
                        pool.indirect_dma_start(out=sorted_dram, out_offset=bass.IndirectOffsetOnAxis(ap=pos_i[:, begun:begun + 1], axis=0),
                                                in_=code_i[:, begun:begun + 1], in_offset=None).then_inc(scattered, 16)
                        begun += 1
            split_rest(U_PROJ, 1, 2, UNIT)
            split_rest(U_ROOT1, 1, 2, UNIT)
            split_rest(U_REL[0], RELS, 2, UNIT)
            split_rest(U_ROOT2, 1, 2, UNIT)
            split_rest(U_REL[1], RELS, 2, UNIT)
            def expert_splits(n):
                pool.iota(iota_e[:, :], [[1, EXPERTS]], base=0, channel_multiplier=0, allow_small_or_imprecise_dtypes=True).then_inc(consts, 1)
                pool.iota(iota_m[:, :], [[1, MORE]], base=0, channel_multiplier=0, allow_small_or_imprecise_dtypes=True).then_inc(consts, 1)
                pool.memset(ones_e[:, :], 1.0).then_inc(consts, 1)
                pool.memset(restart_e[:, :, 1:CHOICES], 1.0).then_inc(consts, 1)
                pool.memset(restart_e[:, :, 0:1], 0.0).then_inc(consts, 1)
                pool.memset(before_e[:, :], 0.0).then_inc(consts, 1)
                pool.wait_ge(consts, 14 + 6 * (n + 1))
                pool.affine_select(out=before_e[:, :], in_=before_e[:, :], compare_op=ALU.is_ge, fill=1.0, base=0,
                                   pattern=[[-1, P]], channel_multiplier=1).then_inc(masks, 1)
                pool.sem_inc(e_lo[n], RING)
                units = FFN_UNITS[n]

                def low(i, b):
                    for c, (rows, k, cols) in enumerate(units):
                        s = (b * len(units) + c) % RING
                        hi, lo = at(W4[s], slice(0, rows), slice(0, k * cols))
                        pool.wait_ge(e_hi[n], (2 * i + b) * len(units) + c + 1)
                        pool.tensor_tensor(lo, RAW4[s][0:rows, 0:k * cols], f32(hi), ALU.subtract).then_inc(e_lo[n], 1)

                pool.wait_ge(cleared, 16)
                pool.wait_ge(placed, 2 * (n + 1))
                for t in range(TILES):
                    rows = LAST if t == FULL else P
                    for k in range(CHOSEN):
                        j = t * CHOSEN + k
                        pool.indirect_dma_start(out=slot_rows_dram, out_offset=bass.IndirectOffsetOnAxis(ap=place[0:rows, j:j + 1], axis=0),
                                                in_=XE[0:rows, t, :], in_offset=None).then_inc(sent, 16)
                with pool.Fori(0, XSLOTS // 2) as i:
                    for b in range(2):
                        low(i, b)
                for b in range(2):
                    pool.wait_ge(y_out[n][b], 16 + 16 * (XSLOTS // 2))
                for k in range(CHOSEN):
                    for t in range(TILES):
                        rows = LAST if t == FULL else P
                        j = t * CHOSEN + k
                        pool.indirect_dma_start(out=out_rows[k][0:rows, t, :], out_offset=None, in_=slot_out_dram[n],
                                                in_offset=bass.IndirectOffsetOnAxis(ap=place[0:rows, j:j + 1], axis=0)).then_inc(back[k], 16)

            after_phase(pool, 7)
            expert_splits(0)
            pool.wait_ge(e_used[0], RING + SPLITS[0])
            split_rest(U_MIX1, 4, 2, UNIT)
            split_rest(U_XL[0], GHEADS, 2, KD * GCOL)
            split_rest(U_XL[1], DIM // GCOL, 2, GAT1 // P * GCOL)
            after_phase(pool, 12)
            expert_splits(1)

        @block.scalar
        def _(act):
            def std_of(n):
                act.wait_ge(ln_var, TILES * (n + 1))
                act.activation(std[:, :], mv[:, :, 1], ACT.Sqrt, bias=eps_col[:, :]).then_inc(ln_std, 1)

            def transposes_hi(start, kd=KD):
                g = start
                for t in range(TILES):
                    for ks in groups_of(kd):
                        (into, k), n = chunk_of(ks[0]), len(ks)
                        act.wait_ge(tr_full, g + 1)
                        act.activation(into[0][:, k:k + n, t * P:(t + 1) * P], ps[:, g % 8, 0:n * P].rearrange("p (k n) -> p k n", k=n),
                                       ACT.Copy).then_inc(tr_hi, 1)
                        g += 1

            def rows_split_hi(src, ready):
                for t in range(TILES):
                    ready(t)
                    act.activation(xn[0][:, t, :], src[:, t, :], ACT.Copy).then_inc(rows_hi, 1)

            act.wait_ge(consts, 12)
            act.dma_start(sorted_dram.rearrange("(p c) o -> p (c o)", p=P), fill_i[:, :]).then_inc(filled, 16)
            act.dma_start(bias_row[0][:, :], a["L0_mix_b_qkv"][2 * DIM:3 * DIM].partition_broadcast(P)).then_inc(bias_in, 16)
            act.dma_start(bias_row[1][:, :], a["L0_mix_b_proj"].partition_broadcast(P)).then_inc(bias_in, 16)
            for h in range(2):
                act.dma_start(rf2[:, :, h * HEAD0:(h + 1) * HEAD0], a["L0_mix_random_features"].rearrange("(c p) d -> p c d", p=P)).then_inc(rf_in, 16)
            act.dma_start(qk_bias[:, :], a["L0_mix_b_qkv"][0:2 * DIM].rearrange("(j p) -> p j", p=P), allow_slow_non_contiguous=True).then_inc(rf_in, 16)
            act.wait_ge(consts, 14)
            act.dma_start(slot_rows_dram.rearrange("(s p) d -> p s d", p=P), zero_row[:, :].unsqueeze(1).broadcast_to([P, 2 * XSLOTS, DIM])).then_inc(cleared, 16)
            std_of(0)
            transposes_hi(TR_0)
            act.wait_ge(rf_full, 1)
            act.activation(rfT[0][:, :], ps[:, 2, 0:FEATS], ACT.Copy).then_inc(rf_hi, 1)
            end_phase(act, "act", 1)
            with act.Fori(0, PAIRS) as j:
                for n in range(2):
                    act.wait_ge(A_full, 12 * j + 2 * n + 2)
                    act.activation(halves((qT, kT)[n][0][:, :]), ps[:, 2 * n:2 * n + 2, 0:HALF], ACT.Identity,
                                   bias=qk_bias[:, ds(n * KD + j, 1)]).then_inc(A_hi, 2)
                for n in range(2):
                    t = slice(4 * n, min(4 * n + 4, TILES))
                    act.wait_ge(B_val, 2 * j + n + 1)
                    act.activation(v[0][:, t, :], v_f[:, t, :], ACT.Copy).then_inc(B_hi, 1)
                for s in range(2):
                    for n in range(3):
                        t = slice(2 * n, min(2 * n + 2, TILES))
                        w = t.stop - t.start
                        act.wait_ge(B_full, 10 * j + 4 * s + n + 3)
                        act.activation(phi_k[0][:, t, :], ps[:, 4 + n % 2, 0:w * FEATS].rearrange("p (t m) -> p t m", t=w),
                                       ACT.Relu).then_inc(B_hi, 1)
                    for n in range(2):
                        act.wait_ge(A_full, 12 * j + 4 * s + 2 * n + 6)
                        act.activation(halves(phi_qT[0][:, n, :]), ps[:, 2 * n:2 * n + 2, 0:HALF], ACT.Relu).then_inc(A_hi, 2)
                    act.wait_ge(B_full, 10 * j + 4 * s + 6)
                    act.activation(kv[0][:, :, s, s * HEAD0:(s + 1) * HEAD0], ps[:, 5, 0:2 * HEAD0].rearrange("p (m d) -> p m d", m=2),
                                   ACT.Copy).then_inc(B_hi, 1)
                act.wait_ge(C_full, 2 * j + 2)
                act.activation(attnT[0][:, ds(j, 1), :].rearrange("p k (h n) -> p (k h) n", h=2), ps[:, 6:8, 0:HALF], ACT.Copy,
                               scale=MIX0_SCALE).then_inc(C_hi, 1)
            end_phase(act, "act", 2)
            act.dma_start(bias_row[0][:, :], a["L0_gnn_b1"].partition_broadcast(P)).then_inc(bias_in, 16)
            act.dma_start(bias_row[1][:, :], a["L0_gnn_b2"].partition_broadcast(P)).then_inc(bias_in, 16)
            end_phase(act, "act", 3)
            act.wait_ge(adj_out, 16)
            act.wait_ge(cleared, 16)
            rows_split_hi(XN, lambda t: None)
            end_phase(act, "act", 4)
            for layer in range(2):
                if layer == 1:
                    rows_split_hi(ACC, lambda t: act.wait_ge(rows_ready, ROWS_H + t + 1))
                    transposes_hi(TR_H)
                    end_phase(act, "act", 6)
                act.sem_inc(a_ready[layer], FREE_BUF)
                with act.Fori(0, RELS // 2) as i:
                    for b in range(2):
                        act.wait_ge(a_in[layer][b], 16 * i + 16)
                        act.wait_ge(agg_full[layer], AGGS * (2 * i + b + 1))
                        act.activation(A_r[b][:, :, :], A_u[b][:, :, :], ACT.Copy).then_inc(a_ready[layer], 1)
                        for n in range(AGGS):
                            act.wait_ge(agg_val[layer], FREE_AGG + AGGS * (2 * i + b) + n + 1)
                            act.activation(XT[0][:, n // 2, cols_half(n)], agg_f[n % 3][:, :], ACT.Copy).then_inc(agg_hi[layer], 1)
                end_phase(act, "act", (5, 7)[layer])

            def experts(n, router_w, router_b, out_bias, in_biases):
                act.dma_start(gate_raw[:, :, :], chunks(router_w)).then_inc(gate_in, 16)
                act.dma_start(gate_b[:, :], router_b.rearrange("(e o) -> e o", o=1)).then_inc(gate_in, 16)
                act.dma_start(out_b[:, :], out_bias).then_inc(gate_in, 16)
                for m, src in enumerate(in_biases):
                    count, width = IN_B[n][m]
                    act.dma_start(in_b_rows[m][0:EXPERTS * count, 0:width], src.rearrange("e (c p) -> (e c) p", p=width)).then_inc(gate_in, 16)
                std_of(LN_FFN[n])
                transposes_hi(TR_FFN[n])
                for m, (count, width) in enumerate(IN_B[n]):
                    act.wait_ge(in_b_full, 2 * n + m + 1)
                    act.activation(in_b[m][0:width, 0:EXPERTS * count], ps[0:width, 3 + m, 0:EXPERTS * count], ACT.Copy).then_inc(in_b_ready, 1)
                act.wait_ge(gate_arg, n + 1)
                act.activation(expo[:, :, :], diff[:, :, :], ACT.Exp).then_inc(gate_exp, 1)
                act.wait_ge(in_b_ready, 2 + n)
                act.sem_inc(h_act[n], FREE_H)
                act.sem_inc(y_out[n][0], 16)
                act.sem_inc(y_out[n][1], 16)
                steps, units = HIDDEN[n], FFN_UNITS[n]

                def high(i, b, c):
                    u = (2 * i + b) * len(units) + c
                    s = (b * len(units) + c) % RING
                    rows, k, cols = units[c % len(units)]
                    act.wait_ge(eraw_ready[n][s], 16 * len(units) // 2 * i + 16 * ((b * len(units) + c) // RING + 1))
                    act.wait_ge(e_used[n], u + 1)
                    act.activation(W4[s][0][0:rows, 0:k * cols], RAW4[s][0:rows, 0:k * cols], ACT.Copy).then_inc(e_hi[n], 1)

                def rows_in(i, b):
                    act.wait_ge(t_full[n], 3 * (2 * i + b) + 1)
                    act.dma_start(slot_in[b][:, :, :], slot_at(slot_rows_dram, i, b)).then_inc(slot_ready[n][b], 16)

                def rows_hi(i, b):
                    for q in range(Q_T):
                        act.wait_ge(t_full[n], FREE_IN + 3 * (2 * i + b) + q + 1)
                        act.activation(XT[0][:, 2 * q:2 * q + 2, b * SLOT_ROWS:(b + 1) * SLOT_ROWS],
                                       ps[:, T_BANK + q, :].rearrange("p (k n) -> p k n", k=2), ACT.Copy).then_inc(t_hi[n], 1)

                def slot(i, b, last):
                    end = i == XSLOTS // 2 - 1 if isinstance(i, int) else False
                    e = act.value_load(slot_expert[0:1, ds(2 * i + b, 1)], min_val=0, max_val=EXPERTS - 1)
                    if not end:
                        rows_in(i + 1, b)
                    for v in range(len(units)):
                        for g, (unit, _, width, _, into, m) in enumerate(steps):
                            if unit != v:
                                continue
                            at_step = 2 * len(steps) * i + b * len(steps) + g
                            act.wait_ge(h_lo[n], at_step + places_left(n, g))
                            act.wait_ge(h_full[n], at_step + 1)
                            full, exact = hidden_at(g, width)
                            bias = in_b[m][0:width, ds(e * IN_B[n][m][0] + (g if m == 0 else g - IN_B[n][0][0]), 1)]
                            act.activation(hT[0][0:width, into, :], full, ACT.Gelu, bias=bias)
                            act.activation(exact, full, ACT.Gelu, bias=bias).then_inc(h_act[n], 1)
                        if v == ROWS_AFTER[n] and not last:
                            rows_hi(i + b, 1 - b)
                        if not (last and v + AHEAD >= len(units)):
                            high(i, b, v + AHEAD)
                    act.wait_ge(y_used[n], FREE_Y + 2 * OUTPUT[n][1] * (2 * i + b + 1))
                    act.dma_start(slot_at(slot_out_dram[n], i, b), y_rows[b][:, :, :]).then_inc(y_out[n][b], 16)

                for c in range(AHEAD):
                    high(0, 0, c)
                act.wait_ge(sent, 16 * CHOICES * (n + 1))
                for b in range(2):
                    rows_in(0, b)
                rows_hi(0, 0)
                act.wait_ge(placed, 2 * (n + 1))
                slot_pairs(act, slot)

            experts(0, a["L0_ffn_Wg"], a["L0_ffn_bg"], a["L0_ffn_b3"], [a["L0_ffn_b1"], a["L0_ffn_b2"]])
            end_phase(act, "act", 8)

            for t, name in ((in_gain, "ln_in_g"), (in_shift, "ln_in_b"), (out_gain, "ln_out_g"), (out_shift, "ln_out_b")):
                act.dma_start(t[:, :], a["L1_mix_" + name].partition_broadcast(P)).then_inc(mix_in, 16)
            std_of(LN_IN1)
            std_of(LN_MIX_IN)
            transposes_hi(TR_MIX_IN)
            for n, (rows, start) in enumerate(((Q, PR_Q), (K, PR_K))):
                for t in range(TILES):
                    act.wait_ge(prod_used, start + TILES + t + 1)
                    if n * TILES + t > 0:
                        act.wait_ge(norm_done, n * TILES + t)
                    act.activation(square[:, :], rows[:, t, :], ACT.Square, accum_out=norm[:, n, t:t + 1]).then_inc(norm_done, 1)
            act.wait_ge(norm_done, 2 * TILES)
            act.activation(norm[:, :, :], norm[:, :, :], ACT.Sqrt).then_inc(norm_done, 1)
            std_of(LN_MIX_OUT)
            transposes_hi(TR_MIX_OUT)
            end_phase(act, "act", 9)
            transposes_hi(TR_XN1)
            end_phase(act, "act", 10)

            def gat(layer):
                heads, units, kd = GAT[layer]
                tiles = heads * TILES
                heads_seen = layer * GHEADS
                seen = heads_seen * TILES
                XL, PT, a_row = ((XL1, PT1, a_row1), (XL2, PT2, a_row2))[layer]

                def xl_chunk(h, u, t):
                    n = (h * units + u) * TILES + t
                    act.wait_ge(xl_full, seen + n + 1)
                    if h >= len(XL):
                        act.wait_ge(o_full, seen + (h - len(XL) + 1) * TILES)
                    act.activation(XL[h % len(XL)][0][:, t, u * GCOL:(u + 1) * GCOL], ps[:, n % 2, 0:GCOL], ACT.Copy).then_inc(xl_hi, 1)

                def weights_hi(g):
                    act.wait_ge(pt_full, seen + g + 1)
                    r = len(PT)
                    if g >= r:
                        act.wait_ge(o_full, seen + g - r + 1)
                    hi = PT[g % r][0]
                    act.activation(hi[:, 0:FULL, :], ps[:, 4, 0:FULL * P].rearrange("p (t n) -> p t n", t=FULL), ACT.Copy)
                    act.activation(hi[:, FULL, :], ps[:, 5, 0:P], ACT.Copy).then_inc(pt_hi, 1)

                def exponentials(g):
                    act.wait_ge(e_ready, seen + g + 1)
                    act.activation(g_e[g % 2][:, :], g_e[g % 2][:, :], ACT.Exp, bias=g_neg[:, g % 2:g % 2 + 1]).then_inc(e_exp, 1)

                for u in range(units):
                    for t in range(TILES):
                        xl_chunk(0, u, t)
                for g in range(tiles + 2):
                    h, t = g // TILES, g % TILES
                    if h + 1 < heads:
                        xl_chunk(h + 1, 0, t)
                    if 0 <= g - 2 < tiles:
                        weights_hi(g - 2)
                    if g < tiles:
                        exponentials(g)
                act.wait_ge(xl_done, seen + heads * units * TILES)
                for k, n in enumerate(("be", "br")):
                    act.dma_start(a_row[k][:, :], a[f"L1_gnn_{n}{layer + 1}"].partition_broadcast(P)).then_inc(late_in[layer], 16)
                std_of(LN_GAT[layer])
                if layer == 0:
                    transposes_hi(TR_H1, GAT1 // P)

            for k, n in enumerate(("L1_gnn_a_src1", "L1_gnn_a_dst1")):
                act.dma_start(a_row1[k][:, :], a[n].rearrange("h c -> (h c)").partition_broadcast(P)).then_inc(gat_in[0], 16)
            for n in row1:
                act.dma_start(row1[n][:, :], a[f"L1_gnn_{n}1"].partition_broadcast(P)).then_inc(gat_in[0], 16)
            gat(0)
            end_phase(act, "act", 11)
            for k, n in enumerate(("L1_gnn_a_src2", "L1_gnn_a_dst2")):
                act.dma_start(a_row2[k][:, :], a[n].rearrange("h c -> (h c)").partition_broadcast(P)).then_inc(gat_in[1], 16)
            act.dma_start(bias_row[0][:, :], a["L1_gnn_b2"].partition_broadcast(P)).then_inc(gat_in[1], 16)
            act.dma_start(bias_row[1][:, :], a["L1_gnn_g2"].partition_broadcast(P)).then_inc(gat_in[1], 16)
            gat(1)
            end_phase(act, "act", 12)
            experts(1, a["L1_ffn_router_w"], a["L1_ffn_router_b"], a["L1_ffn_b2"], [a["L1_ffn_b1"]])
            end_phase(act, "act", 13)

        @block.vector
        def _(vec):
            order = Order(vec, vec_order)

            def normalise(n, src, dst, ready=True, width=DIM):
                for t in range(TILES):
                    for c in range(2):
                        order.step(vec.bn_stats(stats[:, t, c, :], src[:, t, c * width // 2:(c + 1) * width // 2]))
                order.wait()
                for t in range(TILES):
                    vec.bn_aggr(mv[:, t, :], stats[:, t, :, :]).then_inc(ln_var, 1)
                vec.wait_ge(ln_std, n + 1)
                order.step(vec.reciprocal(rstd[:, :], std[:, :]))
                order.wait()
                for t in range(TILES):
                    ins = vec.tensor_scalar(dst[:, t, :], src[:, t, :], mv[:, t, 0:1], rstd[:, t:t + 1], ALU.subtract, ALU.mult)
                    if ready:
                        ins.then_inc(rows_ready, 1)
                    else:
                        order.step(ins)

            def transposes_lo(start, kd=KD):
                g = start
                for t in range(TILES):
                    for ks in groups_of(kd):
                        (into, k), n = chunk_of(ks[0]), len(ks)
                        vec.wait_ge(tr_hi, g + 1)
                        hi, lo = at(into, slice(None), slice(k, k + n), slice(t * P, (t + 1) * P))
                        vec.tensor_tensor(lo, ps[:, g % 8, 0:n * P].rearrange("p (k n) -> p k n", k=n), f32(hi), ALU.subtract).then_inc(tr_done, 1)
                        g += 1

            def rows_split_lo(n, src):
                for t in range(TILES):
                    vec.wait_ge(rows_hi, TILES * n + t + 1)
                    vec.tensor_tensor(xn[1][:, t, :], src[:, t, :], f32(xn[0][:, t, :]), ALU.subtract).then_inc(rows_lo, 1)

            def add_products(start, rows, bias=None, units=2, cols=WCOL):
                for j in range(units * TILES):
                    g = start + j
                    c, t = j // TILES, j % TILES
                    col = slice(c * cols, (c + 1) * cols)
                    vec.wait_ge(prod_full, g + 1)
                    vec.tensor_tensor(rows[:, t, col], ps[:, g % 8, 0:cols],
                                      rows[:, t, col] if bias is None else bias[:, col], ALU.add).then_inc(prod_used, 1)

            def take_products(start, rows):
                for j in range(SET):
                    c, t = j // TILES, j % TILES
                    vec.wait_ge(prod_full, start + j + 1)
                    vec.tensor_copy(rows[:, t, wcols(c)], ps[:, (start + j) % 8, 0:WCOL]).then_inc(prod_used, 1)

            def scale_shift(rows, gain, shift, ready):
                order.wait()
                for t in range(TILES):
                    order.step(vec.tensor_tensor(rows[:, t, :], rows[:, t, :], gain[:, :], ALU.mult))
                order.wait()
                for t in range(TILES):
                    ins = vec.tensor_tensor(rows[:, t, :], rows[:, t, :], shift[:, :], ALU.add)
                    if ready:
                        ins.then_inc(rows_ready, 1)
                    else:
                        order.step(ins)

            def add_bias(rows, bias):
                for t in range(TILES):
                    order.step(vec.tensor_tensor(rows[:, t, :], rows[:, t, :], bias[:, :], ALU.add))

            vec.wait_ge(x_in, 32)
            vec.wait_ge(pad_zero, 1)
            normalise(0, X, XN)
            transposes_lo(TR_0)
            vec.wait_ge(rf_hi, 1)
            order.step(vec.tensor_tensor(rfT[1][:, :], ps[:, 2, 0:FEATS], f32(rfT[0][:, :]), ALU.subtract))
            vec.wait_ge(edges_in, 48)
            vec.wait_ge(consts, 12)
            order.step(vec.tensor_scalar(tile_i[:, :], src_i[:, :], 7, None, ALU.arith_shift_right))
            order.step(vec.tensor_scalar(low_i[:, :], src_i[:, :], P - 1, None, ALU.bitwise_and))
            order.wait()
            order.step(vec.scalar_tensor_tensor(group_f[:, :], typ_i[:, :], float(TILES), tile_i[:, :], ALU.mult, ALU.add))
            order.step(vec.scalar_tensor_tensor(code_i[:, :], low_i[:, :], 1024.0, dst_i[:, :], ALU.mult, ALU.add))
            order.wait()
            every = [EDGE_ROWS, GROUPS, EDGE_COLS]
            order.step(vec.tensor_tensor(onehot_g[:, :, :], group_f[:, :].unsqueeze(1).broadcast_to(every),
                                         iota_g[:, :].unsqueeze(2).broadcast_to(every), ALU.is_equal))
            order.wait()
            order.step(vec.tensor_tensor_scan(rank[:, :, :].rearrange("p g c -> p (g c)"), restart[:, :, :].rearrange("p g c -> p (g c)"),
                                              onehot_g[:, :, :].rearrange("p g c -> p (g c)"), 0.0, ALU.mult, ALU.add))
            order.wait()
            vec.tensor_copy(in_row[:, :], rank[:, :, EDGE_COLS - 1]).then_inc(sort_row, 1)
            vec.wait_ge(sort_sum, 2)
            order.step(vec.tensor_scalar(need_i[:, :], ps[0:EDGE_ROWS, 1, 0:GROUPS], float(SLOT - 1), None, ALU.add))
            order.wait()
            order.step(vec.tensor_scalar(need_s[:, :], need_i[:, :], SLOT.bit_length() - 1, None, ALU.arith_shift_right))
            order.wait()
            order.step(vec.tensor_copy(need_f[:, :], need_s[:, :]))
            order.wait()
            order.step(vec.tensor_tensor_scan(slot_end[:, :], ones_g[:, :], need_f[:, :], 0.0, ALU.mult, ALU.add))
            order.wait()
            order.step(vec.tensor_tensor(slot_base[:, :], slot_end[:, :], need_f[:, :], ALU.subtract))
            order.wait()
            order.step(vec.scalar_tensor_tensor(offset_g[:, :], slot_base[:, :], float(SLOT), ps[0:EDGE_ROWS, 0, 0:GROUPS], ALU.mult, ALU.add))
            order.wait()
            order.step(vec.scalar_tensor_tensor(rank[:, :, :], rank[:, :, :], -1.0, offset_g[:, :].unsqueeze(2).broadcast_to(every), ALU.add, ALU.add))
            order.wait()
            order.step(vec.tensor_tensor(rank[:, :, :], rank[:, :, :], onehot_g[:, :, :], ALU.mult))
            order.wait()
            order.step(vec.tensor_reduce(pos_f[:, :], rank[:, :, :].rearrange("p g c -> p c g"), AX.X, ALU.add))
            order.wait()
            order.step(vec.tensor_copy(spot_i[:, :], pos_f[:, :]))
            order.wait()
            order.step(vec.tensor_scalar(low_i[:, :], spot_i[:, :], P - 1, None, ALU.bitwise_and))
            order.step(vec.tensor_scalar(sub_i[:, :], spot_i[:, :], 7, None, ALU.arith_shift_right))
            order.wait()
            vec.scalar_tensor_tensor(pos_i[:, :], low_i[:, :], float(SUBS), sub_i[:, :], ALU.mult, ALU.add).then_inc(pos_ready, 1)
            sg = [1, SLOTS, GROUPS]
            order.step(vec.tensor_tensor(past[:, :, :], slot_end[0:1, :].unsqueeze(1).broadcast_to(sg), iota_s[:, :].unsqueeze(2).broadcast_to(sg), ALU.is_le))
            order.wait()
            order.step(vec.tensor_reduce(group_of[:, :], past[:, :, :], AX.X, ALU.add))
            order.wait()
            order.step(vec.tensor_scalar(slot_group[:, :], group_of[:, :], float(GROUPS - 1), None, ALU.min))
            vec.wait_ge(bias_in, 32)
            add_bias(X, bias_row[1])
            end_phase(vec, "vec", 1)
            for part in kv:
                order.step(vec.memset(f32(part[:, :, :, :]), 0.0))
            vec.sem_inc(A_done, FREE_A)
            vec.sem_inc(B_done, FREE_B)
            vec.sem_inc(C_done, FREE_C)
            with vec.Fori(0, PAIRS) as j:
                for n in range(2):
                    t = (qT, kT)[n]
                    vec.wait_ge(A_hi, 12 * j + 2 * n + 2)
                    vec.scalar_tensor_tensor(halves(t[1][:, :]), ps[:, 2 * n:2 * n + 2, 0:HALF], qk_bias[:, ds(n * KD + j, 1)], halves(f32(t[0][:, :])),
                                             ALU.add, ALU.subtract).then_inc(A_done, 2)
                for n in range(2):
                    t = slice(4 * n, min(4 * n + 4, TILES))
                    w = t.stop - t.start
                    vec.wait_ge(B_full, 10 * j + n + 1)
                    vec.tensor_tensor(v_f[:, t, :], ps[:, 4 + n, 0:w * P].rearrange("p (t d) -> p t d", t=w),
                                      bias_row[0][:, ds(j * P, P)].unsqueeze(1).broadcast_to([P, w, P]), ALU.add).then_inc(B_val, 1)
                for n in range(2):
                    t = slice(4 * n, min(4 * n + 4, TILES))
                    vec.wait_ge(B_hi, 10 * j + n + 1)
                    vec.tensor_tensor(v[1][:, t, :], v_f[:, t, :], f32(v[0][:, t, :]), ALU.subtract).then_inc(B_done, 1)
                for s in range(2):
                    for n in range(3):
                        t = slice(2 * n, min(2 * n + 2, TILES))
                        w = t.stop - t.start
                        vec.wait_ge(B_hi, 10 * j + 4 * s + n + 3)
                        vec.scalar_tensor_tensor(phi_k[1][:, t, :], ps[:, 4 + n % 2, 0:w * FEATS].rearrange("p (t m) -> p t m", t=w), 0.0,
                                                 f32(phi_k[0][:, t, :]), ALU.max, ALU.subtract).then_inc(B_done, 1)
                    for n in range(2):
                        vec.wait_ge(A_hi, 12 * j + 4 * s + 2 * n + 6)
                        vec.scalar_tensor_tensor(halves(phi_qT[1][:, n, :]), ps[:, 2 * n:2 * n + 2, 0:HALF], 0.0, halves(f32(phi_qT[0][:, n, :])),
                                                 ALU.max, ALU.subtract).then_inc(A_done, 2)
                    vec.wait_ge(B_hi, 10 * j + 4 * s + 6)
                    own = slice(s * HEAD0, (s + 1) * HEAD0)
                    vec.tensor_tensor(kv[1][:, :, s, own], ps[:, 5, 0:2 * HEAD0].rearrange("p (m d) -> p m d", m=2),
                                      f32(kv[0][:, :, s, own]), ALU.subtract).then_inc(B_done, 1)
                vec.wait_ge(C_hi, j + 1)
                hi, lo = [t[:, ds(j, 1), :].rearrange("p k (h n) -> p (k h) n", h=2) for t in attnT]
                vec.scalar_tensor_tensor(lo, ps[:, 6:8, 0:HALF], MIX0_SCALE, f32(hi), ALU.mult, ALU.subtract).then_inc(C_done, 2)
            add_products(PR_PROJ, X)
            end_phase(vec, "vec", 2)
            order.step(vec.memset(adj[:, :, :], 0))
            vec.wait_ge(sorted_in, 16)
            order.step(vec.tensor_scalar(part_i[:, :], sorted_sb[:, :], 10, None, ALU.arith_shift_right))
            order.wait()
            order.step(vec.tensor_copy(srcl_f[:, :], part_i[:, :]))
            order.step(vec.tensor_scalar(sorted_sb[:, :], sorted_sb[:, :], 1023, None, ALU.bitwise_and))
            order.wait()
            order.step(vec.tensor_copy(dst_f[:, :], sorted_sb[:, :]))
            order.wait()
            vec.sem_inc(slot_done, FREE_SUM)
            with vec.Fori(0, SLOTS // 2) as i:
                for b in range(2):
                    vec.wait_ge(slot_full, 2 * i + b + 1)
                    for h in range(2):
                        sub = ds(4 * i + 2 * b + h, 1)
                        vec.tensor_scalar(src_hot[b][:, h, :], dst_iota[:, 0:P], srcl_f[:, sub], None, ALU.is_equal)
                        ins = vec.tensor_scalar(dst_hot[b][:, h, :], dst_iota[:, :], dst_f[:, sub], None, ALU.is_equal)
                        ins.then_inc(hot, 1)
                for b in range(2):
                    g = vec.value_load(slot_group[0:1, ds(2 * i + b, 1)], min_val=0, max_val=GROUPS - 1)
                    vec.wait_ge(slot_full, FREE_HOT + 2 * i + b + 1)
                    vec.wait_ge(slot_done, 2 * i + b + 1)
                    block_of = adj[:, ds(g, 1), :].rearrange("p g (h c) -> p (g h) c", h=2)
                    vec.tensor_tensor(block_of, block_of, ps[:, 2 * b:2 * b + 2, 0:HALF], ALU.add).then_inc(slot_done, 1)
            end_phase(vec, "vec", 3)
            vec.wait_ge(adj_out, 16)
            rows_split_lo(0, XN)
            vec.wait_ge(bias_in, 64)
            add_products(PR_ROOT1, ACC, bias_row[0])
            add_bias(X, bias_row[1])
            end_phase(vec, "vec", 4)
            for layer in range(2):
                rows = (ACC, X)[layer]
                if layer == 1:
                    for t in range(TILES):
                        vec.tensor_scalar(ACC[:, t, :], ACC[:, t, :], 0.0, None, ALU.max).then_inc(rows_ready, 1)
                    rows_split_lo(1, ACC)
                    transposes_lo(TR_H)
                    add_products(PR_ROOT2, X)
                    end_phase(vec, "vec", 6)
                vec.sem_inc(cnt_used[layer], FREE_CNT)
                vec.sem_inc(agg_val[layer], FREE_AGG)
                vec.sem_inc(agg_done[layer], FREE_DONE)
                vec.sem_inc(tra_used[layer], FREE_TRA)
                with vec.Fori(0, RELS // 2) as i:
                    for b in range(2):
                        for n in range(2):
                            vec.wait_ge(cnt_full[layer], 4 * i + 2 * b + n + 1)
                            vec.tensor_scalar(cnt_m[:, n, :], ps[:, 6 + n, 0:HALF], 1.0, None, ALU.max).then_inc(cnt_used[layer], 1)
                        vec.wait_ge(cnt_used[layer], FREE_CNT + 4 * i + 2 * b + 2)
                        if b == 0:
                            order.enter(i, 2)
                        order.step(vec.reciprocal(inv[b][:, :, :], cnt_m[:, :, :]))
                        order.wait()
                        for n in range(AGGS + 1):
                            if n < AGGS:
                                vec.wait_ge(agg_full[layer], FREE_BUF * AGGS + AGGS * (2 * i + b) + n + 1)
                                vec.wait_ge(agg_done[layer], AGGS * (2 * i + b) + n + 1)
                                vec.tensor_tensor(agg_f[n % 3][:, :], ps[:, n % 4, 0:HALF], inv[b][:, n % 2, :], ALU.mult).then_inc(agg_val[layer], 1)
                            if n > 0:
                                m = n - 1
                                vec.wait_ge(agg_hi[layer], AGGS * (2 * i + b) + m + 1)
                                vec.tensor_tensor(XT[1][:, m // 2, cols_half(m)], agg_f[m % 3][:, :], f32(XT[0][:, m // 2, cols_half(m)]),
                                                  ALU.subtract).then_inc(agg_done[layer], 1)
                        for n in range(2 * TILES):
                            c, t = n // TILES, n % TILES
                            vec.wait_ge(tra_full[layer], 2 * TILES * (2 * i + b) + n + 1)
                            vec.wait_ge(tra_used[layer], 2 * TILES * (2 * i + b) + n + 1)
                            vec.tensor_tensor(rows[:, t, wcols(c)], rows[:, t, wcols(c)], ps[:, 4 + n % 2, 0:WCOL], ALU.add).then_inc(tra_used[layer], 1)
                order.leave(RELS // 2)
                end_phase(vec, "vec", (5, 7)[layer])

            def experts(n):
                normalise(LN_FFN[n], X, XE)
                transposes_lo(TR_FFN[n])
                vec.wait_ge(gate_in, 16 * (5 + 4 * n))
                order.step(vec.tensor_copy(gate_w[0][:, :, :], gate_raw[:, :, :]))
                order.wait()
                vec.tensor_tensor(gate_w[1][:, :, :], gate_raw[:, :, :], f32(gate_w[0][:, :, :]), ALU.subtract).then_inc(gate_split, 1)
                every = [P, TILES, EXPERTS]
                vec.wait_ge(gate_full, 2 * n + 1)
                vec.tensor_scalar(halves(scoresT[:, :]), ps[0:EXPERTS, 0:2, 0:HALF], gate_b[:, :], None, ALU.add).then_inc(scoresT_ready, 1)
                vec.wait_ge(gate_full, 2 * (n + 1))
                order.step(vec.tensor_copy(scores[:, :, :], ps[:, 2, 0:TILES * EXPERTS].rearrange("p (t e) -> p t e", t=TILES)))
                order.wait()
                if n == 1:
                    order.step(vec.tensor_reduce(total[:, :], scores[:, :, :], AX.X, ALU.max))
                    order.wait()
                    vec.tensor_tensor(diff[:, :, :], scores[:, :, :], total[:, :].unsqueeze(2).broadcast_to(every), ALU.subtract).then_inc(gate_arg, 1)
                    vec.wait_ge(gate_exp, n + 1)
                    order.step(vec.tensor_reduce(total[:, :], expo[:, :, :], AX.X, ALU.add))
                    order.wait()
                    order.step(vec.reciprocal(share[:, :], total[:, :]))
                    order.wait()
                    order.step(vec.tensor_tensor(choice[:, :, :], expo[:, :, :], share[:, :].unsqueeze(2).broadcast_to(every), ALU.mult))
                    order.wait()
                values = (scores, choice)[n]
                vec.wait_ge(consts, 14 + 6 * (n + 1))
                for k in range(CHOSEN):
                    src = values if k == 0 else others
                    for t in range(TILES):
                        order.step(vec.max(top[k][:, t, :], src[:, t, :]))
                    order.wait()
                    for t in range(TILES):
                        order.step(vec.max_index(top_at[k][:, t, :], top[k][:, t, :], src[:, t, :]))
                    order.wait()
                    order.step(vec.tensor_copy(chosen[:, :, k], top_at[k][:, :, 0]))
                    order.wait()
                    ins = vec.tensor_tensor(is_chosen[:, :, k, :], chosen[:, :, k].unsqueeze(2).broadcast_to(every),
                                            iota_e[:, :].unsqueeze(1).broadcast_to(every), ALU.is_equal)
                    if k == 0:
                        order.step(ins)
                        order.wait()
                        order.step(vec.scalar_tensor_tensor(others[:, :, :], is_chosen[:, :, 0, :], BELOW, values[:, :, :], ALU.mult, ALU.add))
                        order.wait()
                    else:
                        ins.then_inc(chosen_ready, 1)
                if n == 0:
                    vec.tensor_tensor(diff[:, :, :], scores[:, :, :], top[0][:, :, 0].unsqueeze(2).broadcast_to(every), ALU.subtract).then_inc(gate_arg, 1)
                by_expert = [P, CHOICES, EXPERTS]
                flat = is_chosen[:, :, :, :].rearrange("p t k e -> p (t k) e")
                vec.wait_ge(rank_full, 2 * (n + 1))
                order.step(vec.tensor_copy(in_tile[:, :, :].rearrange("p e j -> p j e"), ps[:, 7, 0:CHOICES * EXPERTS].rearrange("p (j e) -> p j e", e=EXPERTS)))
                order.wait()
                order.step(vec.tensor_tensor_scan(through[:, :, :].rearrange("p e j -> p (e j)"), restart_e[:, :, :].rearrange("p e j -> p (e j)"),
                                                  in_tile[:, :, :].rearrange("p e j -> p (e j)"), 0.0, ALU.mult, ALU.add))
                order.wait()
                order.step(vec.tensor_scalar(need_e[:, :], through[:, :, CHOICES - 1], float(SLOT_ROWS - 1), None, ALU.add))
                order.step(vec.tensor_tensor(in_tile[:, :, :], through[:, :, :], in_tile[:, :, :], ALU.subtract))
                order.wait()
                order.step(vec.tensor_scalar(need_es[:, :], need_e[:, :], SLOT_ROWS.bit_length() - 1, None, ALU.arith_shift_right))
                order.step(vec.tensor_tensor(rank_of[:, :, :], ps[:, 1, 0:CHOICES * EXPERTS].rearrange("p (j e) -> p j e", e=EXPERTS),
                                             in_tile[:, :, :].rearrange("p e j -> p j e"), ALU.add))
                order.wait()
                order.step(vec.tensor_scalar(more[:, :], need_es[:, :], -1.0, 0.0, ALU.add, ALU.max))
                order.step(vec.tensor_tensor(rank_of[:, :, :], rank_of[:, :, :], flat, ALU.mult))
                order.wait()
                order.step(vec.tensor_tensor_scan(more_end[:, :], ones_e[:, :], more[:, :], 0.0, ALU.mult, ALU.add))
                order.step(vec.tensor_reduce(rank_e[:, :], rank_of[:, :, :], AX.X, ALU.add))
                order.wait()
                order.step(vec.tensor_tensor(more_at[:, :], more_end[:, :], more[:, :], ALU.subtract))
                order.step(vec.tensor_scalar(is_more[:, :], rank_e[:, :], float(SLOT_ROWS), None, ALU.is_ge))
                order.wait()
                order.step(vec.tensor_tensor(more_of[:, :, :], flat, more_at[:, :].unsqueeze(1).broadcast_to(by_expert), ALU.mult))
                order.step(vec.tensor_scalar(first_at[:, :], chosen[:, :, :].rearrange("p t k -> p (t k)"), float(SLOT_ROWS), None, ALU.mult))
                order.wait()
                order.step(vec.tensor_reduce(spill[:, :], more_of[:, :, :], AX.X, ALU.add))
                order.wait()
                order.step(vec.tensor_scalar(spill[:, :], spill[:, :], float(SLOT_ROWS), float((EXPERTS - 1) * SLOT_ROWS), ALU.mult, ALU.add))
                order.wait()
                order.step(vec.tensor_tensor(spill[:, :], spill[:, :], first_at[:, :], ALU.subtract))
                order.step(vec.tensor_tensor(rank_e[:, :], rank_e[:, :], first_at[:, :], ALU.add))
                order.wait()
                order.step(vec.tensor_tensor(spill[:, :], spill[:, :], is_more[:, :], ALU.mult))
                order.wait()
                order.step(vec.tensor_tensor(place_f[:, :], rank_e[:, :], spill[:, :], ALU.add))
                order.wait()
                vec.tensor_copy(place[:, :], place_f[:, :]).then_inc(placed, 1)
                sg = [1, MORE, EXPERTS]
                order.step(vec.tensor_tensor(past_e[:, :, :], more_end[0:1, :].unsqueeze(1).broadcast_to(sg), iota_m[:, :].unsqueeze(2).broadcast_to(sg), ALU.is_le))
                order.step(vec.tensor_copy(slot_expert_f[:, 0:EXPERTS], iota_e[0:1, :]))
                order.wait()
                order.step(vec.tensor_reduce(slot_expert_f[:, EXPERTS:XSLOTS], past_e[:, :, :], AX.X, ALU.add))
                order.wait()
                vec.tensor_scalar(slot_expert[:, :], slot_expert_f[:, :], float(EXPERTS - 1), None, ALU.min).then_inc(placed, 1)
                weights = share[:, :].unsqueeze(2).broadcast_to(every)
                if n == 0:
                    vec.wait_ge(gate_exp, n + 1)
                    values = expo
                order.step(vec.tensor_tensor(comb[:, :, :], is_chosen[:, :, 0, :], is_chosen[:, :, 1, :], ALU.add))
                order.wait()
                order.step(vec.tensor_tensor(comb[:, :, :], comb[:, :, :], values[:, :, :], ALU.mult))
                order.wait()
                if n == 0:
                    order.step(vec.tensor_reduce(total[:, :], comb[:, :, :], AX.X, ALU.add))
                    order.wait()
                    order.step(vec.reciprocal(share[:, :], total[:, :]))
                    order.wait()
                    order.step(vec.tensor_tensor(comb[:, :, :], comb[:, :, :], weights, ALU.mult))
                    order.wait()
                for k in range(CHOSEN):
                    ins = vec.tensor_tensor(gate_of[:, :, k, :], is_chosen[:, :, k, :], comb[:, :, :], ALU.mult)
                    if k == 0:
                        order.step(ins)
                    else:
                        ins.then_inc(comb_ready, 1)
                order.wait()
                vec.wait_ge(comb_ready, n + 1)
                order.step(vec.tensor_reduce(gate[:, :, :].rearrange("p t k -> p (t k)"), gate_of[:, :, :, :].rearrange("p t k e -> p (t k) e"), AX.X, ALU.add))
                vec.wait_ge(comb_full, n + 1)
                vec.tensor_copy(combT[:, 0:FULL * P], ps[0:EXPERTS, 5, 0:FULL * P]).then_inc(combT_ready, 1)
                vec.tensor_copy(combT[:, FULL * P:COLS], ps[0:EXPERTS, 6, 0:P]).then_inc(combT_ready, 1)
                add_products(PR_FFN[n], X)
                steps = HIDDEN[n]
                _, units, cols, _, _ = OUTPUT[n]

                def rows_lo(i, b):
                    for q in range(Q_T):
                        vec.wait_ge(t_hi[n], 3 * (2 * i + b) + q + 1)
                        hi, lo = at(XT, slice(None), slice(2 * q, 2 * q + 2), slice(b * SLOT_ROWS, (b + 1) * SLOT_ROWS))
                        vec.tensor_tensor(lo, ps[:, T_BANK + q, :].rearrange("p (k n) -> p k n", k=2), f32(hi), ALU.subtract).then_inc(t_lo[n], 1)

                def slot(i, b, last):
                    for g, (unit, _, width, _, into, _) in enumerate(steps):
                        vec.wait_ge(h_act[n], FREE_H + 2 * len(steps) * i + b * len(steps) + g + 1)
                        vec.tensor_tensor(hT[1][0:width, into, :], hidden_at(g, width)[1], f32(hT[0][0:width, into, :]),
                                          ALU.subtract).then_inc(h_lo[n], 1)
                        if unit == ROWS_AFTER[n] and unit != (steps + [(None,)])[g + 1][0] and not last:
                            rows_lo(i + b, 1 - b)
                    vec.wait_ge(y_out[n][b], 16 * i + 16)
                    for y in range(2 * units):
                        c, half = y // 2, y % 2
                        vec.wait_ge(y_full[n], 2 * units * (2 * i + b) + y + 1)
                        vec.tensor_copy(y_rows[b][:, half, c * cols:(c + 1) * cols], ps[:, 2 + y % 2, 0:cols]).then_inc(y_used[n], 1)

                vec.sem_inc(h_lo[n], FREE_LO)
                vec.sem_inc(t_lo[n], FREE_T)
                vec.sem_inc(y_used[n], FREE_Y)
                rows_lo(0, 0)
                slot_pairs(vec, slot)
                for k in range(CHOSEN):
                    vec.wait_ge(back[k], 16 * TILES * (n + 1))
                    order.wait()
                    for t in range(TILES):
                        rows = slice(0, LAST if t == FULL else P)
                        order.step(vec.scalar_tensor_tensor(X[rows, t, :], out_rows[k][rows, t, :], gate[rows, t, k:k + 1], X[rows, t, :], ALU.mult, ALU.add))
                order.wait()

            experts(0)
            end_phase(vec, "vec", 8)

            normalise(LN_IN1, X, XN1, ready=False)
            order.wait()
            normalise(LN_MIX_IN, XN1, XM, ready=False)
            vec.wait_ge(mix_in, 64)
            scale_shift(XM, in_gain, in_shift, True)
            transposes_lo(TR_MIX_IN)
            for start, rows in ((PR_Q, Q), (PR_K, K), (PR_V, V)):
                take_products(start, rows)
            vec.wait_ge(norm_done, 2 * TILES + 1)
            order.step(vec.tensor_scalar(norm_m[:, :, :], norm[:, :, :], NORM_EPS, None, ALU.max))
            order.wait()
            order.step(vec.reciprocal(inv_norm[:, :, :], norm_m[:, :, :]))
            order.wait()
            vec.wait_ge(prod_used, PR_V + SET)
            for t in range(TILES):
                vec.scalar_tensor_tensor(K[:, t, :], K[:, t, :], inv_norm[:, 1, t:t + 1], V[:, t, :], ALU.mult, ALU.mult).then_inc(kv_rows, 1)
            vec.wait_ge(kv_full, 2)
            for t in range(TILES):
                rows = Q[:, t, :].rearrange("p (c n) -> p c n", c=2)
                order.step(vec.scalar_tensor_tensor(rows, rows, inv_norm[:, 0, t:t + 1], ps[:, 0:2, 0:WCOL], ALU.mult, ALU.mult))
            order.wait()
            normalise(LN_MIX_OUT, Q, Q, ready=False)
            scale_shift(Q, out_gain, out_shift, True)
            transposes_lo(TR_MIX_OUT)
            add_products(PR_MIX1, X)
            end_phase(vec, "vec", 9)
            transposes_lo(TR_XN1)
            order.step(vec.memset(csum[:, :, :], 0.0))
            order.wait()
            vec.sem_inc(c_added, FREE_BUF)
            with vec.Fori(0, RELS // 2) as i:
                for b in range(2):
                    vec.wait_ge(c_in[b], 16 * i + 16)
                    vec.wait_ge(c_added, 2 * i + b + FREE_BUF)
                    vec.tensor_tensor(csum[:, :, :], csum[:, :, :], C_u[b][:, :, :], ALU.add).then_inc(c_added, 1)
            vec.wait_ge(c_added, RELS + FREE_BUF)
            for t in range(TILES):
                own = csum[:, t, t * P:(t + 1) * P]
                vec.tensor_tensor(own, own, ident[:, :], ALU.add).then_inc(c_added, 1)
            for t in range(TILES):
                vec.wait_ge(c_full, t + 1)
                order.step(vec.tensor_copy(count[:, t, 0:FULL * P], ps[:, 2 * (t % 2), 0:FULL * P]))
                order.step(vec.tensor_copy(count[:, t, FULL * P:COLS], ps[:, 2 * (t % 2) + 1, 0:P]))
                order.wait()
                vec.tensor_scalar(absent[:, t, :], count[:, t, :], 0.0, NO_EDGE, ALU.is_equal, ALU.mult).then_inc(c_done, 1)
            end_phase(vec, "vec", 10)

            def gat(layer):
                heads, units, kd = GAT[layer]
                tiles = heads * TILES
                heads_seen = layer * GHEADS
                seen = heads_seen * TILES
                XL, PT, a_row = ((XL1, PT1, a_row1), (XL2, PT2, a_row2))[layer]
                width = units * GCOL

                def xl_chunk(h, u, t):
                    n = (h * units + u) * TILES + t
                    vec.wait_ge(xl_hi, seen + n + 1)
                    chunk = ps[:, n % 2, 0:GCOL]
                    hi, lo = at(XL[h % len(XL)], slice(None), t, slice(u * GCOL, (u + 1) * GCOL))
                    order.step(vec.tensor_tensor(lo, chunk, f32(hi), ALU.subtract))
                    if n > 0:
                        vec.wait_ge(xl_done, seen + n)
                    for k in range(2):
                        sums = part_of[k][:, t, u:u + 1] if units > 1 else alpha[k][h % 2][:, t:t + 1]
                        col = slice((h * units + u) * GCOL, (h * units + u + 1) * GCOL)
                        ins = vec.scalar_tensor_tensor(junk[k][:, :], chunk, 1.0, a_row[k][:, col], ALU.mult, ALU.mult, accum_out=sums)
                        if k == 0:
                            order.step(ins)
                        else:
                            ins.then_inc(xl_done, 1)

                def diagonal(h):
                    vec.wait_ge(xl_done, seen + (h + 1) * units * TILES)
                    order.wait()
                    if units > 1:
                        for k in range(2):
                            order.step(vec.tensor_reduce(alpha[k][h % 2][:, :], part_of[k][:, :, :], AX.X, ALU.add))
                        order.wait()
                    if h > 0:
                        vec.wait_ge(row_full, heads_seen + h)
                    for t in range(TILES):
                        vec.tensor_scalar(diag[layer][:, t * P:(t + 1) * P], ident[:, :], alpha[0][h % 2][:, t:t + 1], None, ALU.mult).then_inc(diag_ready, 1)

                def logits(g):
                    h, t, s = g // TILES, g % TILES, g % 2
                    vec.wait_ge(row_full, heads_seen + h + 1)
                    if g >= 2:
                        vec.wait_ge(p_ready, seen + g - 1)
                    e = g_e[s]
                    order.step(vec.tensor_scalar(halves(e[:, :]), ps[:, 2:4, 0:HALF], alpha[1][h % 2][:, t:t + 1], None, ALU.add))
                    order.wait()
                    order.step(vec.scalar_tensor_tensor(e[:, :], e[:, :], SLOPE, e[:, :], ALU.mult, ALU.max))
                    order.wait()
                    order.step(vec.tensor_tensor(e[:, :], e[:, :], absent[:, t, :], ALU.add))
                    order.wait()
                    order.step(vec.tensor_reduce(g_max[:, s:s + 1], e[:, :], AX.X, ALU.max))
                    order.wait()
                    vec.tensor_scalar(g_neg[:, s:s + 1], g_max[:, s:s + 1], -1.0, None, ALU.mult).then_inc(e_ready, 1)

                def weights(g):
                    vec.wait_ge(e_exp, seen + g + 1)
                    if g >= 2:
                        vec.wait_ge(pt_full, seen + g - 1)
                    vec.scalar_tensor_tensor(g_p[g % 2][:, :], g_e[g % 2][:, :], 1.0, count[:, g % TILES, :], ALU.mult, ALU.mult,
                                             accum_out=g_sum[:, g:g + 1]).then_inc(p_ready, 1)

                def weights_lo(g):
                    vec.wait_ge(pt_hi, seen + g + 1)
                    hi, lo = PT[g % len(PT)]
                    order.step(vec.tensor_tensor(lo[:, 0:FULL, :], ps[:, 4, 0:FULL * P].rearrange("p (t n) -> p t n", t=FULL), f32(hi[:, 0:FULL, :]), ALU.subtract))
                    vec.tensor_tensor(lo[:, FULL, :], ps[:, 5, 0:P], f32(hi[:, FULL, :]), ALU.subtract).then_inc(pt_done, 1)
                    order.step(vec.tensor_scalar(g_sum_e[:, g:g + 1], g_sum[:, g:g + 1], SUM_EPS, None, ALU.add))
                    order.wait()
                    order.step(vec.reciprocal(g_inv[:, g:g + 1], g_sum_e[:, g:g + 1]))

                def output(g):
                    h, t = g // TILES, g % TILES
                    vec.wait_ge(o_full, seen + g + 1)
                    order.wait()
                    if layer == 0:
                        vec.tensor_scalar(wide[:, t, h * GCOL:(h + 1) * GCOL], ps[:, 6 + g % 2, 0:GCOL], g_inv[:, g:g + 1], None, ALU.mult).then_inc(o_used, 1)
                    else:
                        vec.tensor_scalar(wide[:, t, 0:DIM].rearrange("p (c n) -> p c n", c=2), ps[:, 6:8, 0:WCOL], g_inv[:, g:g + 1], None,
                                          ALU.mult).then_inc(o_used, 1)

                vec.wait_ge(gat_in[layer], 64)
                for u in range(units):
                    for t in range(TILES):
                        xl_chunk(0, u, t)
                diagonal(0)
                for g in range(tiles + 4):
                    h, t = g // TILES, g % TILES
                    if 0 <= g - 3 < tiles:
                        weights_lo(g - 3)
                    if 0 <= g - 4 < tiles:
                        output(g - 4)
                    if g < tiles:
                        logits(g)
                    if 0 <= g - 1 < tiles:
                        weights(g - 1)
                    if h + 1 < heads:
                        xl_chunk(h + 1, 0, t)
                        if t == FULL:
                            diagonal(h + 1)
                rows = wide if layer == 0 else wide[:, :, 0:DIM]
                bias, gain = (row1["b"], row1["g"]) if layer == 0 else bias_row
                vec.wait_ge(o_used, seen + tiles)
                for t in range(TILES):
                    order.step(vec.tensor_tensor(rows[:, t, :], rows[:, t, :], bias[:, :], ALU.add))
                order.wait()
                normalise(LN_GAT[layer], rows, rows, ready=False, width=heads * width)
                if layer == 0:
                    vec.wait_ge(late_in[0], 32)
                    scale_shift(rows, gain, a_row[0], False)
                    order.wait()
                    for j in range(heads * TILES):
                        n = PR_SKIP[0] + j
                        c, t = j // TILES, j % TILES
                        mine = rows[:, t, c * GCOL:(c + 1) * GCOL]
                        vec.wait_ge(prod_full, n + 1)
                        vec.scalar_tensor_tensor(mine, mine, 0.0, ps[:, n % 8, 0:GCOL], ALU.max, ALU.add).then_inc(prod_used, 1)
                    vec.wait_ge(prod_used, PR_SKIP[0] + heads * TILES)
                    for t in range(TILES):
                        vec.tensor_tensor(rows[:, t, :], rows[:, t, :], a_row[1][:, :], ALU.add).then_inc(rows_ready, 1)
                    transposes_lo(TR_H1, GAT1 // P)
                else:
                    vec.wait_ge(late_in[1], 32)
                    scale_shift(rows, gain, a_row[0], False)
                    order.wait()
                    for t in range(TILES):
                        order.step(vec.tensor_tensor(rows[:, t, :], rows[:, t, :], a_row[1][:, :], ALU.add))
                    order.wait()
                    add_products(PR_SKIP[1], rows, units=units, cols=GCOL)
                    vec.wait_ge(prod_used, PR_SKIP[1] + units * TILES)
                    for t in range(TILES):
                        order.step(vec.tensor_tensor(X[:, t, :], X[:, t, :], rows[:, t, :], ALU.add))
                    order.wait()

            gat(0)
            end_phase(vec, "vec", 11)
            gat(1)
            end_phase(vec, "vec", 12)
            experts(1)
            end_phase(vec, "vec", 13)

        @block.tensor
        def _(pe):
            def transposes(start, src, ready=None, kd=KD):
                g = start
                for t in range(TILES):
                    if ready is not None:
                        pe.wait_ge(rows_ready, ready + t + 1)
                    for ks in groups_of(kd):
                        if g >= 8:
                            pe.wait_ge(tr_done, g - 7)
                        for k in ks:
                            ins = pe.transpose(ps[:, g % 8, (k - ks[0]) * P:(k - ks[0] + 1) * P], src[:, t, k * P:(k + 1) * P], ident[:, :])
                        ins.then_inc(tr_full, 1)
                        g += 1
                return g

            def products(start, first, act_of, kd=KD, units=2, cols=WCOL):
                g = start
                for c in range(units):
                    pe.wait_ge(unit_ready, first + c + 1)
                    w = unit_view((first + c) % 2, kd, cols)
                    for t in range(TILES):
                        if g >= 8:
                            pe.wait_ge(prod_used, g - 7)
                        for k in range(kd):
                            act_t, m = act_of(k)
                            ins = mm3(pe, ps[:, g % 8, 0:cols], at(act_t, slice(None), m, slice(t * P, (t + 1) * P)), at(w, slice(None), k),
                                      k == 0, k == kd - 1)
                        ins.then_inc(prod_full, 1)
                        g += 1
                    used()

            def used(n=1):
                pe.drain().then_inc(unit_used, n)

            pe.wait_ge(masks, 2)
            transposes(TR_0, XN, ROWS_0)
            pe.wait_ge(rf_in, 48)
            pe.wait_ge(tr_done, 10)
            for c in range(2):
                ins = pe.transpose(ps[:, 2, c * P:(c + 1) * P], rf2[:, c, :], ident[:, :])
            ins.then_inc(rf_full, 1)
            pe.wait_ge(sort_row, 1)
            pe.wait_ge(consts, 12)
            pe.matmul(ps[0:EDGE_ROWS, 0, 0:GROUPS], before[0:EDGE_ROWS, 0:EDGE_ROWS], in_row[:, :], start=True, stop=True).then_inc(sort_sum, 1)
            pe.matmul(ps[0:EDGE_ROWS, 1, 0:GROUPS], ones_f[0:EDGE_ROWS, 0:EDGE_ROWS], in_row[:, :], start=True, stop=True).then_inc(sort_sum, 1)
            pe.wait_ge(pos_ready, 1)
            end_phase(pe, "pe", 1)
            with pe.Fori(0, PAIRS) as j:
                pe.wait_ge(unit_ready, U_MIX + 2 * j + 1)
                w = [x[:, 0:KD * 2 * P].rearrange("p (s k o) -> p s k o", k=KD, s=2) for x in W[0]]
                for n in range(4):
                    pe.wait_ge(A_done, 12 * j + n + 1)
                    for k in range(KD):
                        ins = mm3(pe, ps[:, n, 0:HALF], at(w, slice(None), n // 2, k), at(XT, slice(None), k, cols_half(n)), k == 0, k == KD - 1)
                    ins.then_inc(A_full, 1)
                pe.wait_ge(unit_ready, U_MIX + 2 * j + 2)
                w = unit_view(1, KD, P)
                for n in range(2):
                    pe.wait_ge(B_done, 10 * j + n + 1)
                    for t in range(4 * n, min(4 * n + 4, TILES)):
                        for k in range(KD):
                            ins = mm3(pe, ps[:, 4 + n, (t - 4 * n) * P:(t - 4 * n + 1) * P], at(XT, slice(None), k, slice(t * P, (t + 1) * P)),
                                      at(w, slice(None), k), k == 0, k == KD - 1)
                    ins.then_inc(B_full, 1)
                used(2)
                for s in range(2):
                    rows = slice(s * HEAD0, (s + 1) * HEAD0)
                    pe.wait_ge(A_done, FREE_A + 12 * j + 4)
                    for n in range(3):
                        pe.wait_ge(B_done, 10 * j + 4 * s + n + 3)
                        for t in range(2 * n, min(2 * n + 2, TILES)):
                            ins = mm3(pe, ps[:, 4 + n % 2, (t - 2 * n) * FEATS:(t - 2 * n + 1) * FEATS], at(kT, rows, slice(t * P, (t + 1) * P)),
                                      at(rfT, rows), True, True)
                        ins.then_inc(B_full, 1)
                    for n in range(4):
                        pe.wait_ge(A_done, 12 * j + 4 * s + n + 5)
                        mm3(pe, ps[:, n, 0:HALF], at(rfT, rows, slice((n // 2) * P, (n // 2 + 1) * P)), at(qT, rows, cols_half(n)),
                            True, True).then_inc(A_full, 1)
                    pe.wait_ge(B_done, FREE_B + 10 * j + 4 * s + 5)
                    for m in range(2):
                        for t in range(TILES):
                            rows_of = LAST if t == FULL else P
                            ins = mm3(pe, ps[:, 5, m * HEAD0:(m + 1) * HEAD0], at(phi_k, slice(0, rows_of), t, slice(m * P, (m + 1) * P)),
                                      at(v, slice(0, rows_of), t, rows), t == 0, t == TILES - 1)
                    ins.then_inc(B_full, 1)
                    pe.wait_ge(B_done, FREE_B + 10 * j + 4 * s + 6)
                    pe.wait_ge(A_done, FREE_A + 12 * j + 4 * s + 8)
                    for n in range(2):
                        if s == 0:
                            pe.wait_ge(C_done, 2 * j + n + 1)
                        for m in range(2):
                            ins = mm3(pe, ps[:, 6 + n, 0:HALF], at(kv, slice(None), m, s), at(phi_qT, slice(None), m, cols_half(n)),
                                      s == 0 and m == 0, s == 1 and m == 1)
                        if s == 1:
                            ins.then_inc(C_full, 1)
            pe.wait_ge(C_done, FREE_C + 2 * PAIRS)
            products(PR_PROJ, U_PROJ, lambda k: (attnT, k))
            end_phase(pe, "pe", 2)
            pe.sem_inc(slot_full, FREE_HOT)
            with pe.Fori(0, SLOTS // 2) as i:
                for b in range(2):
                    pe.wait_ge(hot, 4 * i + 2 * b + 2)
                    for n in range(2):
                        for h in range(2):
                            ins = pe.matmul(ps[:, 2 * b + n, 0:HALF], src_hot[b][:, h, :], dst_hot[b][:, h, cols_half(n)], start=(h == 0), stop=(h == 1))
                    ins.then_inc(slot_full, 1)
            end_phase(pe, "pe", 3)
            products(PR_ROOT1, U_ROOT1, chunk_of)
            end_phase(pe, "pe", 4)
            for layer in range(2):
                if layer == 1:
                    transposes(TR_H, ACC, ROWS_H)
                    pe.wait_ge(tr_done, 4 * TILES)
                    products(PR_ROOT2, U_ROOT2, chunk_of)
                    end_phase(pe, "pe", 6)
                pe.sem_inc(agg_full[layer], FREE_BUF * AGGS)
                with pe.Fori(0, RELS // 2) as i:
                    for b in range(2):
                        pe.wait_ge(a_ready[layer], FREE_BUF + 2 * i + b + 1)
                        for n in range(2):
                            pe.wait_ge(cnt_used[layer], 4 * i + 2 * b + n + 1)
                            for t in range(TILES):
                                ins = pe.matmul(ps[:, 6 + n, 0:HALF], ones_r[:, :], A_r[b][:, t, cols_half(n)], start=(t == 0), stop=(t == TILES - 1))
                            ins.then_inc(cnt_full[layer], 1)
                        for n in range(AGGS):
                            pe.wait_ge(agg_val[layer], AGGS * (2 * i + b) + n + 1)
                            k = slice((n // 2) * P, (n // 2 + 1) * P)
                            for t in range(TILES):
                                for part in range(2):
                                    ins = pe.matmul(ps[:, n % 4, 0:HALF], xn[part][:, t, k], A_r[b][:, t, cols_half(n)],
                                                    start=(t == 0 and part == 0), stop=(t == FULL and part == 1))
                            ins.then_inc(agg_full[layer], 1)
                        pe.wait_ge(agg_done[layer], FREE_DONE + AGGS * (2 * i + b + 1))
                        for c in range(2):
                            pe.wait_ge(unit_ready, U_REL[layer] + 4 * i + 2 * b + c + 1)
                            w = unit_view(c, KD, WCOL)
                            for t in range(TILES):
                                n = c * TILES + t
                                pe.wait_ge(tra_used[layer], FREE_TRA - 2 + 2 * TILES * (2 * i + b) + n + 1)
                                for k in range(KD):
                                    ins = mm3(pe, ps[:, 4 + n % 2, 0:WCOL], at(XT, slice(None), k, slice(t * P, (t + 1) * P)), at(w, slice(None), k),
                                              k == 0, k == KD - 1)
                                ins.then_inc(tra_full[layer], 1)
                            used()
                end_phase(pe, "pe", (5, 7)[layer])

            def experts(n):
                transposes(TR_FFN[n], XE, ROWS_FFN[n])
                pe.wait_ge(tr_done, TR_FFN[n] + SET)
                pe.wait_ge(gate_in, 16 * (5 + 4 * n))
                for m, (count, width) in enumerate(IN_B[n]):
                    pe.transpose(ps[0:width, 3 + m, 0:EXPERTS * count], in_b_rows[m][0:EXPERTS * count, 0:width],
                                 ident[0:EXPERTS * count, 0:EXPERTS * count]).then_inc(in_b_full, 1)
                pe.wait_ge(gate_split, n + 1)
                for c in range(2):
                    for k in range(KD):
                        ins = mm3(pe, ps[0:EXPERTS, c, 0:HALF], at(gate_w, slice(None), k), at(XT, slice(None), k, cols_half(c)), k == 0, k == KD - 1)
                ins.then_inc(gate_full, 1)
                pe.wait_ge(scoresT_ready, n + 1)
                for t in range(TILES):
                    ins = pe.transpose(ps[:, 2, t * EXPERTS:(t + 1) * EXPERTS], scoresT[:, t * P:(t + 1) * P], ident[0:EXPERTS, 0:EXPERTS])
                ins.then_inc(gate_full, 1)
                pe.wait_ge(chosen_ready, n + 1)
                pe.wait_ge(masks, 3 + n)
                flat = is_chosen[:, :, :, :].rearrange("p t k e -> p (t k e)")
                per = CHOSEN * EXPERTS
                for bank, mask in ((1, before_e), (7, None)):
                    for rows, col in ((P, slice(0, FULL * per)), (LAST, slice(FULL * per, TILES * per))):
                        m = f32(ones_r[0:rows, :]) if mask is None else mask[0:rows, :]
                        ins = pe.matmul(ps[:, bank, col], m, flat[0:rows, col], start=True, stop=True)
                    ins.then_inc(rank_full, 1)
                pe.wait_ge(comb_ready, n + 1)
                for t in range(TILES):
                    ins = pe.transpose(ps[0:EXPERTS, 5 + t // 4, (t % 4) * P:(t % 4 + 1) * P], comb[:, t, :], ident[:, :])
                ins.then_inc(comb_full, 1)
                pe.wait_ge(combT_ready, 2 * (n + 1))
                pe.wait_ge(in_b_ready, 2 + n)
                for j in range(2 * TILES):
                    pe.wait_ge(prod_used, PR_FFN[n] + j - 7)
                    c, t = j // TILES, j % TILES
                    pe.matmul(ps[:, (PR_FFN[n] + j) % 8, 0:WCOL], combT[:, t * P:(t + 1) * P], out_b[:, wcols(c)], start=True, stop=True).then_inc(prod_full, 1)
                pe.wait_ge(prod_used, PR_FFN[n] + SET)
                steps, sizes = HIDDEN[n], FFN_UNITS[n]
                first_y, units, cols, ks, first_h = OUTPUT[n]

                def rows_t(i, b):
                    pe.wait_ge(slot_ready[n][b], 16 * i + 16)
                    for q in range(Q_T):
                        pe.wait_ge(t_lo[n], 3 * (2 * i + b) + q + 1)
                        for k in range(2):
                            for half in range(2):
                                ins = pe.transpose(ps[:, T_BANK + q, (2 * k + half) * P:(2 * k + half + 1) * P],
                                                   slot_in[b][:, half, (2 * q + k) * P:(2 * q + k + 1) * P], ident[:, :])
                        ins.then_inc(t_full[n], 1)

                def slot(i, b, last):
                    def weights(u):
                        pe.wait_ge(e_lo[n], RING + (2 * i + b) * len(sizes) + u + 1)
                        rows, k, width = sizes[u]
                        return unit_view((b * len(sizes) + u) % RING, k, width, rows)

                    pe.wait_ge(t_lo[n], FREE_T + 3 * (2 * i + b + 1))
                    before_u = -1
                    for g, (u, col, width, src, _, _) in enumerate(steps):
                        done = 2 * len(steps) * i + b * len(steps)
                        after = None
                        if u != before_u:
                            after = e_used[n] if u > 0 else None
                            w, before_u = weights(u), u
                        rows, k_of, _ = sizes[u]
                        pe.wait_ge(h_act[n], done + g + places_left(n, g))
                        full, _ = hidden_at(g, width)
                        for k in range(k_of):
                            m = at(XT, slice(None), k, slice(b * SLOT_ROWS, (b + 1) * SLOT_ROWS)) if src is None else at(hT, slice(0, rows), src + k)
                            if src is not None and u != steps[g - 1][0]:
                                pe.wait_ge(h_lo[n], FREE_LO + done + g - k_of + k + 1)
                            ins = mm3(pe, full, at(w, slice(None), k, slice(col, col + width)), m, k == 0, k == k_of - 1,
                                      after if k == 0 else None)
                        ins.then_inc(h_full[n], 1)
                        if u == ROWS_AFTER[n] and u != (steps + [(None,)])[g + 1][0] and not last:
                            rows_t(i + b, 1 - b)
                    for y in range(2 * units):
                        c, half = y // 2, y % 2
                        if half == 0:
                            w = weights(first_y + c)
                        pe.wait_ge(y_used[n], 2 * units * (2 * i + b) + y + 1)
                        for k in range(ks):
                            if y == 0:
                                pe.wait_ge(h_lo[n], FREE_LO + 2 * len(steps) * i + (b + 1) * len(steps) - ks + k + 1)
                            ins = mm3(pe, ps[:, 2 + half, 0:cols], at(hT, slice(None), first_h + k, slice(half * P, (half + 1) * P)),
                                      at(w, slice(None), k), k == 0, k == ks - 1, e_used[n] if k == 0 and half == 0 else None)
                        ins.then_inc(y_full[n], 1)
                    pe.drain().then_inc(e_used[n], 1)

                pe.sem_inc(e_used[n], RING)
                pe.sem_inc(t_full[n], FREE_IN)
                rows_t(0, 0)
                slot_pairs(pe, slot)

            experts(0)
            end_phase(pe, "pe", 8)

            transposes(TR_MIX_IN, XM, ROWS_MIX_IN)
            pe.wait_ge(tr_done, TR_MIX_IN + SET)
            for n, start in enumerate((PR_Q, PR_K, PR_V)):
                products(start, U_MIX1 + 2 * n, chunk_of)
            pe.wait_ge(prod_used, PR_V + SET)
            pe.wait_ge(kv_rows, TILES)
            for c in range(2):
                for t in range(TILES):
                    rows = LAST if t == FULL else P
                    ins = pe.matmul(ps[:, c, 0:WCOL], f32(ones_r[0:rows, :]), K[0:rows, t, wcols(c)], start=(t == 0), stop=(t == FULL))
                ins.then_inc(kv_full, 1)
            transposes(TR_MIX_OUT, Q, ROWS_MIX_OUT)
            pe.wait_ge(tr_done, TR_MIX_OUT + SET)
            products(PR_MIX1, U_MIX1 + 6, chunk_of)
            end_phase(pe, "pe", 9)
            transposes(TR_XN1, XN1)
            pe.wait_ge(c_added, RELS + FREE_BUF + TILES)
            pe.wait_ge(tr_done, TR_XN1 + SET)
            for d in range(TILES):
                if d >= 2:
                    pe.wait_ge(c_done, d - 1)
                for t in range(TILES):
                    ins = pe.transpose(ps[:, 2 * (d % 2) + t // FULL, (t % FULL) * P:(t % FULL + 1) * P], csum[:, t, d * P:(d + 1) * P], ident[:, :])
                ins.then_inc(c_full, 1)
            end_phase(pe, "pe", 10)

            def gat(layer):
                heads, units, kd = GAT[layer]
                tiles = heads * TILES
                heads_seen = layer * GHEADS
                seen = heads_seen * TILES
                XL, PT = ((XL1, PT1), (XL2, PT2))[layer]

                def xl_chunk(h, u, t):
                    n = (h * units + u) * TILES + t
                    unit = U_XL[layer] + h * units + u
                    if t == 0:
                        pe.wait_ge(unit_ready, unit + 1)
                    if n >= 2:
                        pe.wait_ge(xl_done, seen + n - 1)
                    w = unit_view(unit % 2, kd, GCOL)
                    for k in range(kd):
                        act_t, m = chunk_of(k)
                        ins = mm3(pe, ps[:, n % 2, 0:GCOL], at(act_t, slice(None), m, slice(t * P, (t + 1) * P)), at(w, slice(None), k), k == 0, k == kd - 1)
                    ins.then_inc(xl_full, 1)
                    if t == FULL:
                        used()

                def source_row(h):
                    pe.wait_ge(diag_ready, seen + (h + 1) * TILES)
                    if h > 0:
                        pe.wait_ge(e_ready, seen + h * TILES)
                    for c in range(2):
                        ins = pe.matmul(ps[:, 2 + c, 0:HALF], f32(ones_r[:, :]), diag[layer][:, cols_half(c)], start=True, stop=True)
                    ins.then_inc(row_full, 1)

                def weights_t(g):
                    pe.wait_ge(p_ready, seen + g + 1)
                    if g > 0:
                        pe.wait_ge(pt_done, seen + g)
                    for t in range(TILES):
                        ins = pe.transpose(ps[:, 4 + t // FULL, (t % FULL) * P:(t % FULL + 1) * P], g_p[g % 2][:, t * P:(t + 1) * P], ident[:, :])
                    ins.then_inc(pt_full, 1)

                def output(g):
                    h = g // TILES
                    pe.wait_ge(pt_done, seen + g + 1)
                    ring = (2, 1)[layer]
                    if g >= ring:
                        pe.wait_ge(o_used, seen + g - ring + 1)
                    cols = (GCOL, WCOL)[layer]
                    for c in range(units * GCOL // cols):
                        for t in range(TILES):
                            ins = mm3(pe, ps[:, 6 + (g % 2 if layer == 0 else c), 0:cols], at(PT[g % len(PT)], slice(None), t),
                                      at(XL[h % len(XL)], slice(None), t, slice(c * cols, (c + 1) * cols)), t == 0, t == FULL)
                    ins.then_inc(o_full, 1)

                for u in range(units):
                    for t in range(TILES):
                        xl_chunk(0, u, t)
                source_row(0)
                for g in range(tiles + 3):
                    h, t = g // TILES, g % TILES
                    if h + 1 < heads:
                        xl_chunk(h + 1, 0, t)
                    if 0 <= g - 2 < tiles:
                        weights_t(g - 2)
                    if 0 <= g - 3 < tiles:
                        output(g - 3)
                    if h + 1 < heads and t == FULL:
                        source_row(h + 1)
                pe.wait_ge(o_used, seen + tiles)
                products(PR_SKIP[layer], U_SKIP[layer], chunk_of, kd, (heads, units)[layer], GCOL)
                if layer == 0:
                    pe.wait_ge(prod_used, PR_SKIP[0] + heads * TILES)
                    transposes(TR_H1, wide, ROWS_H1, GAT1 // P)
                    pe.wait_ge(tr_done, TR_H1 + 3 * TILES)

            gat(0)
            end_phase(pe, "pe", 11)
            gat(1)
            end_phase(pe, "pe", 12)
            experts(1)
            end_phase(pe, "pe", 13)


_INPUTS = ['x', 'src', 'dst', 'edge_type_8', 'L0_gnn_W1', 'L0_gnn_root1', 'L0_gnn_b1', 'L0_gnn_W2', 'L0_gnn_root2', 'L0_gnn_b2',
           'L0_mix_W_qkv', 'L0_mix_b_qkv', 'L0_mix_W_proj', 'L0_mix_b_proj', 'L0_mix_random_features',
           'L0_ffn_Wg', 'L0_ffn_bg', 'L0_ffn_W1', 'L0_ffn_b1', 'L0_ffn_W2', 'L0_ffn_b2', 'L0_ffn_W3', 'L0_ffn_b3',
           'L1_gnn_W1', 'L1_gnn_a_src1', 'L1_gnn_a_dst1', 'L1_gnn_b1', 'L1_gnn_g1', 'L1_gnn_be1', 'L1_gnn_Wr1', 'L1_gnn_br1',
           'L1_gnn_W2', 'L1_gnn_a_src2', 'L1_gnn_a_dst2', 'L1_gnn_b2', 'L1_gnn_g2', 'L1_gnn_be2', 'L1_gnn_Wr2', 'L1_gnn_br2',
           'L1_mix_w_qkv', 'L1_mix_w_proj', 'L1_mix_ln_in_g', 'L1_mix_ln_in_b', 'L1_mix_ln_out_g', 'L1_mix_ln_out_b',
           'L1_ffn_router_w', 'L1_ffn_router_b', 'L1_ffn_w1', 'L1_ffn_b1', 'L1_ffn_w2', 'L1_ffn_b2']


def kernel(**inputs):
    import numpy as np
    import concourse.bacc as bacc
    from concourse.bass_utils import run_bass_kernel_spmd

    nc = bacc.Bacc("TRN2", target_bir_lowering=False, num_devices=1)
    arrays, views = {}, {}
    for name in _INPUTS:
        arrays[name + "_in"] = np.ascontiguousarray(inputs[name])
        views[name] = nc.dram_tensor(name + "_in", arrays[name + "_in"].shape, mybir.dt.from_np(arrays[name + "_in"].dtype), kind="ExternalInput").ap()
    result = nc.dram_tensor("rows_out", (NODES, DIM), F32, kind="ExternalOutput").ap()
    build(nc, views, result)
    got = run_bass_kernel_spmd(nc, [arrays], core_ids=[0])
    return got.results[0]["rows_out"]
```

```python
from contextlib import ExitStack

import concourse.bass as bass
from concourse import mybir

F32 = mybir.dt.float32
F32R = mybir.dt.float32r
I32 = mybir.dt.int32
I16 = mybir.dt.int16
U16 = mybir.dt.uint16
U32 = mybir.dt.uint32
BF16 = mybir.dt.bfloat16
ALU = mybir.AluOpType
ACT = mybir.ActivationFunctionType
AX = mybir.AxisListType
ds = bass.ds

P = 128
NODES = 625
TILES = 5
FULL = TILES - 1
LAST = NODES - FULL * P
COLS = TILES * P
HALF = COLS // 2
EDGES = 10000
EDGE_ROWS = 125
EDGE_COLS = EDGES // EDGE_ROWS
RELS = 8
DIM = 768
KD = DIM // P
WCOL = 384
UNIT = KD * WCOL
BANK = 512
EPS = 1e-5

GROUPS = RELS * TILES
SLOT = 2 * P
HOTS = 4
SLOTS = -(-((EDGES + GROUPS * (SLOT - 1)) // SLOT) // HOTS) * HOTS
SUBS = 2 * SLOTS

HEADS0, HEAD0 = 12, 64
PAIRS = HEADS0 // 2
FEATS = 256
MIX0_SCALE = (HEAD0 ** -0.5) ** 2 / FEATS

EXPERTS = 8
HID0 = 192
HC0, HP0 = 2, HID0 // 2
HID0B = 2 * HID0
HB0 = HID0B // P
HID1 = 1152
HC1 = HID1 // P
YCOL1 = 256
BELOW = -3e38
SLOT_ROWS = 2 * P
CHOSEN = 2
MORE = NODES * CHOSEN // (SLOT_ROWS + 1)
XSLOTS = EXPERTS + MORE
CHOICES = TILES * CHOSEN
RING = 4
GHEADS, GCOL = 4, 256
GAT1 = GHEADS * GCOL
NORM_EPS = 1e-12
SUM_EPS = 1e-16
SLOPE = 0.2
NO_EDGE = -1e30


class Unit:

    def __init__(self, first, i=0, per=0):
        self.n = first + per * i
        self.slot = first % 2
        self.loads = 16 * (first // 2 + 1) + 8 * per * i


class Order:

    def __init__(self, eng, sem):
        self.eng, self.sem, self.before, self.n = eng, sem, 0, 0

    def step(self, ins):
        ins.then_inc(self.sem, 1)
        self.n += 1

    def wait(self):
        self.eng.wait_ge(self.sem, self.before + self.n)

    def enter(self, i, per):
        self.start, self.per = self.before + self.n, per
        self.before, self.n = self.start + per * i, 0

    def leave(self, times):
        assert self.n == self.per, (self.n, self.per)
        self.before, self.n = self.start + self.per * times, 0


def build(nc, a, out):
    with ExitStack() as ctx:
        def dram(name, shape, dt):
            return nc.dram_tensor(name, shape, dt, kind="Internal").ap()

        def sem(name):
            return ctx.enter_context(nc.semaphore(name))

        def sems(name, n):
            return [sem(f"{name}{k}") for k in range(n)]

        def allocator(stack):
            def one(name, shape, dt):
                return stack.enter_context(nc.sbuf_tensor(name, shape, dt))

            def pair(name, shape):
                return one(name + "_hi", shape, F32R), one(name + "_lo", shape, F32R)

            return one, pair

        sorted_dram = dram("edges_sorted", (P * SUBS, 1), I32)
        slot_rows_dram = dram("slot_rows", (XSLOTS * SLOT_ROWS, DIM), F32)
        slot_out_dram = [dram(f"slot_out{n}", (XSLOTS * SLOT_ROWS, DIM), F32) for n in range(2)]
        count_dram = dram("counts", (P, TILES * COLS), U16)
        adj_dram = dram("adjacency", (RELS, P, TILES * COLS), U16)

        keep, keep2 = allocator(ctx)
        X = keep("x_rows", [P, TILES, DIM], F32)
        XT = keep2("xt", [P, KD, COLS])
        raw = [keep(f"weight_raw{s}", [P, UNIT], F32) for s in range(2)]
        W = [keep2(f"weight{s}", [P, UNIT]) for s in range(2)]
        ident = keep("ident", [P, P], F32)
        ones_r = keep("ones_r", [P, P], F32R)
        zero_col = keep("zero_col", [P, 1], F32)
        eps_col = keep("eps_col", [P, 1], F32)
        warm = keep("sqrt_warm", [P, 8], F32)
        stats = keep("stats", [P, TILES, 2, 6], F32)
        mv = keep("mean_var", [P, TILES, 2], F32)
        std = keep("std", [P, TILES], F32)
        rstd = keep("rstd", [P, TILES], F32)
        bias_rows = keep("bias_rows", [P, 2, DIM], F32)
        bias_row = [bias_rows[:, s, :] for s in range(2)]
        ps = ctx.enter_context(nc.psum_tensor("banks", [P, 8, BANK], F32))

        early = ExitStack()
        er, er2 = allocator(early)
        XN = er("xn_rows", [P, TILES, DIM], F32)
        rf2 = er("rf2", [P, 2, P], F32)
        rfT = er2("rfT", [P, 2, FEATS])
        qk_bias = er("qk_bias", [P, 2 * KD], F32)
        sorted_sb = er("sorted_sb", [P, SUBS], I32)
        part_i = er("part_i", [P, SUBS], I32)
        srcl_f = er("srcl_f", [P, SUBS], F32)
        dst_f = er("dst_f", [P, SUBS], F32)
        dst_iota = er("dst_iota", [P, COLS], I16)
        slot_group = er("slot_group", [1, SLOTS], I32)
        zero_row = er("zero_row", [P, DIM], F32)
        pos_i = er("pos_i", [EDGE_ROWS, EDGE_COLS], I32)
        code_i = er("code_i", [EDGE_ROWS, EDGE_COLS], I32)
        with ExitStack() as here:
            srt, _ = allocator(here)
            src_i = srt("src_i", [EDGE_ROWS, EDGE_COLS], I32)
            dst_i = srt("dst_i", [EDGE_ROWS, EDGE_COLS], I32)
            typ_i = srt("typ_i", [EDGE_ROWS, EDGE_COLS], I32)
            tile_i = srt("tile_i", [EDGE_ROWS, EDGE_COLS], I32)
            low_i = srt("low_i", [EDGE_ROWS, EDGE_COLS], I32)
            sub_i = srt("sub_i", [EDGE_ROWS, EDGE_COLS], I32)
            spot_i = srt("spot_i", [EDGE_ROWS, EDGE_COLS], I32)
            group_f = srt("group_f", [EDGE_ROWS, EDGE_COLS], F32)
            pos_f = srt("pos_f", [EDGE_ROWS, EDGE_COLS], F32)
            iota_g = srt("iota_g", [EDGE_ROWS, GROUPS], F32)
            iota_s = srt("iota_s", [1, SLOTS], F32)
            onehot_g = srt("onehot_g", [EDGE_ROWS, GROUPS, EDGE_COLS], F32)
            restart = srt("restart", [EDGE_ROWS, GROUPS, EDGE_COLS], F32)
            rank = srt("rank", [EDGE_ROWS, GROUPS, EDGE_COLS], F32)
            in_row = srt("in_row", [EDGE_ROWS, GROUPS], F32)
            before = srt("before", [P, P], F32)
            ones_f = srt("ones_f", [P, P], F32)
            ones_g = srt("ones_g", [EDGE_ROWS, GROUPS], F32)
            need_i = srt("need_i", [EDGE_ROWS, GROUPS], I32)
            need_s = srt("need_s", [EDGE_ROWS, GROUPS], I32)
            need_f = srt("need_f", [EDGE_ROWS, GROUPS], F32)
            slot_end = srt("slot_end", [EDGE_ROWS, GROUPS], F32)
            slot_base = srt("slot_base", [EDGE_ROWS, GROUPS], F32)
            offset_g = srt("offset_g", [EDGE_ROWS, GROUPS], F32)
            past = srt("past", [1, SLOTS, GROUPS], F32)
            group_of = srt("group_of", [1, SLOTS], F32)
            fill_i = srt("fill_i", [P, SUBS], I32)
        with ExitStack() as here:
            mx, mx2 = allocator(here)
            attnT = mx2("attnT", [P, KD, COLS])
            qT = mx2("qT", [P, COLS])
            kT = mx2("kT", [P, COLS])
            v_f = [mx(f"v_f{s}", [P, WCOL], F32) for s in range(2)]
            phi_k = mx2("phi_k", [P, TILES, FEATS])
            phi_qT = mx2("phi_qT", [P, 2, COLS])
            kv = mx2("kv", [P, 2, 2, P])
        with ExitStack() as here:
            aj, _ = allocator(here)
            adj = aj("adj", [P, GROUPS, COLS], U16)
            src_hot = [aj(f"src_hot{s}", [P, 2, P], BF16) for s in range(HOTS)]
            dst_hot = [aj(f"dst_hot{s}", [P, 2, COLS], BF16) for s in range(HOTS)]
            apart = [aj(f"apart{s}", [P, COLS], F32) for s in range(2)]
        early.close()
        with ExitStack() as here:
            rg, rg2 = allocator(here)
            A_r = [rg(f"a_rel{s}", [P, TILES, COLS], F32R) for s in range(2)]
            xn = rg2("xn", [P, TILES, DIM])
            A_u = [rg(f"a_stage{s}", [P, TILES, COLS], U16) for s in range(2)]
            cnt_m = rg("cnt_m", [P, 2, HALF], F32)
            inv = [rg(f"inv{s}", [P, 2, HALF], F32) for s in range(2)]
            agg_f = [rg(f"agg_f{s}", [P, HALF], F32) for s in range(3)]
            ACC = rg("acc_rows", [P, TILES, DIM], F32)
            counts = rg("counts_all", [P, TILES, COLS], U16)

        late = ExitStack()
        lt, lt2 = allocator(late)
        wide = lt("wide_rows", [P, TILES, GAT1], F32)
        XN1 = wide[:, :, 0:DIM]
        count = lt("count", [P, TILES, COLS], U16)
        absent = lt("absent", [P, TILES, COLS], BF16)
        with ExitStack() as here:
            ma, _ = allocator(here)
            Q, K, V = [ma(n, [P, TILES, DIM], F32) for n in ("q_rows", "k_rows", "v_rows")]
            XM = Q
            in_gain, in_shift = bias_row
            out_gain, out_shift, square = [ma(n, [P, DIM], F32) for n in ("out_gain", "out_shift", "square")]
            csum = ma("csum", [P, TILES, COLS], F32)
            norm = ma("norm", [P, 2, TILES], F32)
            norm_m = ma("norm_m", [P, 2, TILES], F32)
            inv_norm = ma("inv_norm", [P, 2, TILES], F32)
        g_e = [lt(f"att_logit{s}", [P, COLS], F32) for s in range(2)]
        g_p = [lt(f"att_p{s}", [P, COLS], F32) for s in range(2)]
        g_neg = lt("att_neg", [P, 2], F32)
        g_sum = lt("att_sum", [P, 4 * TILES], F32)
        g_sum_e = lt("att_sum_e", [P, 4 * TILES], F32)
        g_inv = lt("att_inv", [P, 4 * TILES], F32)
        junk = [lt(f"junk{s}", [P, GCOL], F32) for s in range(2)]
        part_of = [lt(f"alpha_part{k}", [P, TILES, 3], F32) for k in range(2)]
        alpha = [[lt(f"alpha{k}_{s}", [P, TILES], F32) for s in range(2)] for k in range(2)]
        with ExitStack() as here:
            g1, g12 = allocator(here)
            PT1 = [g12(f"attT{s}", [P, TILES, P]) for s in range(2)]
            XL1 = [g12(f"xl_head{s}", [P, TILES, GCOL]) for s in range(3)]
            a_row1 = [g1(f"a_row1_{k}", [P, GAT1], F32) for k in range(2)]
            row1 = {n: g1(n + "1_row", [P, GAT1], F32) for n in ("b", "g")}
        with ExitStack() as here:
            g2, g22 = allocator(here)
            XT_more = g22("xt_more", [P, GAT1 // P - KD, COLS])
            PT2 = [g22("att2T", [P, TILES, P])]
            XL2 = [g22("xl2", [P, TILES, DIM])]
            a_row2 = [g2(f"a_row2_{k}", [P, DIM], F32) for k in range(2)]
            diag = [bias_row[0][:, 0:COLS], g2("diag", [P, COLS], F32)]
        late.close()
        with ExitStack() as here:
            fe, fe2 = allocator(here)
            raw_more = [fe(f"weight_raw{s}", [P, UNIT], F32) for s in range(2, RING)]
            W_more = [fe2(f"weight{s}", [P, UNIT]) for s in range(2, RING)]
            gate_w = fe2("gate_w", [P, KD, EXPERTS])
            gate_b = fe("gate_b", [EXPERTS, 1], F32)
            iota_e = fe("iota_e", [P, EXPERTS], F32)
            scores = fe("scores", [P, TILES, EXPERTS], F32)
            choice = fe("choice", [P, TILES, EXPERTS], F32)
            others = fe("others", [P, TILES, EXPERTS], F32)
            top = [fe(f"top{k}", [P, TILES, 8], F32) for k in range(CHOSEN)]
            top_at = [fe(f"top_at{k}", [P, TILES, 8], U32) for k in range(CHOSEN)]
            chosen = fe("chosen", [P, TILES, CHOSEN], F32)
            is_chosen = fe("is_chosen", [P, TILES, CHOSEN, EXPERTS], F32)
            diff = fe("diff", [P, TILES, EXPERTS], F32)
            expo = fe("expo", [P, TILES, EXPERTS], F32)
            total = fe("total", [P, TILES], F32)
            share = fe("share", [P, TILES], F32)
            comb = fe("comb", [P, TILES, EXPERTS], F32)
            gate_of = fe("gate_of", [P, TILES, CHOSEN, EXPERTS], F32)
            gate = fe("gate", [P, TILES, CHOSEN], F32)
            before_e = fe("before_e", [P, P], F32)
            restart_e = fe("restart_e", [P, EXPERTS, CHOICES], F32)
            ones_e = fe("ones_e", [P, EXPERTS], F32)
            in_tile = fe("in_tile", [P, EXPERTS, CHOICES], F32)
            through = fe("through", [P, EXPERTS, CHOICES], F32)
            rank_of = fe("rank_of", [P, CHOICES, EXPERTS], F32)
            rank_e = fe("rank_e", [P, CHOICES], F32)
            need_e = fe("need_e", [P, EXPERTS], I32)
            need_es = fe("need_es", [P, EXPERTS], I32)
            more = fe("more", [P, EXPERTS], F32)
            more_end = fe("more_end", [P, EXPERTS], F32)
            more_at = fe("more_at", [P, EXPERTS], F32)
            more_of = fe("more_of", [P, CHOICES, EXPERTS], F32)
            spill = fe("spill", [P, CHOICES], F32)
            is_more = fe("is_more", [P, CHOICES], F32)
            first_at = fe("first_at", [P, CHOICES], F32)
            place_f = fe("place_f", [P, CHOICES], F32)
            place = fe("place", [P, CHOICES], I32)
            past_e = fe("past_e", [1, MORE, EXPERTS], F32)
            slot_expert_f = fe("slot_expert_f", [1, XSLOTS], F32)
            slot_expert = fe("slot_expert", [1, XSLOTS], I32)
            iota_m = fe("iota_m", [1, MORE], F32)
            in_b = [fe(f"in_b{m}", [P, EXPERTS * HC1], F32) for m in range(2)]
            slot_in = [fe(f"slot_in{s}", [P, 2, DIM], F32) for s in range(2)]
            h_f = [fe(f"h_f{s}", [P, SLOT_ROWS], F32) for s in range(3)]
            with ExitStack() as first:
                start = allocator(first)[0]
                scoresT = start("scoresT", [EXPERTS, COLS], F32)
                combT = scoresT
                gate_raw = start("gate_raw", [P, KD, EXPERTS], F32)
                in_b_rows = [start(f"in_b_rows{m}", [P, P], F32) for m in range(2)]
            y_rows = [bias_rows, fe("y_rows", [P, 2, DIM], F32)]
            with ExitStack() as first:
                XE = allocator(first)[0]("xe_rows", [P, TILES, DIM], F32)
                out_b = allocator(first)[0]("out_b", [EXPERTS, DIM], F32)
            hT = fe2("hT", [P, HC1, SLOT_ROWS])

        raw_ready = sems("raw_ready", 2)
        hi_ready = sem("hi_ready")
        unit_ready = sem("unit_ready")
        unit_used = sem("unit_used")
        x_in, edges_in, rf_in = sem("x_in"), sem("edges_in"), sem("rf_in")
        bias_in = sem("bias_in")
        pad_zero, consts, masks = sem("pad_zero"), sem("consts"), sem("masks")
        vec_order = sem("vec_order")
        ln_var = sem("ln_var")
        ln_std = sem("ln_std")
        rows_ready = sem("rows_ready")
        tr_full = sem("tr_full")
        tr_hi = sem("tr_hi")
        tr_done = sem("tr_done")
        prod_full = sem("prod_full")
        prod_used = sem("prod_used")
        sort_row = sem("sort_row")
        sort_sum = sem("sort_sum")
        pos_ready = sem("pos_ready")
        filled = sem("filled")
        scattered = sem("scattered")
        sorted_in = sem("sorted_in")
        rf_full, rf_hi = sem("rf_full"), sem("rf_hi")
        A_full, A_hi, A_done = sem("mixA_full"), sem("mixA_hi"), sem("mixA_done")
        B_full, B_hi, B_done = sem("mixB_full"), sem("mixB_hi"), sem("mixB_done")
        v_hi, v_lo = sem("v_hi"), sem("v_lo")
        C_full, C_hi, C_done = sem("mixC_full"), sem("mixC_hi"), sem("mixC_done")
        adj_zero = sem("adj_zero")
        dst_ready = sem("dst_ready")
        hot = sem("hot")
        apart_ready = sem("apart_ready")
        hot_b = sem("hot_b")
        slot_full = sem("slot_full")
        slot_done = sem("slot_done")
        adj_out = sem("adj_out")
        rows_hi = sem("rows_hi")
        rows_lo = sem("rows_lo")
        a_in = [sems(f"a_in{layer}_", 2) for layer in range(2)]
        a_ready = sem("a_ready")
        cnt_full, cnt_used = sem("cnt_full"), sem("cnt_used")
        agg_full, agg_val, agg_hi, agg_done = sem("agg_full"), sem("agg_val"), sem("agg_hi"), sem("agg_done")
        tra_full, tra_used = sem("tra_full"), sem("tra_used")
        ends = {e: sem(f"{e}_end") for e in ("pe", "act", "vec")}
        gate_in = sem("gate_in")
        gate_split = sem("gate_split")
        gate_full = sem("gate_full")
        scoresT_ready = sem("scoresT_ready")
        gate_arg = sem("gate_arg")
        gate_exp = sem("gate_exp")
        comb_ready = sem("comb_ready")
        comb_full = sem("comb_full")
        combT_ready = sem("combT_ready")
        in_b_full = sem("in_b_full")
        in_b_ready = sem("in_b_ready")
        cleared = sem("cleared")
        chosen_ready = sem("chosen_ready")
        rank_full = sem("rank_full")
        placed = sem("placed")
        sent = sem("sent")
        slot_ready = [sems(f"slot_ready{n}_", 2) for n in range(2)]
        t_full = sems("t_full", 2)
        t_hi = sems("t_hi", 2)
        t_lo = sems("t_lo", 2)
        eraw_ready = [sems(f"eraw_ready{n}_", RING) for n in range(2)]
        e_hi = sems("e_hi", 2)
        e_lo = sems("e_lo", 2)
        e_used = sems("e_used", 2)
        h_full = sems("h_full", 2)
        h_act = sems("h_act", 2)
        h_lo = sems("h_lo", 2)
        y_full = sems("y_full", 2)
        y_used = sems("y_used", 2)
        y_out = [sems(f"y_out{n}_", 2) for n in range(2)]
        back = sems("back", TILES)
        mix_in, kv_rows, kv_full, norm_done = sem("mix_in"), sem("kv_rows"), sem("kv_full"), sem("norm_done")
        c_added = sem("c_added")
        c_out, c_in = sem("c_out"), sem("c_in")
        c_ready = sem("c_ready")
        c_full, c_done = sem("c_full"), sem("c_done")
        rows_done = sem("rows_done")
        logit_ready = sem("logit_ready")
        gat_in = sems("gat_in", 2)
        late_in = sems("late_in", 2)
        xl_full = sem("xl_full")
        xl_hi = sem("xl_hi")
        xl_done = sem("xl_done")
        diag_ready = sem("diag_ready")
        row_full = sem("row_full")
        e_ready = sem("e_ready")
        e_exp = sem("e_exp")
        p_ready = sem("p_ready")
        inv_ready = sem("inv_ready")
        pt_full = sem("pt_full")
        pt_hi = sem("pt_hi")
        pt_done = sem("pt_done")
        o_full = sem("o_full")
        o_used = sem("o_used")
        stored = sem("stored")

        U_V = 0
        U_MIX = U_V + 2
        U_PROJ = U_MIX + 2 * PAIRS
        U_ROOT1 = U_PROJ + 2
        U_REL = [U_ROOT1 + 2, U_ROOT1 + 2 + 2 * RELS + 2]
        U_ROOT2 = U_REL[1] - 2
        U_FFN0 = U_REL[1] + 2 * RELS
        U_MIX1 = U_FFN0
        U_XL = [U_MIX1 + 8, U_MIX1 + 8 + 2 * GHEADS]
        U_SKIP = [U_XL[0] + GHEADS, U_XL[1] + DIM // GCOL]

        FFN_UNITS = [[(P, KD, HID0), (HP0, HC0, HID0B), (P, HB0, WCOL), (P, HB0, WCOL)],
                     [(P, KD, WCOL)] * 3 + [(P, HC1, YCOL1)] * 3]
        HIDDEN = [[(0, c * HP0, HP0, None, c, 0) for c in range(HC0)] + [(1, c * P, P, 0, HC0 + c, 1) for c in range(HB0)],
                  [(c // 3, c % 3 * P, P, None, c, 0) for c in range(HC1)]]
        OUTPUT = [(2, 2, WCOL, HB0, HC0), (3, 3, YCOL1, HC1, 0)]
        ROWS_AFTER = [0, 2]
        IN_B = [[(HC0, HP0), (HB0, P)], [(HC1, P)]]
        Q_T = KD // 2
        T_BANK = 5
        H_BANKS = (0, 1, 4)
        FREE_H = FREE_LO = len(H_BANKS)
        FREE_Y, FREE_T, FREE_IN = 2, Q_T, 2 * Q_T
        AHEAD = RING - 1
        SPLITS = [XSLOTS * len(u) for u in FFN_UNITS]
        RAW4, W4 = raw + raw_more, W + W_more
        out_rows = [x[:, :, :].rearrange("p k c -> p (k c)").bitcast(F32).rearrange("p (t d) -> p t d", t=TILES) for x in XT]
        LN_FFN, LN_IN1, LN_MIX_IN, LN_MIX_OUT, LN_GAT = [1, 7], 2, 3, 4, [5, 6]
        ROWS_0, ROWS_H, ROWS_FFN, ROWS_MIX_IN, ROWS_MIX_OUT, ROWS_H1 = 0, TILES, [2 * TILES, 6 * TILES], 3 * TILES, 4 * TILES, 5 * TILES
        EARLY = 3
        RF_BANK, SORT_BANK = 5, 6
        SET = 2 * TILES
        TR_0, TR_H, TR_MIX_IN, TR_MIX_OUT, TR_XN1, TR_H1 = 0, SET, 3 * SET, 4 * SET, 5 * SET, 6 * SET
        TR_FFN = [2 * SET, TR_H1 + 3 * TILES]
        PR_V0, PR_PROJ, PR_ROOT1, PR_ROOT2, PR_Q, PR_K, PR_V, PR_MIX1 = 0, SET, 2 * SET, 3 * SET, 5 * SET, 6 * SET, 7 * SET, 8 * SET
        PR_SKIP = [9 * SET, 9 * SET + GHEADS * TILES]
        PR_FFN = [4 * SET, PR_SKIP[1] + DIM // GCOL * TILES]
        GAT = [(GHEADS, 1, KD), (1, DIM // GCOL, GAT1 // P)]

        FREE_A, FREE_B, FREE_C = 4, 2, 2
        FREE_AGG, FREE_TRA, FREE_CNT = 4, 2 * TILES, 2
        AGGS = 2 * KD
        FREE_BUF = 2
        FREE_DONE = 3
        FREE_SUM = HOTS

        def mm3(pe, dst, s, m, start, stop, after=None):
            ins = pe.matmul(dst, s[0], m[0], start=start, stop=False)
            if after is not None:
                ins.then_inc(after, 1)
            pe.matmul(dst, s[0], m[1], start=False, stop=False)
            return pe.matmul(dst, s[1], m[0], start=False, stop=stop)

        def at(pair, *idx):
            return pair[0][idx], pair[1][idx]

        def unit_view(slot, k, n, rows=P):
            return [w[0:rows, 0:k * n].rearrange("p (k n) -> p k n", k=k) for w in W4[slot]]

        def chunks(w):
            return w.rearrange("(k p) o -> p k o", p=P)

        def words(counts):
            return counts.rearrange("p g c -> p (g c)").bitcast(U32)

        def f32(ap):
            return ap.bitcast(F32)

        def end_phase(eng, me, n):
            eng.drain().then_inc(ends[me], 1)
            for e in ends:
                if e != me:
                    eng.wait_ge(ends[e], n)

        def after_phase(eng, n):
            for e in ends:
                eng.wait_ge(ends[e], n)

        def groups_of(kd):
            return [range(c, min(c + 3, kd)) for c in range(0, kd, 3)]

        def chunk_of(g):
            return (XT, g) if g < KD else (XT_more, g - KD)

        def hidden_at(g, width):
            s = g % len(H_BANKS)
            return ps[0:width, H_BANKS[s], 0:SLOT_ROWS], h_f[s][0:width, :]

        def places_left(n, g):
            return 1 if g + len(HIDDEN[n]) % len(H_BANKS) >= len(H_BANKS) or len(HIDDEN[n]) % len(H_BANKS) == 0 else 2

        def slot_at(base, i, b):
            return base[ds((2 * i + b) * SLOT_ROWS, SLOT_ROWS), :].rearrange("(h p) d -> p h d", p=P)

        def slot_pairs(eng, body):
            with eng.Fori(0, XSLOTS // 2 - 1) as i:
                for b in range(2):
                    body(i, b, False)
            for b in range(2):
                body(XSLOTS // 2 - 1, b, b == 1)

        def cols_half(n):
            return slice((n % 2) * HALF, (n % 2 + 1) * HALF)

        def halves(ap):
            return ap.rearrange("p (h n) -> p h n", h=2)

        def wcols(c):
            return slice(c * WCOL, (c + 1) * WCOL)

        block = ctx.enter_context(nc.Block())

        @block.sync
        def _(sp):
            def load(u, src):
                if not (isinstance(u.n, int) and u.n < 2):
                    sp.wait_ge(unit_ready, u.n - 1)
                rows, k, n = src.shape
                dst = raw[u.slot][0:rows, 0:k * n].rearrange("p (k n) -> p k n", k=k)
                sp.dma_start(dst, src).then_inc(raw_ready[u.slot], 16)

            def store():
                for t in range(TILES):
                    rows = LAST if t == FULL else P
                    sp.wait_ge(rows_done, t + 1)
                    sp.dma_start(out[t * P:t * P + rows, :], X[0:rows, t, :]).then_inc(stored, 16)
                sp.wait_ge(stored, 16 * TILES)

            x = a["x"]
            sp.dma_start(X[:, 0:FULL, :], x[0:FULL * P, :].rearrange("(t p) d -> p t d", p=P)).then_inc(x_in, 16)
            sp.wait_ge(pad_zero, 1)
            sp.dma_start(X[0:LAST, FULL, :], x[FULL * P:NODES, :]).then_inc(x_in, 16)
            for t, n in ((src_i, "src"), (dst_i, "dst"), (typ_i, "edge_type_8")):
                sp.dma_start(t[:, :], a[n].rearrange("(p c) -> p c", p=EDGE_ROWS)).then_inc(edges_in, 16)
            qkv = a["L0_mix_W_qkv"].rearrange("(k p) (s o) -> p k s o", p=P, s=3)
            for c in range(2):
                load(Unit(U_V + c), qkv[:, :, 2, wcols(c)])
            with sp.Fori(0, PAIRS) as j:
                for c in range(2):
                    load(Unit(U_MIX + c, j, 2), qkv[:, :, c, ds(j * P, P)])
            sp.wait_ge(scattered, 16 * EDGE_COLS)
            sp.dma_start(sorted_sb[:, :], sorted_dram.rearrange("(p c) o -> p (c o)", p=P)).then_inc(sorted_in, 16)
            for first, name in ((U_PROJ, "L0_mix_W_proj"), (U_ROOT1, "L0_gnn_root1")):
                for c in range(2):
                    load(Unit(first + c), chunks(a[name])[:, :, wcols(c)])
            sp.wait_ge(slot_done, FREE_SUM + SLOTS)
            sp.dma_start(adj_dram.rearrange("r p c -> p r c"), adj[:, :, :].rearrange("p (r t) c -> p r (t c)", r=RELS)).then_inc(adj_out, 16)
            sp.wait_ge(adj_out, 16)
            for layer in range(2):
                w = a[("L0_gnn_W1", "L0_gnn_W2")[layer]].rearrange("r (k p) o -> r p k o", p=P)
                if layer == 1:
                    for c in range(2):
                        load(Unit(U_ROOT2 + c), chunks(a["L0_gnn_root2"])[:, :, wcols(c)])
                    sp.wait_ge(c_added, FREE_BUF + RELS)
                    sp.dma_start(count_dram, counts[:, :, :].rearrange("p t c -> p (t c)")).then_inc(c_out, 16)
                with sp.Fori(0, RELS // 2) as i:
                    for b in range(2):
                        sp.wait_ge(a_ready, layer * RELS + 2 * i + b + 1)
                        if layer == 0:
                            sp.wait_ge(c_added, 2 * i + b + 1)
                        sp.dma_start(A_u[b][:, :, :].rearrange("p t c -> p (t c)"),
                                     adj_dram[ds(2 * i + b, 1), :, :].rearrange("r p c -> (r p) c")).then_inc(a_in[layer][b], 16)
                        for c in range(2):
                            load(Unit(U_REL[layer] + 2 * b + c, i, 4),
                                 w[ds(2 * i + b, 1), :, :, wcols(c)].rearrange("r p k o -> (r p) k o"))
            def expert_loads(n, units):
                def slot(i, b, expert):
                    for c, w in enumerate(units):
                        u = (2 * i + b) * len(units) + c
                        s = (b * len(units) + c) % RING
                        rows, k, cols = FFN_UNITS[n][c]
                        sp.wait_ge(e_lo[n], u + 1)
                        sp.dma_start(RAW4[s][0:rows, 0:k * cols].rearrange("p (k n) -> p k n", k=k),
                                     w[ds(expert, 1)].rearrange("e p k o -> (e p) k o")).then_inc(eraw_ready[n][s], 16)

                with sp.Fori(0, EXPERTS // 2) as i:
                    for b in range(2):
                        slot(i, b, 2 * i + b)
                sp.wait_ge(placed, 2 * (n + 1))
                with sp.Fori(EXPERTS // 2, XSLOTS // 2) as i:
                    for b in range(2):
                        slot(i, b, sp.value_load(slot_expert[0:1, ds(2 * i + b, 1)], min_val=0, max_val=EXPERTS - 1))

            w1 = a["L0_ffn_W1"].rearrange("e (k p) o -> e p k o", p=P)
            w2 = a["L0_ffn_W2"].rearrange("e (k p) o -> e p k o", p=HP0)
            w3 = a["L0_ffn_W3"].rearrange("e (k p) o -> e p k o", p=P)
            expert_loads(0, [w1, w2] + [w3[:, :, :, wcols(c)] for c in range(2)])
            sp.wait_ge(e_lo[0], RING + SPLITS[0])
            with sp.Fori(0, 3) as i:
                for c in range(2):
                    load(Unit(U_MIX1 + c, i, 2), chunks(a["L1_mix_w_qkv"])[:, :, ds((2 * i + c) * WCOL, WCOL)])
            for c in range(2):
                load(Unit(U_MIX1 + 6 + c), chunks(a["L1_mix_w_proj"])[:, :, wcols(c)])
            for layer in range(2):
                units = DIM // GCOL if layer else GHEADS
                for first, name in ((U_XL, ("L1_gnn_W1", "L1_gnn_W2")), (U_SKIP, ("L1_gnn_Wr1", "L1_gnn_Wr2"))):
                    for c in range(units):
                        load(Unit(first[layer] + c), chunks(a[name[layer]])[:, :, c * GCOL:(c + 1) * GCOL])
            w1 = a["L1_ffn_w1"].rearrange("e (k p) o -> e p k o", p=P)
            w2 = a["L1_ffn_w2"].rearrange("e (k p) o -> e p k o", p=P)
            expert_loads(1, [w1[:, :, :, wcols(c)] for c in range(3)] + [w2[:, :, :, c * YCOL1:(c + 1) * YCOL1] for c in range(3)])
            store()

        @block.gpsimd
        def _(pool):
            def split(u, n, rows=P):
                s = u.slot
                pool.wait_ge(raw_ready[s], u.loads)
                if not (isinstance(u.n, int) and u.n < 2):
                    pool.wait_ge(unit_used, u.n - 1)
                hi, lo = at(W[s], slice(0, rows), slice(0, n))
                pool.tensor_tensor(hi, raw[s][0:rows, 0:n], zero_col[0:rows, :].broadcast_to([rows, n]), ALU.add).then_inc(hi_ready, 1)
                pool.wait_ge(hi_ready, u.n + 1)
                pool.tensor_tensor(lo, raw[s][0:rows, 0:n], f32(hi), ALU.subtract).then_inc(unit_ready, 1)

            def split_rest(first, times, per, n):
                with pool.Fori(0, times) as i:
                    for c in range(per):
                        split(Unit(first + c, i, per), n)

            pool.memset(X[:, FULL, :], 0.0).then_inc(pad_zero, 1)
            pool.memset(ident[:, :], 0.0).then_inc(consts, 1)
            pool.memset(before[:, :], 0.0).then_inc(consts, 1)
            pool.memset(fill_i[:, :], -1).then_inc(consts, 1)
            pool.memset(eps_col[:, :], EPS).then_inc(consts, 1)
            pool.memset(ones_f[:, :], 1.0).then_inc(consts, 1)
            pool.memset(f32(ones_r[:, :]), 1.0).then_inc(consts, 1)
            pool.memset(ones_g[:, :], 1.0).then_inc(consts, 1)
            pool.memset(restart[:, :, 1:EDGE_COLS], 1.0).then_inc(consts, 1)
            pool.memset(restart[:, :, 0:1], 0.0).then_inc(consts, 1)
            pool.iota(iota_g[:, :], [[1, GROUPS]], base=0, channel_multiplier=0, allow_small_or_imprecise_dtypes=True).then_inc(consts, 1)
            pool.iota(iota_s[:, :], [[1, SLOTS]], base=0, channel_multiplier=0, allow_small_or_imprecise_dtypes=True).then_inc(consts, 1)
            pool.iota(dst_iota[:, :], [[1, COLS]], base=0, channel_multiplier=0, allow_small_or_imprecise_dtypes=True).then_inc(consts, 1)
            pool.memset(zero_col[:, :], 0.0).then_inc(consts, 1)
            pool.memset(zero_row[:, :], 0.0).then_inc(consts, 1)
            for part in rfT:
                pool.memset(f32(part[:, :, :]), 0.0).then_inc(consts, 1)
            pool.wait_ge(consts, 16)
            pool.affine_select(out=ident[:, :], in_=ident[:, :], compare_op=ALU.not_equal, fill=1.0, base=0,
                               pattern=[[-1, P]], channel_multiplier=1).then_inc(masks, 1)
            pool.affine_select(out=before[:, :], in_=before[:, :], compare_op=ALU.is_ge, fill=1.0, base=0,
                               pattern=[[-1, P]], channel_multiplier=1).then_inc(masks, 1)
            for c in range(2):
                split(Unit(U_V + c), UNIT)
            pool.wait_ge(filled, 16)
            pool.wait_ge(pos_ready, 1)
            begun = 0
            for j in range(PAIRS):
                for c in range(2):
                    split(Unit(U_MIX + 2 * j + c), KD * P)
                    while begun < min(EDGE_COLS, (2 * j + c + 1) * 8):
                        pool.indirect_dma_start(out=sorted_dram, out_offset=bass.IndirectOffsetOnAxis(ap=pos_i[:, begun:begun + 1], axis=0),
                                                in_=code_i[:, begun:begun + 1], in_offset=None).then_inc(scattered, 16)
                        begun += 1
            split_rest(U_PROJ, 1, 2, UNIT)
            after_phase(pool, 2)
            pool.memset(words(adj[:, GROUPS // 2:GROUPS, :]), 0).then_inc(adj_zero, 1)
            split_rest(U_ROOT1, 1, 2, UNIT)
            split_rest(U_REL[0], RELS, 2, UNIT)
            split_rest(U_ROOT2, 1, 2, UNIT)
            split_rest(U_REL[1], RELS, 2, UNIT)
            def expert_splits(n):
                pool.iota(iota_e[:, :], [[1, EXPERTS]], base=0, channel_multiplier=0, allow_small_or_imprecise_dtypes=True).then_inc(consts, 1)
                pool.iota(iota_m[:, :], [[1, MORE]], base=0, channel_multiplier=0, allow_small_or_imprecise_dtypes=True).then_inc(consts, 1)
                pool.memset(ones_e[:, :], 1.0).then_inc(consts, 1)
                pool.memset(restart_e[:, :, 1:CHOICES], 1.0).then_inc(consts, 1)
                pool.memset(restart_e[:, :, 0:1], 0.0).then_inc(consts, 1)
                pool.memset(before_e[:, :], 0.0).then_inc(consts, 1)
                pool.wait_ge(consts, 16 + 6 * (n + 1))
                pool.affine_select(out=before_e[:, :], in_=before_e[:, :], compare_op=ALU.is_ge, fill=1.0, base=0,
                                   pattern=[[-1, P]], channel_multiplier=1).then_inc(masks, 1)
                pool.sem_inc(e_lo[n], RING)
                units = FFN_UNITS[n]

                def low(i, b):
                    for c, (rows, k, cols) in enumerate(units):
                        s = (b * len(units) + c) % RING
                        hi, lo = at(W4[s], slice(0, rows), slice(0, k * cols))
                        pool.wait_ge(e_hi[n], (2 * i + b) * len(units) + c + 1)
                        pool.tensor_tensor(lo, RAW4[s][0:rows, 0:k * cols], f32(hi), ALU.subtract).then_inc(e_lo[n], 1)

                pool.wait_ge(cleared, 16)
                pool.wait_ge(placed, 2 * n + 1)
                for t in range(TILES):
                    rows = LAST if t == FULL else P
                    for k in range(CHOSEN):
                        j = t * CHOSEN + k
                        pool.indirect_dma_start(out=slot_rows_dram, out_offset=bass.IndirectOffsetOnAxis(ap=place[0:rows, j:j + 1], axis=0),
                                                in_=XE[0:rows, t, :], in_offset=None).then_inc(sent, 16)
                with pool.Fori(0, XSLOTS // 2) as i:
                    for b in range(2):
                        low(i, b)
                for b in range(2):
                    pool.wait_ge(y_out[n][b], 16 + 16 * (XSLOTS // 2))
                for t in range(TILES):
                    rows = LAST if t == FULL else P
                    for k in range(CHOSEN):
                        j = t * CHOSEN + k
                        pool.indirect_dma_start(out=out_rows[k][0:rows, t, :], out_offset=None, in_=slot_out_dram[n],
                                                in_offset=bass.IndirectOffsetOnAxis(ap=place[0:rows, j:j + 1], axis=0)).then_inc(back[t], 16)

            after_phase(pool, 7)
            expert_splits(0)
            pool.wait_ge(e_used[0], RING + SPLITS[0])
            split_rest(U_MIX1, 4, 2, UNIT)
            split_rest(U_XL[0], GHEADS, 2, KD * GCOL)
            split_rest(U_XL[1], DIM // GCOL, 2, GAT1 // P * GCOL)
            after_phase(pool, 11)
            expert_splits(1)

        @block.scalar
        def _(act):
            def std_of(n):
                act.activation(warm[:, n:n + 1], eps_col[:, :], ACT.Sqrt)
                act.wait_ge(ln_var, TILES * (n + 1))
                act.activation(std[:, :], mv[:, :, 1], ACT.Sqrt, bias=eps_col[:, :]).then_inc(ln_std, 1)

            def transposes_hi(start, kd=KD):
                g = start
                for t in range(TILES):
                    for ks in groups_of(kd):
                        (into, k), n = chunk_of(ks[0]), len(ks)
                        act.wait_ge(tr_full, g + 1)
                        act.activation(into[0][:, k:k + n, t * P:(t + 1) * P], ps[:, g % 8, 0:n * P].rearrange("p (k n) -> p k n", k=n),
                                       ACT.Copy).then_inc(tr_hi, 1)
                        g += 1

            def rows_split_hi(src, ready):
                for t in range(TILES):
                    ready(t)
                    act.activation(xn[0][:, t, :], src[:, t, :], ACT.Copy).then_inc(rows_hi, 1)

            act.wait_ge(consts, 12)
            act.dma_start(sorted_dram.rearrange("(p c) o -> p (c o)", p=P), fill_i[:, :]).then_inc(filled, 16)
            act.dma_start(bias_row[0][:, :], a["L0_mix_b_qkv"][2 * DIM:3 * DIM].partition_broadcast(P)).then_inc(bias_in, 16)
            act.dma_start(bias_row[1][:, :], a["L0_mix_b_proj"].partition_broadcast(P)).then_inc(bias_in, 16)
            for h in range(2):
                act.dma_start(rf2[:, :, h * HEAD0:(h + 1) * HEAD0], a["L0_mix_random_features"].rearrange("(c p) d -> p c d", p=P)).then_inc(rf_in, 16)
            act.dma_start(qk_bias[:, :], a["L0_mix_b_qkv"][0:2 * DIM].rearrange("(j p) -> p j", p=P), allow_slow_non_contiguous=True).then_inc(rf_in, 16)
            std_of(0)
            transposes_hi(TR_0)
            act.wait_ge(rf_full, 1)
            for s in range(2):
                own = slice(s * HEAD0, (s + 1) * HEAD0)
                act.activation(rfT[0][own, s, :], ps[own, RF_BANK, 0:FEATS], ACT.Copy).then_inc(rf_hi, 1)
            end_phase(act, "act", 1)
            act.wait_ge(consts, 16)
            act.dma_start(slot_rows_dram.rearrange("(s p) d -> p s d", p=P), zero_row[:, :].unsqueeze(1).broadcast_to([P, 2 * XSLOTS, DIM])).then_inc(cleared, 16)
            for j in range(SET):
                col, t = j // TILES, j % TILES
                act.wait_ge(prod_used, PR_V0 + j + 1)
                act.activation(attnT[0][:, 3 * col:3 * col + 3, t * P:(t + 1) * P], v_f[j % 2][:, :].rearrange("p (k n) -> p k n", k=3), ACT.Copy).then_inc(v_hi, 1)
            def key_features(j, s, n):
                t = slice(2 * n, min(2 * n + 2, TILES))
                w = t.stop - t.start
                act.wait_ge(B_full, 8 * j + 4 * s + n + 1)
                act.activation(phi_k[0][:, t, :], ps[:, 4 + n % 2, 0:w * FEATS].rearrange("p (t m) -> p t m", t=w), ACT.Relu).then_inc(B_hi, 1)

            def query_features(j, s, n):
                act.wait_ge(A_full, 12 * j + 4 * s + 2 * n + 6)
                act.activation(halves(phi_qT[0][:, n, :]), ps[:, 2 * n:2 * n + 2, 0:HALF], ACT.Relu).then_inc(A_hi, 2)

            with act.Fori(0, PAIRS) as j:
                for n in range(2):
                    act.wait_ge(A_full, 12 * j + 2 * n + 2)
                    act.activation(halves((kT, qT)[n][0][:, :]), ps[:, 2 * n:2 * n + 2, 0:HALF], ACT.Identity,
                                   bias=qk_bias[:, ds((1 - n) * KD + j, 1)]).then_inc(A_hi, 2)
                for s in range(2):
                    key_features(j, s, 0)
                    key_features(j, s, 1)
                    query_features(j, s, 0)
                    key_features(j, s, 2)
                    query_features(j, s, 1)
                    act.wait_ge(B_full, 8 * j + 4 * s + 4)
                    act.activation(kv[0][:, :, s, s * HEAD0:(s + 1) * HEAD0], ps[:, 5, 0:2 * P].rearrange("p (m d) -> p m d", m=2)[:, :, s * HEAD0:(s + 1) * HEAD0],
                                   ACT.Copy).then_inc(B_hi, 1)
                act.wait_ge(C_full, 2 * j + 2)
                act.activation(attnT[0][:, ds(j, 1), :].rearrange("p k (h n) -> p (k h) n", h=2), ps[:, 6:8, 0:HALF], ACT.Copy,
                               scale=MIX0_SCALE).then_inc(C_hi, 1)
            end_phase(act, "act", 2)
            act.dma_start(bias_row[0][:, :], a["L0_gnn_b1"].partition_broadcast(P)).then_inc(bias_in, 16)
            act.dma_start(bias_row[1][:, :], a["L0_gnn_b2"].partition_broadcast(P)).then_inc(bias_in, 16)
            act.wait_ge(dst_ready, 1)

            def one_hot(s, k):
                act.activation(apart[k % 2][:, :], dst_iota[:, :], ACT.Square, bias=dst_f[:, ds(2 * s + 1, 1)], scale=-1.0).then_inc(apart_ready, 1)
                act.wait_ge(apart_ready, s + 1)
                act.activation(dst_hot[k][:, 1, :], apart[k % 2][:, :], ACT.Relu, bias=f32(ones_r[:, 0:1]), scale=-1.0).then_inc(hot_b, 1)

            for k in range(HOTS):
                if k >= 2:
                    act.wait_ge(hot_b, k - 1)
                one_hot(k, k)
            with act.Fori(1, SLOTS // HOTS) as i:
                for k in range(HOTS):
                    act.wait_ge(hot_b, HOTS * i + k - 1)
                    act.wait_ge(slot_full, HOTS * i + k - HOTS + 1)
                    one_hot(HOTS * i + k, k)
            end_phase(act, "act", 3)
            act.wait_ge(adj_out, 16)
            act.wait_ge(cleared, 16)
            act.sem_inc(a_ready, FREE_BUF)
            rows_split_hi(XN, lambda t: None)
            end_phase(act, "act", 4)
            for layer in range(2):
                if layer == 1:
                    rows_split_hi(ACC, lambda t: act.wait_ge(rows_ready, ROWS_H + t + 1))
                    transposes_hi(TR_H)
                    act.wait_ge(c_out, 16)
                    end_phase(act, "act", 6)
                with act.Fori(0, RELS // 2) as i:
                    for b in range(2):
                        act.wait_ge(a_in[layer][b], 16 * i + 16)
                        act.wait_ge(agg_full, layer * AGGS * RELS + AGGS * (2 * i + b + 1))
                        act.activation(A_r[b][:, :, :], A_u[b][:, :, :], ACT.Copy).then_inc(a_ready, 1)
                        for n in range(AGGS):
                            act.wait_ge(agg_val, layer * AGGS * RELS + FREE_AGG + AGGS * (2 * i + b) + n + 1)
                            act.activation(XT[0][:, n // 2, cols_half(n)], agg_f[n % 3][:, :], ACT.Copy).then_inc(agg_hi, 1)
                end_phase(act, "act", (5, 7)[layer])

            def experts(n, router_w, router_b, out_bias, in_biases):
                act.dma_start(gate_raw[:, :, :], chunks(router_w)).then_inc(gate_in, 16)
                act.dma_start(gate_b[:, :], router_b.rearrange("(e o) -> e o", o=1)).then_inc(gate_in, 16)
                act.dma_start(out_b[:, :], out_bias).then_inc(gate_in, 16)
                for m, src in enumerate(in_biases):
                    count, width = IN_B[n][m]
                    act.dma_start(in_b_rows[m][0:EXPERTS * count, 0:width], src.rearrange("e (c p) -> (e c) p", p=width)).then_inc(gate_in, 16)
                std_of(LN_FFN[n])
                transposes_hi(TR_FFN[n])
                for m, (count, width) in enumerate(IN_B[n]):
                    act.wait_ge(in_b_full, 2 * n + m + 1)
                    act.activation(in_b[m][0:width, 0:EXPERTS * count], ps[0:width, 3 + m, 0:EXPERTS * count], ACT.Copy).then_inc(in_b_ready, 1)
                act.wait_ge(gate_arg, n + 1)
                act.activation(expo[:, :, :], diff[:, :, :], ACT.Exp).then_inc(gate_exp, 1)
                act.wait_ge(in_b_ready, 2 + n)
                act.sem_inc(h_act[n], FREE_H)
                act.sem_inc(y_out[n][0], 16)
                act.sem_inc(y_out[n][1], 16)
                steps, units = HIDDEN[n], FFN_UNITS[n]

                def high(i, b, c):
                    u = (2 * i + b) * len(units) + c
                    s = (b * len(units) + c) % RING
                    rows, k, cols = units[c % len(units)]
                    act.wait_ge(eraw_ready[n][s], 16 * len(units) // 2 * i + 16 * ((b * len(units) + c) // RING + 1))
                    act.wait_ge(e_used[n], u + 1)
                    act.activation(W4[s][0][0:rows, 0:k * cols], RAW4[s][0:rows, 0:k * cols], ACT.Copy).then_inc(e_hi[n], 1)

                def rows_in(i, b):
                    act.wait_ge(t_full[n], 3 * (2 * i + b) + 1)
                    act.dma_start(slot_in[b][:, :, :], slot_at(slot_rows_dram, i, b)).then_inc(slot_ready[n][b], 16)

                def rows_hi(i, b):
                    for q in range(Q_T):
                        act.wait_ge(t_full[n], FREE_IN + 3 * (2 * i + b) + q + 1)
                        act.activation(XT[0][:, 2 * q:2 * q + 2, b * SLOT_ROWS:(b + 1) * SLOT_ROWS],
                                       ps[:, T_BANK + q, :].rearrange("p (k n) -> p k n", k=2), ACT.Copy).then_inc(t_hi[n], 1)

                def slot(i, b, last):
                    end = i == XSLOTS // 2 - 1 if isinstance(i, int) else False
                    e = act.value_load(slot_expert[0:1, ds(2 * i + b, 1)], min_val=0, max_val=EXPERTS - 1)
                    if not end:
                        rows_in(i + 1, b)
                    for v in range(len(units)):
                        for g, (unit, _, width, _, into, m) in enumerate(steps):
                            if unit != v:
                                continue
                            at_step = 2 * len(steps) * i + b * len(steps) + g
                            act.wait_ge(h_lo[n], at_step + places_left(n, g))
                            act.wait_ge(h_full[n], at_step + 1)
                            full, exact = hidden_at(g, width)
                            bias = in_b[m][0:width, ds(e * IN_B[n][m][0] + (g if m == 0 else g - IN_B[n][0][0]), 1)]
                            act.activation(hT[0][0:width, into, :], full, ACT.Gelu, bias=bias)
                            act.activation(exact, full, ACT.Gelu, bias=bias).then_inc(h_act[n], 1)
                        if v == ROWS_AFTER[n] and not last:
                            rows_hi(i + b, 1 - b)
                        if not (last and v + AHEAD >= len(units)):
                            high(i, b, v + AHEAD)
                    act.wait_ge(y_used[n], FREE_Y + 2 * OUTPUT[n][1] * (2 * i + b + 1))
                    act.dma_start(slot_at(slot_out_dram[n], i, b), y_rows[b][:, :, :]).then_inc(y_out[n][b], 16)

                for c in range(AHEAD):
                    high(0, 0, c)
                act.wait_ge(sent, 16 * CHOICES * (n + 1))
                for b in range(2):
                    rows_in(0, b)
                rows_hi(0, 0)
                act.wait_ge(placed, 2 * (n + 1))
                slot_pairs(act, slot)

            experts(0, a["L0_ffn_Wg"], a["L0_ffn_bg"], a["L0_ffn_b3"], [a["L0_ffn_b1"], a["L0_ffn_b2"]])
            end_phase(act, "act", 8)

            for t, name in ((in_gain, "ln_in_g"), (in_shift, "ln_in_b"), (out_gain, "ln_out_g"), (out_shift, "ln_out_b")):
                act.dma_start(t[:, :], a["L1_mix_" + name].partition_broadcast(P)).then_inc(mix_in, 16)
            act.dma_start(count[:, :, :].rearrange("p t c -> p (t c)"), count_dram).then_inc(c_in, 16)
            std_of(LN_IN1)
            std_of(LN_MIX_IN)
            transposes_hi(TR_MIX_IN)
            for n, (rows, start) in enumerate(((Q, PR_Q), (K, PR_K))):
                for t in range(TILES):
                    act.wait_ge(prod_used, start + TILES + t + 1)
                    if n * TILES + t > 0:
                        act.wait_ge(norm_done, n * TILES + t)
                    act.activation(square[:, :], rows[:, t, :], ACT.Square, accum_out=norm[:, n, t:t + 1]).then_inc(norm_done, 1)
            for t in range(TILES):
                act.wait_ge(c_full, t + 1)
                act.activation(count[:, t, 0:FULL * P], ps[:, 4 + 2 * (t % 2), 0:FULL * P], ACT.Copy)
                act.activation(count[:, t, FULL * P:COLS], ps[:, 4 + 2 * (t % 2) + 1, 0:P], ACT.Copy).then_inc(c_done, 1)
            act.wait_ge(norm_done, 2 * TILES)
            act.activation(norm[:, :, :], norm[:, :, :], ACT.Sqrt).then_inc(norm_done, 1)
            std_of(LN_MIX_OUT)
            transposes_hi(TR_MIX_OUT)
            end_phase(act, "act", 9)
            transposes_hi(TR_XN1)

            def gat(layer):
                heads, units, kd = GAT[layer]
                tiles = heads * TILES
                heads_seen = layer * GHEADS
                seen = heads_seen * TILES
                XL, PT, a_row = ((XL1, PT1, a_row1), (XL2, PT2, a_row2))[layer]

                def xl_chunk(h, u, t):
                    n = (h * units + u) * TILES + t
                    act.wait_ge(xl_full, seen + n + 1)
                    if h >= len(XL):
                        act.wait_ge(o_full, seen + (h - len(XL) + 1) * TILES)
                    act.activation(XL[h % len(XL)][0][:, t, u * GCOL:(u + 1) * GCOL], ps[:, n % 2, 0:GCOL], ACT.Copy).then_inc(xl_hi, 1)

                def weights_hi(g):
                    act.wait_ge(pt_full, seen + g + 1)
                    r = len(PT)
                    if g >= r:
                        act.wait_ge(o_full, seen + g - r + 1)
                    hi = PT[g % r][0]
                    act.activation(hi[:, 0:FULL, :], ps[:, 4, 0:FULL * P].rearrange("p (t n) -> p t n", t=FULL), ACT.Copy)
                    act.activation(hi[:, FULL, :], ps[:, 5, 0:P], ACT.Copy).then_inc(pt_hi, 1)

                def output(g):
                    h, t = g // TILES, g % TILES
                    act.wait_ge(o_full, seen + g + 1)
                    act.wait_ge(inv_ready, seen + g + 1)
                    if layer == 0:
                        act.activation(wide[:, t, h * GCOL:(h + 1) * GCOL], ps[:, 6 + g % 2, 0:GCOL], ACT.Copy,
                                       scale=g_inv[:, g:g + 1]).then_inc(o_used, 1)
                    else:
                        act.activation(wide[:, t, 0:DIM].rearrange("p (c n) -> p c n", c=2), ps[:, 6:8, 0:WCOL], ACT.Copy,
                                       scale=g_inv[:, g:g + 1]).then_inc(o_used, 1)

                def exponentials(g):
                    act.wait_ge(e_ready, seen + g + 1)
                    act.activation(g_e[g % 2][:, :], g_e[g % 2][:, :], ACT.Exp, bias=g_neg[:, g % 2:g % 2 + 1]).then_inc(e_exp, 1)

                for u in range(units):
                    for t in range(TILES):
                        xl_chunk(0, u, t)
                for g in range(tiles + 4):
                    h, t = g // TILES, g % TILES
                    if 0 <= g - 4 < tiles:
                        output(g - 4)
                    if h + 1 < heads:
                        xl_chunk(h + 1, 0, t)
                    if 0 <= g - 2 < tiles:
                        weights_hi(g - 2)
                    if g < tiles:
                        exponentials(g)
                act.wait_ge(xl_done, seen + heads * units * TILES)
                for k, n in enumerate(("be", "br")):
                    act.dma_start(a_row[k][:, :], a[f"L1_gnn_{n}{layer + 1}"].partition_broadcast(P)).then_inc(late_in[layer], 16)
                std_of(LN_GAT[layer])
                if layer == 0:
                    transposes_hi(TR_H1, GAT1 // P)

            for k, n in enumerate(("L1_gnn_a_src1", "L1_gnn_a_dst1")):
                act.dma_start(a_row1[k][:, :], a[n].rearrange("h c -> (h c)").partition_broadcast(P)).then_inc(gat_in[0], 16)
            for n in row1:
                act.dma_start(row1[n][:, :], a[f"L1_gnn_{n}1"].partition_broadcast(P)).then_inc(gat_in[0], 16)
            gat(0)
            end_phase(act, "act", 10)
            for k, n in enumerate(("L1_gnn_a_src2", "L1_gnn_a_dst2")):
                act.dma_start(a_row2[k][:, :], a[n].rearrange("h c -> (h c)").partition_broadcast(P)).then_inc(gat_in[1], 16)
            act.dma_start(bias_row[0][:, :], a["L1_gnn_b2"].partition_broadcast(P)).then_inc(gat_in[1], 16)
            act.dma_start(bias_row[1][:, :], a["L1_gnn_g2"].partition_broadcast(P)).then_inc(gat_in[1], 16)
            gat(1)
            end_phase(act, "act", 11)
            experts(1, a["L1_ffn_router_w"], a["L1_ffn_router_b"], a["L1_ffn_b2"], [a["L1_ffn_b1"]])
            end_phase(act, "act", 12)

        @block.vector
        def _(vec):
            order = Order(vec, vec_order)

            def row_stats(src, t, width=DIM):
                for c in range(2):
                    order.step(vec.bn_stats(stats[:, t, c, :], src[:, t, c * width // 2:(c + 1) * width // 2]))

            def normalise(n, src, dst, ready=True, width=DIM, gain=None, shift=None, counted=False):
                if not counted:
                    for t in range(TILES):
                        row_stats(src, t, width)
                order.wait()
                for t in range(TILES):
                    vec.bn_aggr(mv[:, t, :], stats[:, t, :, :]).then_inc(ln_var, 1)
                if gain is not None:
                    vec.wait_ge(ln_var, TILES * (n + 1))
                    for t in range(TILES):
                        order.step(vec.scalar_tensor_tensor(dst[:, t, :], src[:, t, :], mv[:, t, 0:1], gain[:, :], ALU.subtract, ALU.mult))
                vec.wait_ge(ln_std, n + 1)
                order.step(vec.reciprocal(rstd[:, :], std[:, :]))
                order.wait()
                for t in range(TILES):
                    if gain is None:
                        ins = vec.tensor_scalar(dst[:, t, :], src[:, t, :], mv[:, t, 0:1], rstd[:, t:t + 1], ALU.subtract, ALU.mult)
                    else:
                        ins = vec.scalar_tensor_tensor(dst[:, t, :], dst[:, t, :], rstd[:, t:t + 1], shift[:, :], ALU.mult, ALU.add)
                    if ready:
                        ins.then_inc(rows_ready, 1)
                    else:
                        order.step(ins)

            def transposes_lo(start, kd=KD):
                g = start
                for t in range(TILES):
                    for ks in groups_of(kd):
                        (into, k), n = chunk_of(ks[0]), len(ks)
                        vec.wait_ge(tr_hi, g + 1)
                        hi, lo = at(into, slice(None), slice(k, k + n), slice(t * P, (t + 1) * P))
                        vec.tensor_tensor(lo, ps[:, g % 8, 0:n * P].rearrange("p (k n) -> p k n", k=n), f32(hi), ALU.subtract).then_inc(tr_done, 1)
                        g += 1

            def rows_split_lo(n, src):
                for t in range(TILES):
                    vec.wait_ge(rows_hi, TILES * n + t + 1)
                    vec.tensor_tensor(xn[1][:, t, :], src[:, t, :], f32(xn[0][:, t, :]), ALU.subtract).then_inc(rows_lo, 1)

            def add_products(start, rows, bias=None, units=2, cols=WCOL, first=0):
                for j in range(first * TILES, units * TILES):
                    g = start + j
                    c, t = j // TILES, j % TILES
                    col = slice(c * cols, (c + 1) * cols)
                    vec.wait_ge(prod_full, g + 1)
                    vec.tensor_tensor(rows[:, t, col], ps[:, g % 8, 0:cols],
                                      rows[:, t, col] if bias is None else bias[:, col], ALU.add).then_inc(prod_used, 1)

            def take_products(start, rows):
                for j in range(SET):
                    c, t = j // TILES, j % TILES
                    vec.wait_ge(prod_full, start + j + 1)
                    vec.tensor_copy(rows[:, t, wcols(c)], ps[:, (start + j) % 8, 0:WCOL]).then_inc(prod_used, 1)

            def add_bias(rows, bias):
                for t in range(TILES):
                    order.step(vec.tensor_tensor(rows[:, t, :], rows[:, t, :], bias[:, :], ALU.add))

            vec.wait_ge(x_in, 32)
            vec.wait_ge(pad_zero, 1)
            normalise(0, X, XN)
            transposes_lo(TR_0)
            vec.wait_ge(rf_hi, 2)
            for s in range(2):
                own = slice(s * HEAD0, (s + 1) * HEAD0)
                order.step(vec.tensor_tensor(rfT[1][own, s, :], ps[own, RF_BANK, 0:FEATS], f32(rfT[0][own, s, :]), ALU.subtract))
            vec.wait_ge(edges_in, 48)
            vec.wait_ge(consts, 12)
            order.step(vec.tensor_scalar(tile_i[:, :], src_i[:, :], 7, None, ALU.arith_shift_right))
            order.step(vec.tensor_scalar(low_i[:, :], src_i[:, :], P - 1, None, ALU.bitwise_and))
            order.wait()
            order.step(vec.scalar_tensor_tensor(group_f[:, :], typ_i[:, :], float(TILES), tile_i[:, :], ALU.mult, ALU.add))
            order.step(vec.scalar_tensor_tensor(code_i[:, :], low_i[:, :], 1024.0, dst_i[:, :], ALU.mult, ALU.add))
            order.wait()
            every = [EDGE_ROWS, GROUPS, EDGE_COLS]
            order.step(vec.tensor_tensor(onehot_g[:, :, :], group_f[:, :].unsqueeze(1).broadcast_to(every),
                                         iota_g[:, :].unsqueeze(2).broadcast_to(every), ALU.is_equal))
            order.wait()
            order.step(vec.tensor_tensor_scan(rank[:, :, :].rearrange("p g c -> p (g c)"), restart[:, :, :].rearrange("p g c -> p (g c)"),
                                              onehot_g[:, :, :].rearrange("p g c -> p (g c)"), 0.0, ALU.mult, ALU.add))
            order.wait()
            vec.tensor_copy(in_row[:, :], rank[:, :, EDGE_COLS - 1]).then_inc(sort_row, 1)
            vec.wait_ge(sort_sum, 2)
            order.step(vec.tensor_scalar(need_i[:, :], ps[0:EDGE_ROWS, SORT_BANK + 1, 0:GROUPS], float(SLOT - 1), None, ALU.add))
            order.wait()
            order.step(vec.tensor_scalar(need_s[:, :], need_i[:, :], SLOT.bit_length() - 1, None, ALU.arith_shift_right))
            order.wait()
            order.step(vec.tensor_copy(need_f[:, :], need_s[:, :]))
            order.wait()
            order.step(vec.tensor_tensor_scan(slot_end[:, :], ones_g[:, :], need_f[:, :], 0.0, ALU.mult, ALU.add))
            order.wait()
            order.step(vec.tensor_tensor(slot_base[:, :], slot_end[:, :], need_f[:, :], ALU.subtract))
            order.wait()
            order.step(vec.scalar_tensor_tensor(offset_g[:, :], slot_base[:, :], float(SLOT), ps[0:EDGE_ROWS, SORT_BANK, 0:GROUPS], ALU.mult, ALU.add))
            order.wait()
            order.step(vec.scalar_tensor_tensor(rank[:, :, :], rank[:, :, :], -1.0, offset_g[:, :].unsqueeze(2).broadcast_to(every), ALU.add, ALU.add))
            order.wait()
            order.step(vec.tensor_tensor(rank[:, :, :], rank[:, :, :], onehot_g[:, :, :], ALU.mult))
            order.wait()
            order.step(vec.tensor_reduce(pos_f[:, :], rank[:, :, :].rearrange("p g c -> p c g"), AX.X, ALU.add))
            order.wait()
            order.step(vec.tensor_copy(spot_i[:, :], pos_f[:, :]))
            order.wait()
            order.step(vec.tensor_scalar(low_i[:, :], spot_i[:, :], P - 1, None, ALU.bitwise_and))
            order.step(vec.tensor_scalar(sub_i[:, :], spot_i[:, :], 7, None, ALU.arith_shift_right))
            order.wait()
            vec.scalar_tensor_tensor(pos_i[:, :], low_i[:, :], float(SUBS), sub_i[:, :], ALU.mult, ALU.add).then_inc(pos_ready, 1)
            sg = [1, SLOTS, GROUPS]
            order.step(vec.tensor_tensor(past[:, :, :], slot_end[0:1, :].unsqueeze(1).broadcast_to(sg), iota_s[:, :].unsqueeze(2).broadcast_to(sg), ALU.is_le))
            order.wait()
            order.step(vec.tensor_reduce(group_of[:, :], past[:, :, :], AX.X, ALU.add))
            order.wait()
            order.step(vec.tensor_scalar(slot_group[:, :], group_of[:, :], float(GROUPS - 1), None, ALU.min))
            vec.wait_ge(bias_in, 32)
            vec.wait_ge(filled, 16)
            end_phase(vec, "vec", 1)
            for part in kv:
                order.step(vec.memset(f32(part[:, :, :, :]), 0.0))
            for j in range(SET + 1):
                if j < SET:
                    col = j // TILES
                    vec.wait_ge(prod_full, PR_V0 + j + 1)
                    if j >= 2:
                        vec.wait_ge(v_lo, j - 1)
                    vec.tensor_tensor(v_f[j % 2][:, :], ps[:, (PR_V0 + j) % 8, 0:WCOL], bias_row[0][:, wcols(col)], ALU.add).then_inc(prod_used, 1)
                if j > 0:
                    m = j - 1
                    col, t = m // TILES, m % TILES
                    vec.wait_ge(v_hi, m + 1)
                    hi, lo = at(attnT, slice(None), slice(3 * col, 3 * col + 3), slice(t * P, (t + 1) * P))
                    vec.tensor_tensor(lo, v_f[m % 2][:, :].rearrange("p (k n) -> p k n", k=3), f32(hi), ALU.subtract).then_inc(v_lo, 1)
            vec.sem_inc(A_done, FREE_A)
            vec.sem_inc(B_done, FREE_B)
            vec.sem_inc(C_done, FREE_C)

            def key_features(j, s, n):
                t = slice(2 * n, min(2 * n + 2, TILES))
                w = t.stop - t.start
                vec.wait_ge(B_hi, 8 * j + 4 * s + n + 1)
                vec.scalar_tensor_tensor(phi_k[1][:, t, :], ps[:, 4 + n % 2, 0:w * FEATS].rearrange("p (t m) -> p t m", t=w), 0.0,
                                         f32(phi_k[0][:, t, :]), ALU.max, ALU.subtract).then_inc(B_done, 1)

            def query_features(j, s, n):
                vec.wait_ge(A_hi, 12 * j + 4 * s + 2 * n + 6)
                vec.scalar_tensor_tensor(halves(phi_qT[1][:, n, :]), ps[:, 2 * n:2 * n + 2, 0:HALF], 0.0, halves(f32(phi_qT[0][:, n, :])),
                                         ALU.max, ALU.subtract).then_inc(A_done, 2)

            with vec.Fori(0, PAIRS) as j:
                for n in range(2):
                    t = (kT, qT)[n]
                    vec.wait_ge(A_hi, 12 * j + 2 * n + 2)
                    vec.scalar_tensor_tensor(halves(t[1][:, :]), ps[:, 2 * n:2 * n + 2, 0:HALF], qk_bias[:, ds((1 - n) * KD + j, 1)], halves(f32(t[0][:, :])),
                                             ALU.add, ALU.subtract).then_inc(A_done, 2)
                for s in range(2):
                    key_features(j, s, 0)
                    key_features(j, s, 1)
                    query_features(j, s, 0)
                    key_features(j, s, 2)
                    query_features(j, s, 1)
                    vec.wait_ge(B_hi, 8 * j + 4 * s + 4)
                    own = slice(s * HEAD0, (s + 1) * HEAD0)
                    vec.tensor_tensor(kv[1][:, :, s, own], ps[:, 5, 0:2 * P].rearrange("p (m d) -> p m d", m=2)[:, :, own],
                                      f32(kv[0][:, :, s, own]), ALU.subtract).then_inc(B_done, 1)
                vec.wait_ge(C_hi, j + 1)
                hi, lo = [t[:, ds(j, 1), :].rearrange("p k (h n) -> p (k h) n", h=2) for t in attnT]
                vec.scalar_tensor_tensor(lo, ps[:, 6:8, 0:HALF], MIX0_SCALE, f32(hi), ALU.mult, ALU.subtract).then_inc(C_done, 2)
            add_bias(X, bias_row[1])
            vec.wait_ge(sorted_in, 16)
            order.step(vec.tensor_scalar(part_i[:, :], sorted_sb[:, :], 10, None, ALU.arith_shift_right))
            order.wait()
            order.step(vec.tensor_copy(srcl_f[:, :], part_i[:, :]))
            order.step(vec.tensor_scalar(sorted_sb[:, :], sorted_sb[:, :], 1023, None, ALU.bitwise_and))
            order.wait()
            vec.tensor_copy(dst_f[:, :], sorted_sb[:, :]).then_inc(dst_ready, 1)
            order.wait()
            vec.wait_ge(dst_ready, 1)
            add_products(PR_PROJ, X)
            end_phase(vec, "vec", 2)
            def one_hot(s, k):
                for half in range(2):
                    vec.tensor_scalar(src_hot[k][:, half, :], dst_iota[:, 0:P], srcl_f[:, ds(2 * s + half, 1)], None, ALU.is_equal)
                vec.tensor_scalar(dst_hot[k][:, 0, :], dst_iota[:, :], dst_f[:, ds(2 * s, 1)], None, ALU.is_equal).then_inc(hot, 1)

            def add_slot(s, k):
                g = vec.value_load(slot_group[0:1, ds(s, 1)], min_val=0, max_val=GROUPS - 1)
                vec.wait_ge(slot_done, FREE_SUM + s)
                block_of = adj[:, ds(g, 1), :].rearrange("p g (h c) -> p (g h) c", h=2)
                vec.tensor_tensor(block_of, block_of, ps[:, 2 * k:2 * k + 2, 0:HALF], ALU.add).then_inc(slot_done, 1)

            for k in range(HOTS):
                one_hot(k, k)
            vec.sem_inc(slot_done, FREE_SUM)
            vec.memset(words(adj[:, 0:GROUPS // 2, :]), 0).then_inc(adj_zero, 1)
            vec.wait_ge(adj_zero, 2)
            with vec.Fori(0, SLOTS // HOTS - 1) as i:
                for k in range(HOTS):
                    vec.wait_ge(slot_full, HOTS * i + k + 1)
                    one_hot(HOTS * i + k + HOTS, k)
                    add_slot(HOTS * i + k, k)
            for k in range(HOTS):
                vec.wait_ge(slot_full, SLOTS - HOTS + k + 1)
                add_slot(SLOTS - HOTS + k, k)
            end_phase(vec, "vec", 3)
            vec.wait_ge(bias_in, 64)
            add_bias(X, bias_row[1])
            add_products(PR_ROOT1, ACC, bias_row[0], 1)
            vec.wait_ge(adj_out, 16)
            rows_split_lo(0, XN)
            vec.memset(counts[:, :, :], 0).then_inc(c_added, 1)
            vec.wait_ge(c_added, 1)
            vec.sem_inc(c_added, FREE_BUF - 1)
            add_products(PR_ROOT1, ACC, bias_row[0], first=1)
            end_phase(vec, "vec", 4)
            for layer in range(2):
                rows = (ACC, X)[layer]
                if layer == 1:
                    for t in range(TILES):
                        vec.tensor_scalar(ACC[:, t, :], ACC[:, t, :], 0.0, None, ALU.max).then_inc(rows_ready, 1)
                    rows_split_lo(1, ACC)
                    transposes_lo(TR_H)
                    add_products(PR_ROOT2, X)
                    end_phase(vec, "vec", 6)
                if layer == 0:
                    vec.sem_inc(cnt_used, FREE_CNT)
                    vec.sem_inc(agg_val, FREE_AGG)
                    vec.sem_inc(agg_done, FREE_DONE)
                    vec.sem_inc(tra_used, FREE_TRA)
                with vec.Fori(0, RELS // 2) as i:
                    for b in range(2):
                        for n in range(2):
                            vec.wait_ge(cnt_full, layer * 2 * RELS + 4 * i + 2 * b + n + 1)
                            vec.tensor_scalar(cnt_m[:, n, :], ps[:, 6 + n, 0:HALF], 1.0, None, ALU.max).then_inc(cnt_used, 1)
                        vec.wait_ge(cnt_used, layer * 2 * RELS + FREE_CNT + 4 * i + 2 * b + 2)
                        if b == 0:
                            order.enter(i, 2)
                        order.step(vec.reciprocal(inv[b][:, :, :], cnt_m[:, :, :]))
                        order.wait()
                        for n in range(AGGS + 1):
                            if n < AGGS:
                                vec.wait_ge(agg_full, layer * AGGS * RELS + FREE_BUF * AGGS + AGGS * (2 * i + b) + n + 1)
                                vec.wait_ge(agg_done, layer * AGGS * RELS + AGGS * (2 * i + b) + n + 1)
                                vec.tensor_tensor(agg_f[n % 3][:, :], ps[:, n % 4, 0:HALF], inv[b][:, n % 2, :], ALU.mult).then_inc(agg_val, 1)
                            if n > 0:
                                m = n - 1
                                vec.wait_ge(agg_hi, layer * AGGS * RELS + AGGS * (2 * i + b) + m + 1)
                                vec.tensor_tensor(XT[1][:, m // 2, cols_half(m)], agg_f[m % 3][:, :], f32(XT[0][:, m // 2, cols_half(m)]),
                                                  ALU.subtract).then_inc(agg_done, 1)
                        if layer == 0:
                            vec.wait_ge(a_in[0][b], 16 * i + 16)
                            vec.wait_ge(c_added, FREE_BUF + 2 * i + b)
                            vec.tensor_tensor(counts[:, :, :], counts[:, :, :], A_u[b][:, :, :], ALU.add).then_inc(c_added, 1)
                        for n in range(2 * TILES):
                            c, t = n // TILES, n % TILES
                            vec.wait_ge(tra_full, layer * 2 * TILES * RELS + 2 * TILES * (2 * i + b) + n + 1)
                            vec.wait_ge(tra_used, layer * 2 * TILES * RELS + 2 * TILES * (2 * i + b) + n + 1)
                            vec.tensor_tensor(rows[:, t, wcols(c)], rows[:, t, wcols(c)], ps[:, 4 + n % 2, 0:WCOL], ALU.add).then_inc(tra_used, 1)
                order.leave(RELS // 2)
                end_phase(vec, "vec", (5, 7)[layer])

            def experts(n):
                normalise(LN_FFN[n], X, XE, counted=n == 1)
                transposes_lo(TR_FFN[n])
                vec.wait_ge(gate_in, 16 * (5 + 4 * n))
                order.step(vec.tensor_copy(gate_w[0][:, :, :], gate_raw[:, :, :]))
                order.wait()
                vec.tensor_tensor(gate_w[1][:, :, :], gate_raw[:, :, :], f32(gate_w[0][:, :, :]), ALU.subtract).then_inc(gate_split, 1)
                every = [P, TILES, EXPERTS]
                vec.wait_ge(gate_full, 2 * n + 1)
                vec.tensor_scalar(halves(scoresT[:, :]), ps[0:EXPERTS, 0:2, 0:HALF], gate_b[:, :], None, ALU.add).then_inc(scoresT_ready, 1)
                vec.wait_ge(gate_full, 2 * (n + 1))
                order.step(vec.tensor_copy(scores[:, :, :], ps[:, 2, 0:TILES * EXPERTS].rearrange("p (t e) -> p t e", t=TILES)))
                order.wait()
                if n == 1:
                    order.step(vec.tensor_reduce(total[:, :], scores[:, :, :], AX.X, ALU.max))
                    order.wait()
                    vec.tensor_tensor(diff[:, :, :], scores[:, :, :], total[:, :].unsqueeze(2).broadcast_to(every), ALU.subtract).then_inc(gate_arg, 1)
                    vec.wait_ge(gate_exp, n + 1)
                    order.step(vec.tensor_reduce(total[:, :], expo[:, :, :], AX.X, ALU.add))
                    order.wait()
                    order.step(vec.reciprocal(share[:, :], total[:, :]))
                    order.wait()
                    order.step(vec.tensor_tensor(choice[:, :, :], expo[:, :, :], share[:, :].unsqueeze(2).broadcast_to(every), ALU.mult))
                    order.wait()
                values = (scores, choice)[n]
                vec.wait_ge(consts, 16 + 6 * (n + 1))
                for k in range(CHOSEN):
                    src = values if k == 0 else others
                    for t in range(TILES):
                        order.step(vec.max(top[k][:, t, :], src[:, t, :]))
                    order.wait()
                    for t in range(TILES):
                        order.step(vec.max_index(top_at[k][:, t, :], top[k][:, t, :], src[:, t, :]))
                    order.wait()
                    order.step(vec.tensor_copy(chosen[:, :, k], top_at[k][:, :, 0]))
                    order.wait()
                    ins = vec.tensor_tensor(is_chosen[:, :, k, :], chosen[:, :, k].unsqueeze(2).broadcast_to(every),
                                            iota_e[:, :].unsqueeze(1).broadcast_to(every), ALU.is_equal)
                    if k == 0:
                        order.step(ins)
                        order.wait()
                        order.step(vec.scalar_tensor_tensor(others[:, :, :], is_chosen[:, :, 0, :], BELOW, values[:, :, :], ALU.mult, ALU.add))
                        order.wait()
                    else:
                        ins.then_inc(chosen_ready, 1)
                if n == 0:
                    vec.tensor_tensor(diff[:, :, :], scores[:, :, :], top[0][:, :, 0].unsqueeze(2).broadcast_to(every), ALU.subtract).then_inc(gate_arg, 1)
                by_expert = [P, CHOICES, EXPERTS]
                flat = is_chosen[:, :, :, :].rearrange("p t k e -> p (t k) e")
                vec.wait_ge(rank_full, 2 * (n + 1))
                order.step(vec.tensor_copy(in_tile[:, :, :].rearrange("p e j -> p j e"), ps[:, 7, 0:CHOICES * EXPERTS].rearrange("p (j e) -> p j e", e=EXPERTS)))
                order.wait()
                order.step(vec.tensor_tensor_scan(through[:, :, :].rearrange("p e j -> p (e j)"), restart_e[:, :, :].rearrange("p e j -> p (e j)"),
                                                  in_tile[:, :, :].rearrange("p e j -> p (e j)"), 0.0, ALU.mult, ALU.add))
                order.wait()
                order.step(vec.tensor_scalar(need_e[:, :], through[:, :, CHOICES - 1], float(SLOT_ROWS - 1), None, ALU.add))
                order.step(vec.tensor_tensor(in_tile[:, :, :], through[:, :, :], in_tile[:, :, :], ALU.subtract))
                order.wait()
                order.step(vec.tensor_scalar(need_es[:, :], need_e[:, :], SLOT_ROWS.bit_length() - 1, None, ALU.arith_shift_right))
                order.step(vec.tensor_tensor(rank_of[:, :, :], ps[:, 1, 0:CHOICES * EXPERTS].rearrange("p (j e) -> p j e", e=EXPERTS),
                                             in_tile[:, :, :].rearrange("p e j -> p j e"), ALU.add))
                order.wait()
                order.step(vec.tensor_scalar(more[:, :], need_es[:, :], -1.0, 0.0, ALU.add, ALU.max))
                order.step(vec.tensor_tensor(rank_of[:, :, :], rank_of[:, :, :], flat, ALU.mult))
                order.wait()
                order.step(vec.tensor_tensor_scan(more_end[:, :], ones_e[:, :], more[:, :], 0.0, ALU.mult, ALU.add))
                order.step(vec.tensor_reduce(rank_e[:, :], rank_of[:, :, :], AX.X, ALU.add))
                order.wait()
                order.step(vec.tensor_tensor(more_at[:, :], more_end[:, :], more[:, :], ALU.subtract))
                order.step(vec.tensor_scalar(is_more[:, :], rank_e[:, :], float(SLOT_ROWS), None, ALU.is_ge))
                order.wait()
                order.step(vec.tensor_tensor(more_of[:, :, :], flat, more_at[:, :].unsqueeze(1).broadcast_to(by_expert), ALU.mult))
                order.step(vec.tensor_scalar(first_at[:, :], chosen[:, :, :].rearrange("p t k -> p (t k)"), float(SLOT_ROWS), None, ALU.mult))
                order.wait()
                order.step(vec.tensor_reduce(spill[:, :], more_of[:, :, :], AX.X, ALU.add))
                order.wait()
                order.step(vec.tensor_scalar(spill[:, :], spill[:, :], float(SLOT_ROWS), float((EXPERTS - 1) * SLOT_ROWS), ALU.mult, ALU.add))
                order.wait()
                order.step(vec.tensor_tensor(spill[:, :], spill[:, :], first_at[:, :], ALU.subtract))
                order.step(vec.tensor_tensor(rank_e[:, :], rank_e[:, :], first_at[:, :], ALU.add))
                order.wait()
                order.step(vec.tensor_tensor(spill[:, :], spill[:, :], is_more[:, :], ALU.mult))
                order.wait()
                order.step(vec.tensor_tensor(place_f[:, :], rank_e[:, :], spill[:, :], ALU.add))
                order.wait()
                vec.tensor_copy(place[:, :], place_f[:, :]).then_inc(placed, 1)
                sg = [1, MORE, EXPERTS]
                order.step(vec.tensor_tensor(past_e[:, :, :], more_end[0:1, :].unsqueeze(1).broadcast_to(sg), iota_m[:, :].unsqueeze(2).broadcast_to(sg), ALU.is_le))
                order.step(vec.tensor_copy(slot_expert_f[:, 0:EXPERTS], iota_e[0:1, :]))
                order.wait()
                order.step(vec.tensor_reduce(slot_expert_f[:, EXPERTS:XSLOTS], past_e[:, :, :], AX.X, ALU.add))
                order.wait()
                vec.tensor_scalar(slot_expert[:, :], slot_expert_f[:, :], float(EXPERTS - 1), None, ALU.min).then_inc(placed, 1)
                weights = share[:, :].unsqueeze(2).broadcast_to(every)
                if n == 0:
                    vec.wait_ge(gate_exp, n + 1)
                    values = expo
                order.step(vec.tensor_tensor(comb[:, :, :], is_chosen[:, :, 0, :], is_chosen[:, :, 1, :], ALU.add))
                order.wait()
                order.step(vec.tensor_tensor(comb[:, :, :], comb[:, :, :], values[:, :, :], ALU.mult))
                order.wait()
                if n == 0:
                    order.step(vec.tensor_reduce(total[:, :], comb[:, :, :], AX.X, ALU.add))
                    order.wait()
                    order.step(vec.reciprocal(share[:, :], total[:, :]))
                    order.wait()
                    order.step(vec.tensor_tensor(comb[:, :, :], comb[:, :, :], weights, ALU.mult))
                    order.wait()
                for k in range(CHOSEN):
                    ins = vec.tensor_tensor(gate_of[:, :, k, :], is_chosen[:, :, k, :], comb[:, :, :], ALU.mult)
                    if k == 0:
                        order.step(ins)
                    else:
                        ins.then_inc(comb_ready, 1)
                order.wait()
                vec.wait_ge(comb_ready, n + 1)
                order.step(vec.tensor_reduce(gate[:, :, :].rearrange("p t k -> p (t k)"), gate_of[:, :, :, :].rearrange("p t k e -> p (t k) e"), AX.X, ALU.add))
                vec.wait_ge(comb_full, n + 1)
                vec.tensor_copy(combT[:, 0:FULL * P], ps[0:EXPERTS, 5, 0:FULL * P]).then_inc(combT_ready, 1)
                vec.tensor_copy(combT[:, FULL * P:COLS], ps[0:EXPERTS, 6, 0:P]).then_inc(combT_ready, 1)
                add_products(PR_FFN[n], X)
                steps = HIDDEN[n]
                _, units, cols, _, _ = OUTPUT[n]

                def rows_lo(i, b):
                    for q in range(Q_T):
                        vec.wait_ge(t_hi[n], 3 * (2 * i + b) + q + 1)
                        hi, lo = at(XT, slice(None), slice(2 * q, 2 * q + 2), slice(b * SLOT_ROWS, (b + 1) * SLOT_ROWS))
                        vec.tensor_tensor(lo, ps[:, T_BANK + q, :].rearrange("p (k n) -> p k n", k=2), f32(hi), ALU.subtract).then_inc(t_lo[n], 1)

                def slot(i, b, last):
                    for g, (unit, _, width, _, into, _) in enumerate(steps):
                        vec.wait_ge(h_act[n], FREE_H + 2 * len(steps) * i + b * len(steps) + g + 1)
                        vec.tensor_tensor(hT[1][0:width, into, :], hidden_at(g, width)[1], f32(hT[0][0:width, into, :]),
                                          ALU.subtract).then_inc(h_lo[n], 1)
                        if unit == ROWS_AFTER[n] and unit != (steps + [(None,)])[g + 1][0] and not last:
                            rows_lo(i + b, 1 - b)
                    vec.wait_ge(y_out[n][b], 16 * i + 16)
                    for y in range(2 * units):
                        c, half = y // 2, y % 2
                        vec.wait_ge(y_full[n], 2 * units * (2 * i + b) + y + 1)
                        vec.tensor_copy(y_rows[b][:, half, c * cols:(c + 1) * cols], ps[:, 2 + y % 2, 0:cols]).then_inc(y_used[n], 1)

                vec.sem_inc(h_lo[n], FREE_LO)
                vec.sem_inc(t_lo[n], FREE_T)
                vec.sem_inc(y_used[n], FREE_Y)
                rows_lo(0, 0)
                slot_pairs(vec, slot)
                for t in range(TILES):
                    rows = slice(0, LAST if t == FULL else P)
                    vec.wait_ge(back[t], 16 * CHOSEN * (n + 1))
                    for k in range(CHOSEN):
                        ins = vec.scalar_tensor_tensor(X[rows, t, :], out_rows[k][rows, t, :], gate[rows, t, k:k + 1], X[rows, t, :], ALU.mult, ALU.add)
                        if n == 0 or k == 0:
                            order.step(ins)
                            order.wait()
                        else:
                            ins.then_inc(rows_done, 1)
                    if n == 0:
                        row_stats(X, t)

            experts(0)
            end_phase(vec, "vec", 8)

            normalise(LN_IN1, X, XN1, ready=False, counted=True)
            order.wait()
            vec.wait_ge(mix_in, 64)
            normalise(LN_MIX_IN, XN1, XM, gain=in_gain, shift=in_shift)
            transposes_lo(TR_MIX_IN)
            vec.wait_ge(c_in, 16)
            order.step(vec.tensor_copy(csum[:, :, :], count[:, :, :]))
            order.wait()
            for t in range(TILES):
                own = csum[:, t, t * P:(t + 1) * P]
                vec.tensor_tensor(own, own, ident[:, :], ALU.add).then_inc(c_ready, 1)
            for start, rows in ((PR_Q, Q), (PR_K, K), (PR_V, V)):
                take_products(start, rows)
            vec.wait_ge(norm_done, 2 * TILES + 1)
            order.step(vec.tensor_scalar(norm_m[:, :, :], norm[:, :, :], NORM_EPS, None, ALU.max))
            order.wait()
            order.step(vec.reciprocal(inv_norm[:, :, :], norm_m[:, :, :]))
            order.wait()
            vec.wait_ge(prod_used, PR_V + SET)
            for t in range(TILES):
                vec.scalar_tensor_tensor(K[:, t, :], K[:, t, :], inv_norm[:, 1, t:t + 1], V[:, t, :], ALU.mult, ALU.mult).then_inc(kv_rows, 1)
            vec.wait_ge(kv_full, 2)
            for t in range(TILES):
                rows = Q[:, t, :].rearrange("p (c n) -> p c n", c=2)
                order.step(vec.scalar_tensor_tensor(rows, rows, inv_norm[:, 0, t:t + 1], ps[:, 0:2, 0:WCOL], ALU.mult, ALU.mult))
            order.wait()
            normalise(LN_MIX_OUT, Q, Q, gain=out_gain, shift=out_shift)
            transposes_lo(TR_MIX_OUT)
            vec.wait_ge(c_done, TILES)
            order.step(vec.tensor_scalar(absent[:, :, :], count[:, :, :], 0.0, NO_EDGE, ALU.is_equal, ALU.mult))
            add_products(PR_MIX1, X)
            end_phase(vec, "vec", 9)
            transposes_lo(TR_XN1)

            def gat(layer):
                heads, units, kd = GAT[layer]
                tiles = heads * TILES
                heads_seen = layer * GHEADS
                seen = heads_seen * TILES
                XL, PT, a_row = ((XL1, PT1, a_row1), (XL2, PT2, a_row2))[layer]
                width = units * GCOL

                def xl_chunk(h, u, t):
                    n = (h * units + u) * TILES + t
                    vec.wait_ge(xl_hi, seen + n + 1)
                    chunk = ps[:, n % 2, 0:GCOL]
                    hi, lo = at(XL[h % len(XL)], slice(None), t, slice(u * GCOL, (u + 1) * GCOL))
                    order.step(vec.tensor_tensor(lo, chunk, f32(hi), ALU.subtract))
                    if n > 0:
                        vec.wait_ge(xl_done, seen + n)
                    for k in range(2):
                        sums = part_of[k][:, t, u:u + 1] if units > 1 else alpha[k][h % 2][:, t:t + 1]
                        col = slice((h * units + u) * GCOL, (h * units + u + 1) * GCOL)
                        ins = vec.scalar_tensor_tensor(junk[k][:, :], chunk, 1.0, a_row[k][:, col], ALU.mult, ALU.mult, accum_out=sums)
                        if k == 0:
                            order.step(ins)
                        else:
                            ins.then_inc(xl_done, 1)

                def diagonal(h):
                    vec.wait_ge(xl_done, seen + (h + 1) * units * TILES)
                    order.wait()
                    if units > 1:
                        for k in range(2):
                            order.step(vec.tensor_reduce(alpha[k][h % 2][:, :], part_of[k][:, :, :], AX.X, ALU.add))
                        order.wait()
                    if h > 0:
                        vec.wait_ge(row_full, heads_seen + h)
                    for t in range(TILES):
                        vec.tensor_scalar(diag[layer][:, t * P:(t + 1) * P], ident[:, :], alpha[0][h % 2][:, t:t + 1], None, ALU.mult).then_inc(diag_ready, 1)

                def logits(g):
                    h, t, s = g // TILES, g % TILES, g % 2
                    vec.wait_ge(row_full, heads_seen + h + 1)
                    if g >= 2:
                        vec.wait_ge(p_ready, seen + g - 1)
                    e = g_e[s]
                    vec.scalar_tensor_tensor(halves(e[:, :]), ps[:, 2:4, 0:HALF], alpha[1][h % 2][:, t:t + 1], halves(absent[:, t, :]),
                                             ALU.add, ALU.add).then_inc(logit_ready, 1)
                    vec.wait_ge(logit_ready, seen + g + 1)
                    order.step(vec.scalar_tensor_tensor(e[:, :], e[:, :], SLOPE, e[:, :], ALU.mult, ALU.max))
                    order.wait()
                    vec.tensor_reduce(g_neg[:, s:s + 1], e[:, :], AX.X, ALU.max, negate=True).then_inc(e_ready, 1)

                def weights(g):
                    vec.wait_ge(e_exp, seen + g + 1)
                    if g >= 2:
                        vec.wait_ge(pt_full, seen + g - 1)
                    vec.scalar_tensor_tensor(g_p[g % 2][:, :], g_e[g % 2][:, :], 1.0, count[:, g % TILES, :], ALU.mult, ALU.mult,
                                             accum_out=g_sum[:, g:g + 1]).then_inc(p_ready, 1)

                def weights_lo(g):
                    vec.wait_ge(pt_hi, seen + g + 1)
                    hi, lo = PT[g % len(PT)]
                    order.step(vec.tensor_tensor(lo[:, 0:FULL, :], ps[:, 4, 0:FULL * P].rearrange("p (t n) -> p t n", t=FULL), f32(hi[:, 0:FULL, :]), ALU.subtract))
                    vec.tensor_tensor(lo[:, FULL, :], ps[:, 5, 0:P], f32(hi[:, FULL, :]), ALU.subtract).then_inc(pt_done, 1)
                    order.step(vec.tensor_scalar(g_sum_e[:, g:g + 1], g_sum[:, g:g + 1], SUM_EPS, None, ALU.add))
                    order.wait()
                    vec.reciprocal(g_inv[:, g:g + 1], g_sum_e[:, g:g + 1]).then_inc(inv_ready, 1)

                vec.wait_ge(gat_in[layer], 64)
                for u in range(units):
                    for t in range(TILES):
                        xl_chunk(0, u, t)
                diagonal(0)
                for g in range(tiles + 3):
                    h, t = g // TILES, g % TILES
                    if 0 <= g - 3 < tiles:
                        weights_lo(g - 3)
                    if g < tiles:
                        logits(g)
                    if 0 <= g - 1 < tiles:
                        weights(g - 1)
                    if h + 1 < heads:
                        xl_chunk(h + 1, 0, t)
                        if t == FULL:
                            diagonal(h + 1)
                rows = wide if layer == 0 else wide[:, :, 0:DIM]
                bias, gain = (row1["b"], row1["g"]) if layer == 0 else bias_row
                vec.wait_ge(o_used, seen + tiles)
                for t in range(TILES):
                    order.step(vec.tensor_tensor(rows[:, t, :], rows[:, t, :], bias[:, :], ALU.add))
                order.wait()
                vec.wait_ge(late_in[layer], 32)
                normalise(LN_GAT[layer], rows, rows, ready=False, width=heads * width, gain=gain, shift=a_row[0])
                order.wait()
                n_rows = heads if layer == 0 else units
                for j in range(n_rows * TILES):
                    n = PR_SKIP[layer] + j
                    t, cols = j % TILES, slice(j // TILES * GCOL, (j // TILES + 1) * GCOL)
                    mine = rows[:, t, cols]
                    if layer == 0:
                        order.step(vec.scalar_tensor_tensor(mine, mine, 0.0, a_row[1][:, cols], ALU.max, ALU.add))
                        into = mine
                    else:
                        order.step(vec.tensor_tensor(mine, mine, a_row[1][:, cols], ALU.add))
                        order.wait()
                        into = X[:, t, cols]
                        order.step(vec.tensor_tensor(into, into, mine, ALU.add))
                    order.wait()
                    vec.wait_ge(prod_full, n + 1)
                    vec.tensor_tensor(into, into, ps[:, n % 8, 0:GCOL], ALU.add).then_inc(prod_used, 1)
                for t in range(TILES):
                    vec.wait_ge(prod_used, PR_SKIP[layer] + (n_rows - 1) * TILES + t + 1)
                    if layer == 0:
                        vec.sem_inc(rows_ready, 1)
                    else:
                        row_stats(X, t)
                if layer == 0:
                    transposes_lo(TR_H1, GAT1 // P)

            gat(0)
            end_phase(vec, "vec", 10)
            gat(1)
            end_phase(vec, "vec", 11)
            experts(1)
            end_phase(vec, "vec", 12)

        @block.tensor
        def _(pe):
            def transposes(start, src, ready=None, kd=KD):
                g = start
                for t in range(TILES):
                    if ready is not None:
                        pe.wait_ge(rows_ready, ready + t + 1)
                    for ks in groups_of(kd):
                        if g >= 8:
                            pe.wait_ge(tr_done, g - 7)
                        for k in ks:
                            ins = pe.transpose(ps[:, g % 8, (k - ks[0]) * P:(k - ks[0] + 1) * P], src[:, t, k * P:(k + 1) * P], ident[:, :])
                        ins.then_inc(tr_full, 1)
                        g += 1
                return g

            def products(start, first, act_of, kd=KD, units=2, cols=WCOL):
                g = start
                for c in range(units):
                    pe.wait_ge(unit_ready, first + c + 1)
                    w = unit_view((first + c) % 2, kd, cols)
                    for t in range(TILES):
                        if g >= 8:
                            pe.wait_ge(prod_used, g - 7)
                        for k in range(kd):
                            act_t, m = act_of(k)
                            ins = mm3(pe, ps[:, g % 8, 0:cols], at(act_t, slice(None), m, slice(t * P, (t + 1) * P)), at(w, slice(None), k),
                                      k == 0, k == kd - 1, unit_used if c > 0 and t == 0 and k == 0 else None)
                        ins.then_inc(prod_full, 1)
                        g += 1
                used()

            def used(n=1):
                pe.drain().then_inc(unit_used, n)

            pe.wait_ge(masks, 2)
            transposes(TR_0, XN, ROWS_0)
            pe.wait_ge(rf_in, 48)
            pe.wait_ge(tr_done, 10)
            for c in range(2):
                ins = pe.transpose(ps[:, RF_BANK, c * P:(c + 1) * P], rf2[:, c, :], ident[:, :])
            ins.then_inc(rf_full, 1)
            def values(tiles, c):
                pe.wait_ge(unit_ready, U_V + c + 1)
                w = unit_view((U_V + c) % 2, KD, WCOL)
                for t in tiles:
                    g = PR_V0 + c * TILES + t
                    if g >= 8:
                        pe.wait_ge(prod_used, g - 7)
                    for k in range(KD):
                        act_t, m = chunk_of(k)
                        ins = mm3(pe, ps[:, g % 8, 0:WCOL], at(act_t, slice(None), m, slice(t * P, (t + 1) * P)), at(w, slice(None), k), k == 0, k == KD - 1)
                    ins.then_inc(prod_full, 1)

            values(range(EARLY), 0)
            pe.wait_ge(sort_row, 1)
            pe.wait_ge(consts, 12)
            pe.matmul(ps[0:EDGE_ROWS, SORT_BANK, 0:GROUPS], before[0:EDGE_ROWS, 0:EDGE_ROWS], in_row[:, :], start=True, stop=True).then_inc(sort_sum, 1)
            pe.matmul(ps[0:EDGE_ROWS, SORT_BANK + 1, 0:GROUPS], ones_f[0:EDGE_ROWS, 0:EDGE_ROWS], in_row[:, :], start=True, stop=True).then_inc(sort_sum, 1)
            values(range(EARLY, TILES), 0)
            used()
            values(range(1), 1)
            pe.wait_ge(pos_ready, 1)
            values(range(1, 3), 1)
            end_phase(pe, "pe", 1)
            values(range(3, TILES), 1)
            used()
            pe.wait_ge(prod_used, PR_V0 + SET)
            pe.wait_ge(v_lo, SET)

            def key_features(j, s, n):
                pe.wait_ge(B_done, 8 * j + 4 * s + n + 1)
                for t in range(2 * n, min(2 * n + 2, TILES)):
                    ins = mm3(pe, ps[:, 4 + n % 2, (t - 2 * n) * FEATS:(t - 2 * n + 1) * FEATS], at(kT, slice(None), slice(t * P, (t + 1) * P)),
                              at(rfT, slice(None), s), True, True)
                ins.then_inc(B_full, 1)

            def query_features(j, s, n):
                pe.wait_ge(A_done, 12 * j + 4 * s + n + 5)
                mm3(pe, ps[:, n, 0:HALF], at(rfT, slice(None), s, slice((n // 2) * P, (n // 2 + 1) * P)), at(qT, slice(None), cols_half(n)),
                    True, True).then_inc(A_full, 1)

            def key_values(j, s):
                pe.wait_ge(B_done, FREE_B + 8 * j + 4 * s + 2)
                for m in range(2):
                    for t in range(TILES):
                        rows_of = LAST if t == FULL else P
                        if m == 0 and t == FULL:
                            pe.wait_ge(B_done, FREE_B + 8 * j + 4 * s + 3)
                        ins = mm3(pe, ps[:, 5, m * P:(m + 1) * P], at(phi_k, slice(0, rows_of), t, slice(m * P, (m + 1) * P)),
                                  at(attnT, slice(0, rows_of), ds(j, 1), slice(t * P, (t + 1) * P)), t == 0, t == TILES - 1)
                ins.then_inc(B_full, 1)

            def attention(j, s):
                pe.wait_ge(B_done, FREE_B + 8 * j + 4 * s + 4)
                pe.wait_ge(A_done, FREE_A + 12 * j + 4 * s + 8)
                for n in range(2):
                    if s == 0:
                        pe.wait_ge(C_done, 2 * j + n + 1)
                    for m in range(2):
                        ins = mm3(pe, ps[:, 6 + n, 0:HALF], at(kv, slice(None), m, s), at(phi_qT, slice(None), m, cols_half(n)),
                                  s == 0 and m == 0, s == 1 and m == 1)
                    if s == 1:
                        ins.then_inc(C_full, 1)

            with pe.Fori(0, PAIRS) as j:
                for n in range(4):
                    if n % 2 == 0:
                        pe.wait_ge(unit_ready, U_MIX + 2 * j + 2)
                        w = unit_view(1 - n // 2, KD, P)
                    pe.wait_ge(A_done, 12 * j + n + 1)
                    for k in range(KD):
                        ins = mm3(pe, ps[:, n, 0:HALF], at(w, slice(None), k), at(XT, slice(None), k, cols_half(n)), k == 0, k == KD - 1)
                    ins.then_inc(A_full, 1)
                used(2)
                pe.wait_ge(A_done, FREE_A + 12 * j + 2)
                for s in range(2):
                    key_features(j, s, 0)
                    if s == 1:
                        attention(j, 0)
                    key_features(j, s, 1)
                    if s == 0:
                        pe.wait_ge(A_done, FREE_A + 12 * j + 4)
                    for n in range(2):
                        query_features(j, s, n)
                    key_features(j, s, 2)
                    for n in range(2, 4):
                        query_features(j, s, n)
                    key_values(j, s)
                attention(j, 1)
            pe.wait_ge(C_done, FREE_C + 2 * PAIRS)
            products(PR_PROJ, U_PROJ, lambda k: (attnT, k))
            end_phase(pe, "pe", 2)
            with pe.Fori(0, SLOTS // HOTS) as i:
                for k in range(HOTS):
                    pe.wait_ge(hot, HOTS * i + k + 1)
                    pe.wait_ge(hot_b, HOTS * i + k + 1)
                    pe.wait_ge(slot_done, HOTS * i + k + 1)
                    for n in range(2):
                        for half in range(2):
                            ins = pe.matmul(ps[:, 2 * k + n, 0:HALF], src_hot[k][:, half, :], dst_hot[k][:, half, cols_half(n)],
                                            start=(half == 0), stop=(half == 1))
                    ins.then_inc(slot_full, 1)
            end_phase(pe, "pe", 3)
            products(PR_ROOT1, U_ROOT1, chunk_of)
            end_phase(pe, "pe", 4)
            for layer in range(2):
                if layer == 1:
                    transposes(TR_H, ACC, ROWS_H)
                    pe.wait_ge(tr_done, 4 * TILES)
                    products(PR_ROOT2, U_ROOT2, chunk_of)
                    end_phase(pe, "pe", 6)
                if layer == 0:
                    pe.sem_inc(agg_full, FREE_BUF * AGGS)
                with pe.Fori(0, RELS // 2) as i:
                    for b in range(2):
                        pe.wait_ge(a_ready, layer * RELS + FREE_BUF + 2 * i + b + 1)
                        for n in range(2):
                            pe.wait_ge(cnt_used, layer * 2 * RELS + 4 * i + 2 * b + n + 1)
                            for t in range(TILES):
                                ins = pe.matmul(ps[:, 6 + n, 0:HALF], ones_r[:, :], A_r[b][:, t, cols_half(n)], start=(t == 0), stop=(t == TILES - 1))
                            ins.then_inc(cnt_full, 1)
                        for n in range(AGGS):
                            pe.wait_ge(agg_val, layer * AGGS * RELS + AGGS * (2 * i + b) + n + 1)
                            k = slice((n // 2) * P, (n // 2 + 1) * P)
                            for t in range(TILES):
                                for part in range(2):
                                    ins = pe.matmul(ps[:, n % 4, 0:HALF], xn[part][:, t, k], A_r[b][:, t, cols_half(n)],
                                                    start=(t == 0 and part == 0), stop=(t == FULL and part == 1))
                            ins.then_inc(agg_full, 1)
                        for c in range(2):
                            pe.wait_ge(unit_ready, U_REL[layer] + 4 * i + 2 * b + c + 1)
                            w = unit_view(c, KD, WCOL)
                            for t in range(TILES):
                                n = c * TILES + t
                                pe.wait_ge(tra_used, layer * 2 * TILES * RELS + FREE_TRA - 2 + 2 * TILES * (2 * i + b) + n + 1)
                                if n == 2:
                                    pe.wait_ge(agg_done, layer * AGGS * RELS + FREE_DONE + AGGS * (2 * i + b + 1))
                                for k in range(KD):
                                    if n == 0:
                                        pe.wait_ge(agg_done, layer * AGGS * RELS + FREE_DONE + AGGS * (2 * i + b) + 2 * k + 1)
                                    ins = mm3(pe, ps[:, 4 + n % 2, 0:WCOL], at(XT, slice(None), k, slice(t * P, (t + 1) * P)), at(w, slice(None), k),
                                              k == 0, k == KD - 1, unit_used if n == TILES and k == 0 else None)
                                ins.then_inc(tra_full, 1)
                        used()
                end_phase(pe, "pe", (5, 7)[layer])

            def experts(n):
                transposes(TR_FFN[n], XE, ROWS_FFN[n])
                pe.wait_ge(tr_done, TR_FFN[n] + SET)
                pe.wait_ge(gate_in, 16 * (5 + 4 * n))
                for m, (count, width) in enumerate(IN_B[n]):
                    pe.transpose(ps[0:width, 3 + m, 0:EXPERTS * count], in_b_rows[m][0:EXPERTS * count, 0:width],
                                 ident[0:EXPERTS * count, 0:EXPERTS * count]).then_inc(in_b_full, 1)
                pe.wait_ge(gate_split, n + 1)
                for c in range(2):
                    for k in range(KD):
                        ins = mm3(pe, ps[0:EXPERTS, c, 0:HALF], at(gate_w, slice(None), k), at(XT, slice(None), k, cols_half(c)), k == 0, k == KD - 1)
                ins.then_inc(gate_full, 1)
                pe.wait_ge(scoresT_ready, n + 1)
                for t in range(TILES):
                    ins = pe.transpose(ps[:, 2, t * EXPERTS:(t + 1) * EXPERTS], scoresT[:, t * P:(t + 1) * P], ident[0:EXPERTS, 0:EXPERTS])
                ins.then_inc(gate_full, 1)
                pe.wait_ge(chosen_ready, n + 1)
                pe.wait_ge(masks, 3 + n)
                flat = is_chosen[:, :, :, :].rearrange("p t k e -> p (t k e)")
                per = CHOSEN * EXPERTS
                for bank, mask in ((1, before_e), (7, None)):
                    for rows, col in ((P, slice(0, FULL * per)), (LAST, slice(FULL * per, TILES * per))):
                        m = f32(ones_r[0:rows, :]) if mask is None else mask[0:rows, :]
                        ins = pe.matmul(ps[:, bank, col], m, flat[0:rows, col], start=True, stop=True)
                    ins.then_inc(rank_full, 1)
                pe.wait_ge(comb_ready, n + 1)
                for t in range(TILES):
                    ins = pe.transpose(ps[0:EXPERTS, 5 + t // 4, (t % 4) * P:(t % 4 + 1) * P], comb[:, t, :], ident[:, :])
                ins.then_inc(comb_full, 1)
                pe.wait_ge(combT_ready, 2 * (n + 1))
                pe.wait_ge(in_b_ready, 2 + n)
                for j in range(2 * TILES):
                    pe.wait_ge(prod_used, PR_FFN[n] + j - 7)
                    c, t = j // TILES, j % TILES
                    pe.matmul(ps[:, (PR_FFN[n] + j) % 8, 0:WCOL], combT[:, t * P:(t + 1) * P], out_b[:, wcols(c)], start=True, stop=True).then_inc(prod_full, 1)
                pe.wait_ge(prod_used, PR_FFN[n] + SET)
                steps, sizes = HIDDEN[n], FFN_UNITS[n]
                first_y, units, cols, ks, first_h = OUTPUT[n]

                def rows_t(i, b):
                    pe.wait_ge(slot_ready[n][b], 16 * i + 16)
                    for q in range(Q_T):
                        pe.wait_ge(t_lo[n], 3 * (2 * i + b) + q + 1)
                        for k in range(2):
                            for half in range(2):
                                ins = pe.transpose(ps[:, T_BANK + q, (2 * k + half) * P:(2 * k + half + 1) * P],
                                                   slot_in[b][:, half, (2 * q + k) * P:(2 * q + k + 1) * P], ident[:, :])
                        ins.then_inc(t_full[n], 1)

                def slot(i, b, last):
                    def weights(u):
                        pe.wait_ge(e_lo[n], RING + (2 * i + b) * len(sizes) + u + 1)
                        rows, k, width = sizes[u]
                        return unit_view((b * len(sizes) + u) % RING, k, width, rows)

                    pe.wait_ge(t_lo[n], FREE_T + 3 * (2 * i + b + 1))
                    before_u = -1
                    for g, (u, col, width, src, _, _) in enumerate(steps):
                        done = 2 * len(steps) * i + b * len(steps)
                        after = None
                        if u != before_u:
                            after = e_used[n] if u > 0 else None
                            w, before_u = weights(u), u
                        rows, k_of, _ = sizes[u]
                        pe.wait_ge(h_act[n], done + g + places_left(n, g))
                        full, _ = hidden_at(g, width)
                        for k in range(k_of):
                            m = at(XT, slice(None), k, slice(b * SLOT_ROWS, (b + 1) * SLOT_ROWS)) if src is None else at(hT, slice(0, rows), src + k)
                            if src is not None and u != steps[g - 1][0]:
                                pe.wait_ge(h_lo[n], FREE_LO + done + g - k_of + k + 1)
                            ins = mm3(pe, full, at(w, slice(None), k, slice(col, col + width)), m, k == 0, k == k_of - 1,
                                      after if k == 0 else None)
                        ins.then_inc(h_full[n], 1)
                        if u == ROWS_AFTER[n] and u != (steps + [(None,)])[g + 1][0] and not last:
                            rows_t(i + b, 1 - b)
                    for y in range(2 * units):
                        c, half = y // 2, y % 2
                        if half == 0:
                            w = weights(first_y + c)
                        pe.wait_ge(y_used[n], 2 * units * (2 * i + b) + y + 1)
                        for k in range(ks):
                            if y == 0:
                                pe.wait_ge(h_lo[n], FREE_LO + 2 * len(steps) * i + (b + 1) * len(steps) - ks + k + 1)
                            ins = mm3(pe, ps[:, 2 + half, 0:cols], at(hT, slice(None), first_h + k, slice(half * P, (half + 1) * P)),
                                      at(w, slice(None), k), k == 0, k == ks - 1, e_used[n] if k == 0 and half == 0 else None)
                        ins.then_inc(y_full[n], 1)
                    pe.drain().then_inc(e_used[n], 1)

                pe.sem_inc(e_used[n], RING)
                pe.sem_inc(t_full[n], FREE_IN)
                rows_t(0, 0)
                slot_pairs(pe, slot)

            experts(0)
            end_phase(pe, "pe", 8)

            transposes(TR_MIX_IN, XM, ROWS_MIX_IN)
            pe.wait_ge(tr_done, TR_MIX_IN + SET)
            for n, start in enumerate((PR_Q, PR_K, PR_V)):
                products(start, U_MIX1 + 2 * n, chunk_of)
            pe.wait_ge(prod_used, PR_V + SET)
            pe.wait_ge(c_ready, TILES)
            for d in range(TILES):
                if d >= 2:
                    pe.wait_ge(c_done, d - 1)
                for t in range(TILES):
                    ins = pe.transpose(ps[:, 4 + 2 * (d % 2) + t // FULL, (t % FULL) * P:(t % FULL + 1) * P], csum[:, t, d * P:(d + 1) * P], ident[:, :])
                ins.then_inc(c_full, 1)
            pe.wait_ge(kv_rows, TILES)
            for c in range(2):
                for t in range(TILES):
                    rows = LAST if t == FULL else P
                    ins = pe.matmul(ps[:, c, 0:WCOL], f32(ones_r[0:rows, :]), K[0:rows, t, wcols(c)], start=(t == 0), stop=(t == FULL))
                ins.then_inc(kv_full, 1)
            transposes(TR_MIX_OUT, Q, ROWS_MIX_OUT)
            pe.wait_ge(tr_done, TR_MIX_OUT + SET)
            products(PR_MIX1, U_MIX1 + 6, chunk_of)
            end_phase(pe, "pe", 9)
            transposes(TR_XN1, XN1)
            pe.wait_ge(tr_done, TR_XN1 + SET)

            def gat(layer):
                heads, units, kd = GAT[layer]
                tiles = heads * TILES
                heads_seen = layer * GHEADS
                seen = heads_seen * TILES
                XL, PT = ((XL1, PT1), (XL2, PT2))[layer]

                def xl_chunk(h, u, t):
                    n = (h * units + u) * TILES + t
                    unit = U_XL[layer] + h * units + u
                    if t == 0:
                        pe.wait_ge(unit_ready, unit + 1)
                    if n >= 2:
                        pe.wait_ge(xl_done, seen + n - 1)
                    w = unit_view(unit % 2, kd, GCOL)
                    for k in range(kd):
                        act_t, m = chunk_of(k)
                        ins = mm3(pe, ps[:, n % 2, 0:GCOL], at(act_t, slice(None), m, slice(t * P, (t + 1) * P)), at(w, slice(None), k), k == 0, k == kd - 1)
                    ins.then_inc(xl_full, 1)
                    if t == FULL:
                        used()

                def source_row(h):
                    pe.wait_ge(diag_ready, seen + (h + 1) * TILES)
                    if h > 0:
                        pe.wait_ge(logit_ready, seen + h * TILES)
                    for c in range(2):
                        ins = pe.matmul(ps[:, 2 + c, 0:HALF], f32(ones_r[:, :]), diag[layer][:, cols_half(c)], start=True, stop=True)
                    ins.then_inc(row_full, 1)

                def weights_t(g):
                    pe.wait_ge(p_ready, seen + g + 1)
                    if g > 0:
                        pe.wait_ge(pt_done, seen + g)
                    for t in range(TILES):
                        ins = pe.transpose(ps[:, 4 + t // FULL, (t % FULL) * P:(t % FULL + 1) * P], g_p[g % 2][:, t * P:(t + 1) * P], ident[:, :])
                    ins.then_inc(pt_full, 1)

                def output(g):
                    h = g // TILES
                    pe.wait_ge(pt_done, seen + g + 1)
                    ring = (2, 1)[layer]
                    if g >= ring:
                        pe.wait_ge(o_used, seen + g - ring + 1)
                    cols = (GCOL, WCOL)[layer]
                    for c in range(units * GCOL // cols):
                        for t in range(TILES):
                            ins = mm3(pe, ps[:, 6 + (g % 2 if layer == 0 else c), 0:cols], at(PT[g % len(PT)], slice(None), t),
                                      at(XL[h % len(XL)], slice(None), t, slice(c * cols, (c + 1) * cols)), t == 0, t == FULL)
                    ins.then_inc(o_full, 1)

                for u in range(units):
                    for t in range(TILES):
                        xl_chunk(0, u, t)
                source_row(0)
                for g in range(tiles + 3):
                    h, t = g // TILES, g % TILES
                    if h + 1 < heads:
                        xl_chunk(h + 1, 0, t)
                    if 0 <= g - 2 < tiles:
                        weights_t(g - 2)
                    if 0 <= g - 3 < tiles:
                        output(g - 3)
                    if h + 1 < heads and t == FULL:
                        source_row(h + 1)
                pe.wait_ge(o_used, seen + tiles)
                products(PR_SKIP[layer], U_SKIP[layer], chunk_of, kd, (heads, units)[layer], GCOL)
                if layer == 0:
                    pe.wait_ge(prod_used, PR_SKIP[0] + heads * TILES)
                    transposes(TR_H1, wide, ROWS_H1, GAT1 // P)
                    pe.wait_ge(tr_done, TR_H1 + 3 * TILES)

            gat(0)
            end_phase(pe, "pe", 10)
            gat(1)
            end_phase(pe, "pe", 11)
            experts(1)
            end_phase(pe, "pe", 12)


_INPUTS = ['x', 'src', 'dst', 'edge_type_8', 'L0_gnn_W1', 'L0_gnn_root1', 'L0_gnn_b1', 'L0_gnn_W2', 'L0_gnn_root2', 'L0_gnn_b2',
           'L0_mix_W_qkv', 'L0_mix_b_qkv', 'L0_mix_W_proj', 'L0_mix_b_proj', 'L0_mix_random_features',
           'L0_ffn_Wg', 'L0_ffn_bg', 'L0_ffn_W1', 'L0_ffn_b1', 'L0_ffn_W2', 'L0_ffn_b2', 'L0_ffn_W3', 'L0_ffn_b3',
           'L1_gnn_W1', 'L1_gnn_a_src1', 'L1_gnn_a_dst1', 'L1_gnn_b1', 'L1_gnn_g1', 'L1_gnn_be1', 'L1_gnn_Wr1', 'L1_gnn_br1',
           'L1_gnn_W2', 'L1_gnn_a_src2', 'L1_gnn_a_dst2', 'L1_gnn_b2', 'L1_gnn_g2', 'L1_gnn_be2', 'L1_gnn_Wr2', 'L1_gnn_br2',
           'L1_mix_w_qkv', 'L1_mix_w_proj', 'L1_mix_ln_in_g', 'L1_mix_ln_in_b', 'L1_mix_ln_out_g', 'L1_mix_ln_out_b',
           'L1_ffn_router_w', 'L1_ffn_router_b', 'L1_ffn_w1', 'L1_ffn_b1', 'L1_ffn_w2', 'L1_ffn_b2']


def kernel(**inputs):
    import numpy as np
    import concourse.bacc as bacc
    from concourse.bass_utils import run_bass_kernel_spmd

    nc = bacc.Bacc("TRN2", target_bir_lowering=False, num_devices=1)
    arrays, views = {}, {}
    for name in _INPUTS:
        arrays[name + "_in"] = np.ascontiguousarray(inputs[name])
        views[name] = nc.dram_tensor(name + "_in", arrays[name + "_in"].shape, mybir.dt.from_np(arrays[name + "_in"].dtype), kind="ExternalInput").ap()
    result = nc.dram_tensor("rows_out", (NODES, DIM), F32, kind="ExternalOutput").ap()
    build(nc, views, result)
    got = run_bass_kernel_spmd(nc, [arrays], core_ids=[0])
    return got.results[0]["rows_out"]
```
